# Optimizing a Trainium2 kernel written in Bass

```python
import numpy as np
import jax
import jax.numpy as jnp

def _softmax(x, axis=-1):
    return jax.nn.softmax(x, axis=axis)

def _gelu(x):
    return jax.nn.gelu(x, approximate=True)

def _silu(x):
    return jax.nn.silu(x)

def _sigmoid(x):
    return jax.nn.sigmoid(x)

def _layernorm(x, axis=-1, eps=1e-05):
    m = jnp.mean(x, axis=axis, keepdims=True)
    v = jnp.var(x, axis=axis, keepdims=True)
    return (x - m) / jnp.sqrt(v + eps)

def _scatter_add(tgt, idx, src, axis=0):
    return tgt.at[idx].add(src)

def _segment_sum(src, seg, n):
    return jax.ops.segment_sum(src, seg, n)
kernel_name = 'mk_vit_tower_cls_d1_tok_img1024_r4_c0a0ec'

def setup_inputs(seed: int=0):
    np.random.seed(seed)
    _w = jnp.asarray

    def _rec_inputs():
        import jax
        import jax.numpy as jnp
        _rk = jax.random.key(seed)
        x = -0.00040386 + 0.999972 * jax.random.normal(jax.random.fold_in(_rk, 1), (128, 3, 64, 64), jnp.float32)
        cls_tok = 0.02 * jax.random.normal(jax.random.fold_in(_rk, 5), (1, 1, 256), jnp.float32)
        return (x, cls_tok)
    x, cls_tok = _rec_inputs()

    def _L0_tok_setup():
        import math
        import jax, jax.numpy as jnp
        import numpy as np
        PATCH = 16
        HIDDEN = 256
        IMG = 64
        GRID = IMG // PATCH
        N_TOK = GRID * GRID
        PDIM = 3 * PATCH * PATCH

        def make_pos_emb(n: int, d: int) -> jnp.ndarray:
            pos = jnp.arange(n, dtype=jnp.float32)[:, None]
            div = jnp.exp(jnp.arange(0, d, 2, dtype=jnp.float32) * (-math.log(10000.0) / d))
            pe = jnp.zeros((n, d), dtype=jnp.float32)
            pe = pe.at[:, 0::2].set(jnp.sin(pos * div))
            pe = pe.at[:, 1::2].set(jnp.cos(pos * div[:d // 2]))
            return pe
        key = jax.random.key(seed)
        k_img, k_w, k_b = jax.random.split(key, 3)
        img = jax.random.normal(k_img, (64, 3, IMG, IMG), dtype=jnp.float32)
        bound = 1.0 / math.sqrt(PDIM)
        W = jax.random.uniform(k_w, (HIDDEN, PDIM), minval=-bound, maxval=bound, dtype=jnp.float32)
        b = jax.random.uniform(k_b, (HIDDEN,), minval=-bound, maxval=bound, dtype=jnp.float32)
        pos_emb = make_pos_emb(N_TOK, HIDDEN)
        return {'img': img, 'W': W, 'b': b, 'pos_emb': pos_emb}
    _L0_tok_all = _L0_tok_setup()
    _L0_tok_in = {k: v for k, v in _L0_tok_all.items() if k in ('W', 'b', 'pos_emb')}
    del _L0_tok_all

    def _L0_attn_setup():
        import jax, jax.numpy as jnp
        import numpy as np
        DIM = 256
        NH = 16
        HD = DIM // NH
        DROPE = 16
        MAXSEQ = 512
        LAT = 64
        BATCH = 2
        SEQ = 512

        def _rope_freqs(max_seq, head_dim):
            inv = 1.0 / 10000.0 ** (jnp.arange(0, head_dim, 2, dtype=jnp.float32) / head_dim)
            ang = jnp.arange(max_seq, dtype=jnp.float32)[:, None] * inv[None, :]
            return (jnp.cos(ang), jnp.sin(ang))

        def _apply_decoupled_rope(x, cosf, sinf, d_rope):
            b, d1, d2, hd = x.shape
            half = d_rope // 2
            xr = x[..., :d_rope].astype(jnp.float32).reshape(b, d1, d2, half, 2)
            xa, xb = (xr[..., 0], xr[..., 1])
            c = cosf[:d1, :half][None, :, None, :]
            s = sinf[:d1, :half][None, :, None, :]
            rot = jnp.stack([xa * c - xb * s, xa * s + xb * c], axis=-1)
            rot = rot.reshape(b, d1, d2, d_rope)
            return jnp.concatenate([rot, x[..., d_rope:]], axis=-1)
        key = jax.random.key(seed)
        ks = jax.random.split(key, 8)

        def w(k, o, i):
            return jax.random.normal(k, (o, i), jnp.float32) / np.sqrt(i).astype(np.float32)
        return {'x': jax.random.normal(ks[0], (BATCH, SEQ, DIM), jnp.float32), 'wq': w(ks[1], NH * HD, DIM), 'wk_a': w(ks[2], LAT, DIM), 'wk_b': w(ks[3], NH * HD, LAT), 'wv_a': w(ks[4], LAT, DIM), 'wv_b': w(ks[5], NH * HD, LAT), 'wo': w(ks[6], DIM, NH * HD)}
    _L0_attn_all = _L0_attn_setup()
    _L0_attn_in = {k: v for k, v in _L0_attn_all.items() if k in ('wq', 'wk_a', 'wk_b', 'wv_a', 'wv_b', 'wo')}
    del _L0_attn_all

    def _L0_ffn_setup():
        import jax, jax.numpy as jnp
        import numpy as np
        N_HEAD = 16
        N_ACTIVE = 4
        D_MODEL = 256
        D_ATTN = 64
        B = 4
        S = 512
        key = jax.random.key(seed)
        ks = jax.random.split(key, 6)
        sc = 1.0 / np.sqrt(D_MODEL).astype(np.float32)
        return {'x': jax.random.normal(ks[0], (B, S, D_MODEL), jnp.float32), 'Wq': jax.random.normal(ks[1], (D_MODEL, N_HEAD * D_ATTN), jnp.float32) * sc, 'bq': jnp.zeros((N_HEAD * D_ATTN,), jnp.float32), 'Wk': jax.random.normal(ks[2], (D_MODEL, N_HEAD * D_ATTN), jnp.float32) * sc, 'bk': jnp.zeros((N_HEAD * D_ATTN,), jnp.float32), 'Wv': jax.random.normal(ks[3], (D_MODEL, N_HEAD * D_ATTN), jnp.float32) * sc, 'bv': jnp.zeros((N_HEAD * D_ATTN,), jnp.float32), 'Wr': jax.random.normal(ks[4], (D_MODEL, N_HEAD), jnp.float32) * sc, 'br': jnp.zeros((N_HEAD,), jnp.float32), 'Wo': jax.random.normal(ks[5], (N_ACTIVE * D_ATTN, D_MODEL), jnp.float32) * (1.0 / np.sqrt(N_ACTIVE * D_ATTN).astype(np.float32)), 'bo': jnp.zeros((D_MODEL,), jnp.float32)}
    _L0_ffn_all = _L0_ffn_setup()
    _L0_ffn_in = {k: v for k, v in _L0_ffn_all.items() if k in ('Wq', 'bq', 'Wk', 'bk', 'Wv', 'bv', 'Wr', 'br', 'Wo', 'bo')}
    del _L0_ffn_all
    return {'x': x, 'cls_tok': cls_tok, 'L0_tok_W': _L0_tok_in['W'], 'L0_tok_b': _L0_tok_in['b'], 'L0_tok_pos_emb': _L0_tok_in['pos_emb'], 'L0_attn_wq': _L0_attn_in['wq'], 'L0_attn_wk_a': _L0_attn_in['wk_a'], 'L0_attn_wk_b': _L0_attn_in['wk_b'], 'L0_attn_wv_a': _L0_attn_in['wv_a'], 'L0_attn_wv_b': _L0_attn_in['wv_b'], 'L0_attn_wo': _L0_attn_in['wo'], 'L0_ffn_Wq': _L0_ffn_in['Wq'], 'L0_ffn_bq': _L0_ffn_in['bq'], 'L0_ffn_Wk': _L0_ffn_in['Wk'], 'L0_ffn_bk': _L0_ffn_in['bk'], 'L0_ffn_Wv': _L0_ffn_in['Wv'], 'L0_ffn_bv': _L0_ffn_in['bv'], 'L0_ffn_Wr': _L0_ffn_in['Wr'], 'L0_ffn_br': _L0_ffn_in['br'], 'L0_ffn_Wo': _L0_ffn_in['Wo'], 'L0_ffn_bo': _L0_ffn_in['bo']}

def reference(x, cls_tok, L0_tok_W, L0_tok_b, L0_tok_pos_emb, L0_attn_wq, L0_attn_wk_a, L0_attn_wk_b, L0_attn_wv_a, L0_attn_wv_b, L0_attn_wo, L0_ffn_Wq, L0_ffn_bq, L0_ffn_Wk, L0_ffn_bk, L0_ffn_Wv, L0_ffn_bv, L0_ffn_Wr, L0_ffn_br, L0_ffn_Wo, L0_ffn_bo):
    import jax
    import jax.numpy as jnp

    def _L0_tok_ref(img, W, b, pos_emb):
        import math
        import jax, jax.numpy as jnp
        import numpy as np
        PATCH = 16
        HIDDEN = 256
        IMG = 64
        GRID = IMG // PATCH
        N_TOK = GRID * GRID
        PDIM = 3 * PATCH * PATCH

        def make_pos_emb(n: int, d: int) -> jnp.ndarray:
            pos = jnp.arange(n, dtype=jnp.float32)[:, None]
            div = jnp.exp(jnp.arange(0, d, 2, dtype=jnp.float32) * (-math.log(10000.0) / d))
            pe = jnp.zeros((n, d), dtype=jnp.float32)
            pe = pe.at[:, 0::2].set(jnp.sin(pos * div))
            pe = pe.at[:, 1::2].set(jnp.cos(pos * div[:d // 2]))
            return pe
        B, C, H, Wd = img.shape
        p = PATCH
        gh, gw = (H // p, Wd // p)
        x = img.reshape(B, C, gh, p, gw, p)
        x = jnp.transpose(x, (0, 2, 4, 1, 3, 5))
        x = x.reshape(B, gh * gw, C * p * p)
        z = jnp.einsum('bnd,hd->bnh', x, W) + b
        return z + pos_emb[None, :, :]

    def _L0_attn_ref(x, wq, wk_a, wk_b, wv_a, wv_b, wo):
        import jax, jax.numpy as jnp
        import numpy as np
        DIM = 256
        NH = 16
        HD = DIM // NH
        DROPE = 16
        MAXSEQ = 512
        LAT = 64
        BATCH = 2
        SEQ = 512

        def _rope_freqs(max_seq, head_dim):
            inv = 1.0 / 10000.0 ** (jnp.arange(0, head_dim, 2, dtype=jnp.float32) / head_dim)
            ang = jnp.arange(max_seq, dtype=jnp.float32)[:, None] * inv[None, :]
            return (jnp.cos(ang), jnp.sin(ang))

        def _apply_decoupled_rope(x, cosf, sinf, d_rope):
            b, d1, d2, hd = x.shape
            half = d_rope // 2
            xr = x[..., :d_rope].astype(jnp.float32).reshape(b, d1, d2, half, 2)
            xa, xb = (xr[..., 0], xr[..., 1])
            c = cosf[:d1, :half][None, :, None, :]
            s = sinf[:d1, :half][None, :, None, :]
            rot = jnp.stack([xa * c - xb * s, xa * s + xb * c], axis=-1)
            rot = rot.reshape(b, d1, d2, d_rope)
            return jnp.concatenate([rot, x[..., d_rope:]], axis=-1)
        b, s, _ = x.shape
        q = (x @ wq.T).reshape(b, s, NH, HD).transpose(0, 2, 1, 3)
        k = (x @ wk_a.T @ wk_b.T).reshape(b, s, NH, HD).transpose(0, 2, 1, 3)
        v = (x @ wv_a.T @ wv_b.T).reshape(b, s, NH, HD).transpose(0, 2, 1, 3)
        cosf, sinf = _rope_freqs(MAXSEQ, HD)
        q = _apply_decoupled_rope(q, cosf, sinf, DROPE)
        k = _apply_decoupled_rope(k, cosf, sinf, DROPE)
        scores = jnp.einsum('bhqd,bhkd->bhqk', q, k) / np.float32(np.sqrt(HD))
        attn = jax.nn.softmax(scores, axis=-1)
        out = jnp.einsum('bhqk,bhkd->bhqd', attn, v)
        out = out.transpose(0, 2, 1, 3).reshape(b, s, NH * HD)
        return out @ wo.T

    def _L0_ffn_ref(x, Wq, bq, Wk, bk, Wv, bv, Wr, br, Wo, bo):
        import jax, jax.numpy as jnp
        import numpy as np
        N_HEAD = 16
        N_ACTIVE = 4
        D_MODEL = 256
        D_ATTN = 64
        B = 4
        S = 512
        b, s, _ = x.shape
        dist = jax.nn.softmax(jnp.mean(x @ Wr + br, axis=1), axis=-1)
        _, idx = jax.lax.top_k(dist, N_ACTIVE)
        idx = jnp.sort(idx, axis=-1)

        def proj(W, bias):
            return (x @ W + bias).reshape(b, s, N_HEAD, D_ATTN).transpose(0, 2, 1, 3)
        Q = proj(Wq, bq)
        K = proj(Wk, bk)
        V = proj(Wv, bv)
        gather = lambda t: jnp.take_along_axis(t, idx[:, :, None, None], axis=1)
        Qs, Ks, Vs = (gather(Q), gather(K), gather(V))
        scale = 1.0 / jnp.sqrt(jnp.asarray(D_ATTN, x.dtype))
        score = jax.nn.softmax(jnp.einsum('bhqd,bhkd->bhqk', Qs, Ks) * scale, axis=-1)
        O = jnp.einsum('bhqk,bhkd->bhqd', score, Vs)
        O = O.transpose(0, 2, 1, 3).reshape(b, s, N_ACTIVE * D_ATTN)
        return O @ Wo + bo
    h = _L0_tok_ref(x, L0_tok_W, L0_tok_b, L0_tok_pos_emb)
    h = jnp.concatenate([jnp.broadcast_to(cls_tok, (h.shape[0], 1, h.shape[2])), h], axis=1)
    h = h + _L0_attn_ref(_layernorm(h, axis=-1), L0_attn_wq, L0_attn_wk_a, L0_attn_wk_b, L0_attn_wv_a, L0_attn_wv_b, L0_attn_wo)
    h = h + _L0_ffn_ref(_layernorm(h, axis=-1), L0_ffn_Wq, L0_ffn_bq, L0_ffn_Wk, L0_ffn_bk, L0_ffn_Wv, L0_ffn_bv, L0_ffn_Wr, L0_ffn_br, L0_ffn_Wo, L0_ffn_bo)
    return h

_drawn_inputs = setup_inputs


def setup_inputs(seed=0):
    import zlib

    import numpy as np

    out = dict(_drawn_inputs(seed))
    spreads = {'L0_ffn_bq': (0.0, 0.629),
     'L0_ffn_bk': (0.0, 0.8),
     'L0_ffn_bv': (0.0, 0.1),
     'L0_ffn_br': (0.0, 0.1),
     'L0_ffn_bo': (0.0, 0.1)}
    factors = {}
    for name, (base, spread) in spreads.items():
        noise = np.random.default_rng([zlib.crc32(name.encode()), seed]).standard_normal(out[name].shape)
        drawn = base * np.exp(spread * noise) if base else spread * noise
        out[name] = jnp.asarray(drawn.astype(out[name].dtype))
    for name, factor in factors.items():
        out[name] = (out[name] * factor).astype(out[name].dtype)
    return out
```

```python
from contextlib import ExitStack

import concourse.bass as bass
from concourse import mybir

ALU = mybir.AluOpType
ACT = mybir.ActivationFunctionType
AX_X = mybir.AxisListType.X
F32 = mybir.dt.float32
F16 = mybir.dt.float16
I32 = mybir.dt.int32

P = 128
B = 128
D = 256
KT = D // P
NPATCH = 16
NTOK = NPATCH + 1
PDIM = 768
PKT = PDIM // P
NH1, HD1 = 16, 16
NE, HD2 = 16, 64
NSLOT = 4
EPS = 1e-5
BANK = 512
QROW = 32
IPG = P // QROW
NGRP = B // IPG

CHUNKS = [[0]] + [[4 * c + 1 + i for i in range(4)] for c in range(NPATCH // 4)]

UG = 2
UI = UG * IPG
NU = NGRP // UG
HH = NH1 // 2
ROWH = HH * NTOK

TP = 8
TU = 8
PU = TP * TU
GU = PU // IPG
NV = -(-(B * NSLOT + NE * (TP - 1)) // TP // TU)
NTILE = NV * TU
NPAIR = NTILE * TP
XS, WS = 16.0, 64.0

CONSTS = {}
_at = 0
for _name, _n in (("ident", P), ("before", P), ("one", P), ("tri", NE * NE), ("tile_starts", NE), ("pair", NPAIR),
                  ("row", 1), ("own_head", HH), ("even", 1), ("odd", 1), ("cos", D), ("sin", D),
                  ("slot", NSLOT * NE), ("br", NE), ("eps", 1)):
    CONSTS[_name] = (_at, _at + _n)
    _at += _n
NCONST = _at


def free(ap, *dims):
    return bass.AP(ap.tensor, ap.offset, [tuple(ap.ap[0])] + [tuple(d) for d in dims])


def flat(ap):
    return ap.rearrange("p a b -> p (a b)")


def build(nc, a, out, pair_rows):
    with ExitStack() as ctx:
        def sb(name, cols, dt=F32):
            return ctx.enter_context(nc.sbuf_tensor(name, [P, cols], dt))

        def sem(name):
            return ctx.enter_context(nc.semaphore(name))

        r1 = sb("r1", 2 * 2 * UI * ROWH + NGRP * D)
        xT = r1[:, 0:4 * PKT * 512].rearrange("p (c k n) -> p c k n", c=4, k=PKT)
        kx = r1[:, 0:4 * UI * ROWH].rearrange("p (u f n) -> p u f n", u=2, f=2)
        v1 = r1[:, 4 * UI * ROWH:].rearrange("p (g d) -> p g d", g=NGRP)
        _half = NTOK * D // 2
        xh = r1[:, 0:_half].bitcast(F16).rearrange("p (n d) -> p n d", n=NTOK)
        xl = r1[:, _half:2 * _half].bitcast(F16).rearrange("p (n d) -> p n d", n=NTOK)
        og = r1[:, 2 * _half:2 * _half + NSLOT * NTOK * HD2].rearrange("p (s n) -> p s n", s=NSLOT)
        og2 = r1[:, 0:NTOK * D].rearrange("p (n d) -> p n d", n=NTOK)
        ogT = r1[:, 4 * _half:4 * _half + 2 * D].rearrange("p (u d) -> p u d", u=2)
        r2 = sb("r2", 6144)
        tokw = r2[:, 0:PKT * D].rearrange("p (k d) -> p k d", k=PKT)
        xn = r2[:, 1536:1536 + 8 * D].rearrange("p (r d) -> p r d", r=8)
        xnT = r2[:, 3584:3584 + 2 * KT * 512].rearrange("p (u k n) -> p u k n", u=2, k=KT)
        wst = r2[:, 0:4 * 1536].rearrange("p (s n) -> p s n", s=4)
        v2 = r2[:, 0:2048].rearrange("p (u g d) -> p u g d", u=2, g=GU)
        o2 = r2[:, 2048:4096].rearrange("p (u g d) -> p u g d", u=2, g=GU)
        p2 = r2[:, 4096:5120].rearrange("p (u g q) -> p u g q", u=2, g=GU)
        p2T = r2[:, 5120:6144].rearrange("p (u g q) -> p u g q", u=2, g=GU)
        r3 = sb("r3", 2 * 2 * B * NTOK + B * QROW)
        qr = r3[:, 0:2 * B * NTOK].rearrange("p (f n) -> p f n", f=2)
        oT = qr
        kr = r3[:, 4352:8704].rearrange("p (f n) -> p f n", f=2)
        lat = r3[:, 8704:8704 + B * QROW]
        p1 = lat[:, 0:2048].rearrange("p (u b q) -> p u b q", u=2, b=32)
        p1T = lat[:, 2048:4096].rearrange("p (u b q) -> p u b q", u=2, b=32)
        xg = r3[:, 0:8192].bitcast(F16).rearrange("p (u k n) -> p u k n", u=2, k=2 * KT)
        q2 = r3[0:HD2, 8192:8192 + 2 * PU * NTOK].rearrange("p (u n) -> p u n", u=2)
        k2 = r3[0:HD2, 10368:10368 + 2 * PU * NTOK].rearrange("p (u n) -> p u n", u=2)
        h = sb("h", NTOK * D)[:, :].rearrange("p (n d) -> p n d", n=NTOK)
        wh = sb("wh", KT * NE * 192, F16)[:, :].rearrange("p (k e d) -> p k e d", k=KT, e=NE)
        wl = sb("wl", KT * NE * 192, F16)[:, :].rearrange("p (k e d) -> p k e d", k=KT, e=NE)
        wb = sb("wb", NE * 192, F16)[:, :].rearrange("p (e d) -> p e d", e=NE)
        ones = sb("ones", TP * NTOK, F16)
        ident16 = sb("ident16", P, F16)
        pairs_of = sb("pairs_of", NPAIR, F16)
        cst = sb("cst", NCONST)
        wq = sb("wq", KT * 2 * D)[:, :].rearrange("p (k t d) -> p k t d", k=KT, t=2)
        wlat = sb("wlat", KT * P)[:, :].rearrange("p (k d) -> p k d", k=KT)
        wk = sb("wk", 2 * D)[:, :].rearrange("p (t d) -> p t d", t=2)
        wv = sb("wv", D)
        wo1 = sb("wo1", KT * D)[:, :].rearrange("p (k d) -> p k d", k=KT)
        wo2 = sb("wo2", KT * D)[:, :].rearrange("p (k d) -> p k d", k=KT)
        wr = sb("wr", KT * NE)[:, :].rearrange("p (k e) -> p k e", k=KT)
        tokb = sb("tokb", D)
        bo = sb("bo", D)
        stats = sb("stats", 2 * NTOK * 6)[:, :].rearrange("p (n s) -> p n s", s=6)
        mv = sb("mv", 2 * NTOK * 2)[:, :].rearrange("p (n s) -> p n s", s=2)
        sd = sb("sd", 2 * NTOK)
        rstd = sb("rstd", 2 * NTOK)
        xs = sb("xs", 2 * D)[:, :].rearrange("p (u d) -> p u d", u=2)
        mx = sb("mx", 2 * 32)[:, :].rearrange("p (u b) -> p u b", u=2)
        rs = sb("rs", 2 * 32)[:, :].rearrange("p (u b) -> p u b", u=2)
        rinv = sb("rinv", 2 * 32)[:, :].rearrange("p (u b) -> p u b", u=2)
        odd_part = sb("odd_part", 2 * 136)[:, :].rearrange("p (f n) -> p f n", f=2)
        msumT = sb("msumT", KT * P)[:, :].rearrange("p (k n) -> p k n", k=KT)
        rt = r2[:, 0:1536]
        idx = sb("idx", NSLOT, I32)
        heads = sb("heads", NTILE, I32)
        ps = ctx.enter_context(nc.psum_tensor("ps", [P, 8 * BANK], F32))

        def bank(i, lo=0, hi=BANK):
            return ps[:, i * BANK + lo:i * BANK + hi]

        def const(name):
            lo, hi = CONSTS[name]
            return cst[:, lo:hi]

        ident = const("ident")

        ld = {n: sem(f"ld_{n}") for n in
              ("tokw", "x0", "x1", "x2", "x3", "cst", "cls", "pos", "tokb", "wq", "wlat", "wk", "wv",
               "wo1", "wo2", "wr", "bo", "w0", "w1", "w2", "w3", "w4", "w5")}
        ps_clear = sem("ps_clear")
        lat_clear = sem("lat_clear")
        p1_clear = sem("p1_clear")
        hb_ready = sem("hb_ready")
        embedded = sem("embedded")
        h_ready = sem("h_ready")
        st_ready = sem("st_ready")
        mv_ready = sem("mv_ready")
        sd_ready = sem("sd_ready")
        rstd_ready = sem("rstd_ready")
        xn_ready = sem("xn_ready")
        xn_turned = sem("xn_turned")
        xnT_ready = sem("xnT_ready")
        turning = sem("turning")
        rotated = sem("rotated")
        proj_in = sem("proj_in")
        proj_act = sem("proj_act")
        proj_dve = sem("proj_dve")
        lat_in = sem("lat_in")
        lat_ready = sem("lat_ready")
        v_in = sem("v_in")
        v_act = sem("v_act")
        v_dve = sem("v_dve")
        kx0_ready = sem("kx0_ready")
        kx1_ready = sem("kx1_ready")
        s_done = sem("s_done")
        mx_ready = sem("mx_ready")
        sub_done = sem("sub_done")
        exp_done = sem("exp_done")
        rs_ready = sem("rs_ready")
        rinv_ready = sem("rinv_ready")
        norm_done = sem("norm_done")
        p1T_ready = sem("p1T_ready")
        row_done = sem("row_done")
        odd_ready = sem("odd_ready")
        oT_ready = sem("oT_ready")
        w_high = sem("w_high")
        w_scaled = sem("w_scaled")
        w_low = sem("w_low")
        wo1_done = sem("wo1_done")
        h2_ready = sem("h2_ready")
        st2_ready = sem("st2_ready")
        mv2_ready = sem("mv2_ready")
        sd2_ready = sem("sd2_ready")
        rstd2_ready = sem("rstd2_ready")
        xs_ready = sem("xs_ready")
        xh_ready = sem("xh_ready")
        xl_ready = sem("xl_ready")
        small = sem("small")
        msum_done = sem("msum_done")
        msum_ready = sem("msum_ready")
        logits_done = sem("logits_done")
        nmax_ready = sem("nmax_ready")
        rexp_done = sem("rexp_done")
        route = sem("route")
        mask_ready = sem("mask_ready")
        ranks_done = sem("ranks_done")
        head_col = sem("head_col")
        head_row = sem("head_row")
        heads_ready = sem("heads_ready")
        pairs_ready = sem("pairs_ready")
        idx_ready = sem("idx_ready")
        hbo_ready = sem("hbo_ready")
        xg_clear = sem("xg_clear")
        p2_clear = sem("p2_clear")
        fill_done = sem("fill_done")
        fill_act = sem("fill_act")
        fill_dve = sem("fill_dve")
        qk_done = sem("qk_done")
        q2_ready = sem("q2_ready")
        k2_ready = sem("k2_ready")
        v2_in = sem("v2_in")
        v2_ready = sem("v2_ready")
        s2_done = sem("s2_done")
        mx2_ready = sem("mx2_ready")
        sub2_done = sem("sub2_done")
        exp2_done = sem("exp2_done")
        rs2_ready = sem("rs2_ready")
        rinv2_ready = sem("rinv2_ready")
        p2T_ready = sem("p2T_ready")
        pv2_done = sem("pv2_done")
        o2_ready = sem("o2_ready")
        o2_stored = [sem(f"o2_stored{i}") for i in range(2)]
        og_ready = [sem(f"og_ready{s}") for s in range(NSLOT)]
        og2_ready = sem("og2_ready")
        og_turned = sem("og_turned")
        ogT_ready = sem("ogT_ready")
        wo2_done = sem("wo2_done")
        y_ready = sem("y_ready")
        stored = sem("stored")

        def turned_pairs(c):
            return sum(-(-len(x) // 2) for x in CHUNKS[:c + 1])

        NPROJ = 4 * len(CHUNKS)
        HALF_PROJ = NPROJ // 2
        NFILL = 9
        FILL_ACT = [0, 2, 4, 6, 8]
        FILL_DVE = [1, 3, 5, 7]
        QK_ROUNDS = [[0, 1, 2], [3, 4, 5], [6, 7]]

        block = ctx.enter_context(nc.Block())

        @block.sync
        def _(sp):
            def load(name, dst, src):
                sp.dma_start(dst, src).then_inc(ld[name], 16)

            load("cls", h[:, 0, :], a["cls"].partition_broadcast(P))
            load("tokw", tokw, a["tokw"])
            load("x0", xT[:, 0], a["x"][0])
            load("tokb", tokb[:, :], a["tokb"].partition_broadcast(P))
            load("pos", h[:, 1:, :], a["pos"].partition_broadcast(P))
            load("cst", cst[:, :], a["cst"])
            load("wq", wq, a["wq"])
            load("wlat", wlat, a["wlat"])
            load("wk", wk, a["wk"])
            for c in range(1, 4):
                load(f"x{c}", xT[:, c], a["x"][c])
            load("wv", wv[:, :], a["wv"])
            load("wo1", wo1, a["wo1"])
            load("wo2", wo2, a["wo2"])
            load("wr", wr, a["wr"])
            load("bo", bo[:, :], a["bo"].partition_broadcast(P))
            sp.wait_ge(lat_in, len(CHUNKS))
            sp.wait_ge(proj_in, NPROJ)
            for s in range(4):
                load(f"w{s}", wst[:, s, :], a["w"][s])
            for s in range(2):
                sp.wait_ge(w_low, s + 1)
                load(f"w{4 + s}", wst[:, s, :], a["w"][4 + s])
            for v in range(NV):
                sp.wait_ge(o2_ready, v + 1)
                rows = pair_rows[v * PU:(v + 1) * PU, :].rearrange("(g j) (q d) -> j q g d", j=IPG, q=NTOK)
                for j in range(IPG):
                    sp.dma_start(rows[j, 0:16], o2[QROW * j:QROW * j + 16, v % 2]).then_inc(o2_stored[v % 2], 16)
                for j in range(IPG):
                    sp.dma_start(rows[j, 16:17], o2[QROW * j + 16:QROW * j + 17, v % 2])\
                        .then_inc(o2_stored[v % 2], 16)
            for c in CHUNKS:
                sp.wait_ge(y_ready, c[-1] + 1)
                sp.dma_start(out[:, c[0]:c[-1] + 1, :], h[:, c[0]:c[-1] + 1, :]).then_inc(stored, 16)
            sp.wait_ge(stored, 16 * len(CHUNKS))

        @block.gpsimd
        def _(pool):
            pool.wait_ge(ld["tokb"], 16)
            pool.wait_ge(ld["pos"], 16)
            for n in range(1, NTOK):
                pool.tensor_tensor(h[:, n, :], h[:, n, :], tokb[:, :], ALU.add).then_inc(hb_ready, 1)
                if n == 4:
                    for name in ("cst", "wq", "wk"):
                        pool.wait_ge(ld[name], 16)
                    parts = [wq[:, 0], wq[:, 1], wk]
                    for w in parts:
                        pool.tensor_tensor(w[:, 0, :], w[:, 0, :], const("cos"), ALU.mult).then_inc(turning, 1)
                        pool.tensor_tensor(w[:, 1, :], w[:, 1, :], const("sin"), ALU.mult).then_inc(turning, 1)
                    pool.wait_ge(turning, 2 * len(parts))
                    for w in parts:
                        pool.tensor_tensor(w[:, 0, :], w[:, 0, :], w[:, 1, :], ALU.add).then_inc(rotated, 1)

            def expand(u):
                if u >= 2:
                    pool.wait_ge(s_done, u - 1)
                pool.tensor_tensor(
                    free(kx[:, u % 2, 0, :], (ROWH, UI), (NTOK, HH), (1, NTOK)),
                    free(kr[:, 0, UI * NTOK * u:], (NTOK, UI), (0, HH), (1, NTOK)),
                    free(const("own_head"), (0, UI), (1, HH), (0, NTOK)), ALU.mult).then_inc(kx0_ready, 1)

            def normalise(u):
                pool.wait_ge(rinv_ready, u + 1)
                pool.tensor_tensor(p1[:, u % 2, :, 0:NTOK], p1[:, u % 2, :, 0:NTOK],
                                   free(rinv[:, u % 2, :], (1, 32), (0, NTOK)), ALU.mult).then_inc(norm_done, 1)

            def split_low(s):
                pool.wait_ge(w_high, s + 1)
                src = wst[:, s % 4, :]
                pool.tensor_scalar(src, src, WS, None, ALU.mult).then_inc(w_scaled, 1)
                pool.wait_ge(w_scaled, s + 1)
                if s < 4:
                    dst = free(wl[:, s // 2, NE // 2 * (s % 2), :], (1, 1536))
                    high = free(wh[:, s // 2, NE // 2 * (s % 2), :], (1, 1536))
                    pool.tensor_tensor(dst, src, high, ALU.subtract).then_inc(w_low, 1)
                else:
                    part = free(wb[QROW:2 * QROW, NE // 2 * (s - 4), :], (1, 1536))
                    pool.wait_ge(norm_done, s + 1)
                    pool.tensor_tensor(part, src[QROW:2 * QROW], part, ALU.subtract).then_inc(w_low, 1)
                    pool.wait_ge(w_low, s + 1)

            pool.wait_ge(proj_act, HALF_PROJ)
            pool.wait_ge(proj_dve, HALF_PROJ)
            pool.wait_ge(embedded, NPATCH)
            expand(0)
            pool.wait_ge(v_in, NGRP // 2)
            pool.memset(p1, 0.0).then_inc(p1_clear, 1)
            expand(1)
            for u in range(NU):
                if u + 2 < NU:
                    expand(u + 2)
                normalise(u)
                if u < 6:
                    split_low(u)
            pool.wait_ge(wo1_done, NTOK)
            pool.memset(xg, 0.0).then_inc(xg_clear, 1)
            pool.memset(p2, 0.0).then_inc(p2_clear, 1)
            pool.wait_ge(ld["bo"], 16)
            pool.wait_ge(xs_ready, NTOK)
            for n in range(NTOK):
                pool.tensor_tensor(h[:, n, :], h[:, n, :], bo[:, :], ALU.add).then_inc(hbo_ready, 1)
            for i in range(2):
                pool.wait_ge(o2_stored[i], NV // 2 * 8 * 16)
            pool.wait_ge(idx_ready, 1)
            for s in range(NSLOT):
                pool.indirect_dma_start(og[:, s, :], None, pair_rows,
                                        bass.IndirectOffsetOnAxis(ap=idx[:, s:s + 1], axis=0))\
                    .then_inc(og_ready[s], 16)

        @block.scalar
        def _(act):
            def turned(c, k):
                i = (turned_pairs(c - 1) if c else 0) + k
                act.wait_ge(xn_turned, i + 1)
                if c >= 2:
                    act.wait_ge(proj_in, 4 * (c - 2) + 2)
                    act.wait_ge(lat_in, c - 1)
                n = min(2, len(CHUNKS[c]) - 2 * k) * P
                nc.scalar.activation(free(xnT[:, c % 2, 0, 2 * P * k:], (512, KT), (1, n)),
                                     free(bank(2 + k), (256, KT), (1, n)), ACT.Copy).then_inc(xnT_ready, 1)

            def project_out(r):
                act.wait_ge(proj_in, r + 1)
                chunk = CHUNKS[r // 4]
                nc.scalar.activation(free((qr if r % 4 < 2 else kr)[:, r % 2, chunk[0]:], (1, len(chunk)), (NTOK, B)),
                                     free(bank(4 + r % 4), (P, len(chunk)), (1, P)), ACT.Copy).then_inc(proj_act, 1)

            act.wait_ge(ld["cst"], 16)
            act.wait_ge(lat_clear, 1)
            def deviation(n):
                act.wait_ge(mv_ready, n + 1)
                nc.scalar.activation(sd[:, n:n + 1], mv[:, n, 1:2], ACT.Sqrt, bias=const("eps")).then_inc(sd_ready, 1)

            deviation(0)
            for c, chunk in enumerate(CHUNKS):
                for n in CHUNKS[c + 1] if c + 1 < len(CHUNKS) else ():
                    deviation(n)
                for k in range(-(-len(chunk) // 2)):
                    turned(c, k)
                project_out(4 * c)
                act.wait_ge(lat_in, c + 1)
                nc.scalar.activation(free(lat[:, chunk[0]:], (1, len(chunk)), (QROW, B)),
                                     free(bank(2), (P, len(chunk)), (1, P)), ACT.Copy).then_inc(lat_ready, 1)
                project_out(4 * c + 2)
            for r in range(0, NGRP // 2, 2):
                act.wait_ge(v_in, r + 1)
                nc.scalar.activation(free(v1[:, 2 * r, :], (1, BANK)), bank(4 + r % 4), ACT.Copy).then_inc(v_act, 1)

            def expand(u):
                if u >= 2:
                    act.wait_ge(s_done, u - 1)
                for e in range(HH):
                    lo = CONSTS["own_head"][0] + e
                    nc.scalar.activation(free(kx[:, u % 2, 1, e * NTOK:], (ROWH, UI), (1, NTOK)),
                                         free(kr[:, 1, UI * NTOK * u:], (NTOK, UI), (1, NTOK)), ACT.Copy,
                                         scale=cst[:, lo:lo + 1]).then_inc(kx1_ready, 1)

            act.wait_ge(proj_act, HALF_PROJ)
            act.wait_ge(proj_dve, HALF_PROJ)
            act.wait_ge(embedded, NPATCH)
            expand(0)
            expand(1)

            def odd_heads(u):
                act.wait_ge(row_done, 2 * IPG * (u + 1))
                if u >= 1:
                    act.wait_ge(oT_ready, 2 * u)
                nc.scalar.activation(free(odd_part[:, 0, :], (136, 2), (NTOK, UI), (1, NTOK)),
                                     free(bank(4 + 2 * (u % 2), NTOK), (BANK, 2), (2 * NTOK, UI), (1, NTOK)),
                                     ACT.Copy, scale=const("odd")).then_inc(odd_ready, 1)

            def split_high(s):
                act.wait_ge(ld[f"w{s}"], 16)
                dst = free(wh[:, s // 2, NE // 2 * (s % 2), :] if s < 4 else wb[:, NE // 2 * (s - 4), :], (1, 1536))
                nc.scalar.activation(dst, wst[:, s % 4, :], ACT.Copy, scale=WS).then_inc(w_high, 1)

            for i in range(NU + 3):
                if i < NU:
                    act.wait_ge(sub_done, i + 1)
                    nc.scalar.activation(p1[:, i % 2, :, 0:NTOK], p1[:, i % 2, :, 0:NTOK], ACT.Exp,
                                         scale=HD1 ** -0.5).then_inc(exp_done, 1)
                if i >= 3:
                    odd_heads(i - 3)
                if i + 2 < NU:
                    expand(i + 2)
                if i < 6:
                    split_high(i)
            nc.scalar.activation(ident16[:, :], ident, ACT.Copy).then_inc(small, 1)
            for n in range(NTOK + 1):
                if n < NTOK:
                    at = NTOK + n
                    act.wait_ge(mv2_ready, n + 1)
                    nc.scalar.activation(sd[:, at:at + 1], mv[:, at, 1:2], ACT.Sqrt, bias=const("eps"))\
                        .then_inc(sd2_ready, 1)
                if n == 0:
                    continue
                n -= 1
                act.wait_ge(xs_ready, n + 1)
                nc.scalar.activation(xh[:, n, :], xs[:, n % 2, :], ACT.Copy, scale=XS).then_inc(xh_ready, 1)
            act.wait_ge(nmax_ready, 1)
            nc.scalar.activation(rt[:, 32:48], rt[:, 0:16], ACT.Exp, bias=rt[:, 16:17],
                                 accum_out=rt[:, 17:18]).then_inc(rexp_done, 1)
            act.wait_ge(xg_clear, 1)

            def fill_out(v, f):
                at = NFILL * v + f
                act.wait_ge(fill_done, at + 1)
                if v >= 2 and f == 0:
                    act.wait_ge(v2_in, 2 * (v - 1))
                    act.wait_ge(qk_done, 3 * (v - 1))
                if f < 8:
                    dst = free(xg[:, v % 2, f // 2, 8 * (f % 2):], (QROW, PU), (1, 8))
                    src = free(bank(at % 2), (1, PU), (PU, 8))
                else:
                    dst = free(xg[:, v % 2, 0, NPATCH:], (PU * QROW, 4), (QROW, PU))
                    src = free(bank(at % 2), (PU, 4), (1, PU))
                nc.scalar.activation(dst, src, ACT.Copy).then_inc(fill_act, 1)

            def q_out(v, r):
                act.wait_ge(qk_done, 3 * v + r + 1)
                if v >= 2:
                    act.wait_ge(s2_done, v - 1)
                lo, n = QK_ROUNDS[r][0] * 136, 136 * len(QK_ROUNDS[r])
                nc.scalar.activation(q2[:, v % 2, lo:lo + n], bank(2 + (3 * v + r) % 2, 0, n)[0:HD2], ACT.Copy,
                                     scale=1 / (XS * WS)).then_inc(q2_ready, 1)

            def v_out(v, f):
                act.wait_ge(v2_in, 2 * v + f + 1)
                if v >= 2:
                    act.wait_ge(pv2_done, v - 1)
                nc.scalar.activation(free(v2[:, v % 2, 8 * f, :], (1, BANK)), bank(4), ACT.Copy,
                                     scale=1 / (XS * WS)).then_inc(v2_ready, 1)

            for f in FILL_ACT:
                fill_out(0, f)
            for v in range(NV + 1):
                if v < NV:
                    for r in range(3):
                        q_out(v, r)
                    v_out(v, 0)
                    if v + 1 < NV:
                        for f in FILL_ACT[:2]:
                            fill_out(v + 1, f)
                    v_out(v, 1)
                    if v + 1 < NV:
                        for f in FILL_ACT[2:]:
                            fill_out(v + 1, f)
                    act.wait_ge(sub2_done, v + 1)
                    nc.scalar.activation(p2[:, v % 2, :, 0:NTOK], p2[:, v % 2, :, 0:NTOK], ACT.Exp,
                                         scale=HD2 ** -0.5).then_inc(exp2_done, 1)
            for n in range(NTOK):
                act.wait_ge(og_turned, n + 1)
                if n >= 2:
                    act.wait_ge(wo2_done, n - 1)
                nc.scalar.activation(ogT[:, n % 2, :], bank(n % 2, 0, D), ACT.Copy).then_inc(ogT_ready, 1)

        @block.vector
        def _(dve):
            dve.memset(ps[:, 0:4 * BANK], 0.0).then_inc(ps_clear, 1)
            dve.memset(ones[:, :], XS).then_inc(small, 1)

            def norm_stats(n):
                if n:
                    dve.wait_ge(embedded, n)
                    dve.wait_ge(hb_ready, n)
                    dve.tensor_tensor(h[:, n, :], bank((n - 1) % 2, 0, D), h[:, n, :], ALU.add).then_inc(h_ready, 1)
                    dve.wait_ge(h_ready, n)
                dve.bn_stats(stats[:, n, :], h[:, n, :]).then_inc(st_ready, 1)
                dve.wait_ge(st_ready, n + 1)
                dve.bn_aggr(mv[:, n, :], stats[:, n, :]).then_inc(mv_ready, 1)

            def norm_out(n):
                dve.wait_ge(sd_ready, n + 1)
                dve.reciprocal(rstd[:, n:n + 1], sd[:, n:n + 1]).then_inc(rstd_ready, 1)
                dve.wait_ge(rstd_ready, n + 1)
                if n >= 8:
                    c = (n - 8 + 3) // 4
                    dve.wait_ge(xn_turned, turned_pairs(c))
                dve.tensor_scalar(xn[:, n % 8, :], h[:, n, :], mv[:, n, 0:1], rstd[:, n:n + 1],
                                  ALU.subtract, ALU.mult).then_inc(xn_ready, 1)

            def project_out(r):
                dve.wait_ge(proj_in, r + 1)
                chunk = CHUNKS[r // 4]
                dve.tensor_copy(free((qr if r % 4 < 2 else kr)[:, r % 2, chunk[0]:], (1, len(chunk)), (NTOK, B)),
                                free(bank(4 + r % 4), (P, len(chunk)), (1, P))).then_inc(proj_dve, 1)

            dve.memset(lat, 0.0).then_inc(lat_clear, 1)
            dve.wait_ge(ld["cls"], 16)
            norm_stats(0)
            norm_out(0)
            for c in range(1, len(CHUNKS) + 1):
                if c < len(CHUNKS):
                    for n in CHUNKS[c]:
                        norm_stats(n)
                        if n != CHUNKS[c][0]:
                            norm_out(n - 1)
                    norm_out(CHUNKS[c][-1])
                project_out(4 * (c - 1) + 1)
                project_out(4 * (c - 1) + 3)
            for r in range(1, NGRP // 2, 2):
                dve.wait_ge(v_in, r + 1)
                dve.tensor_copy(free(v1[:, 2 * r, :], (1, BANK)), bank(4 + r % 4)).then_inc(v_dve, 1)

            def scores(u):
                return free(bank(2 * (u % 2)), (BANK, 2), (NTOK, 16), (1, NTOK))

            dve.wait_ge(p1_clear, 1)
            for i in range(NU + 3):
                if 2 <= i < NU + 2:
                    u = i - 2
                    dve.wait_ge(norm_done, u + 1)
                    if u >= 2:
                        dve.wait_ge(row_done, 2 * IPG * (u - 1))
                    dve.transpose(free(p1T[:, u % 2], (1, 1024)), free(p1[:, u % 2], (1, 1024)))\
                        .then_inc(p1T_ready, 1)
                if i < NU:
                    u = i
                    dve.wait_ge(s_done, u + 1)
                    dve.tensor_reduce(mx[:, u % 2, :], scores(u), AX_X, ALU.max).then_inc(mx_ready, 1)
                    dve.wait_ge(mx_ready, u + 1)
                    if u >= 2:
                        dve.wait_ge(p1T_ready, u - 1)
                    dve.tensor_tensor(free(p1[:, u % 2], (512, 2), (32, 16), (1, NTOK)), scores(u),
                                      free(mx[:, u % 2, :], (16, 2), (1, 16), (0, NTOK)),
                                      ALU.subtract).then_inc(sub_done, 1)
                if 1 <= i < NU + 1:
                    u = i - 1
                    dve.wait_ge(exp_done, u + 1)
                    dve.tensor_reduce(rs[:, u % 2, :], p1[:, u % 2, :, 0:NTOK], AX_X, ALU.add).then_inc(rs_ready, 1)
                    dve.wait_ge(rs_ready, u + 1)
                    if u >= 2:
                        dve.wait_ge(norm_done, u - 1)
                    dve.reciprocal(rinv[:, u % 2, :], rs[:, u % 2, :]).then_inc(rinv_ready, 1)
                if i >= 3:
                    u = i - 3
                    dve.wait_ge(odd_ready, u + 1)
                    for f in range(2):
                        dve.scalar_tensor_tensor(
                            out=free(oT[:, f, UI * NTOK * u:], (NTOK, UI), (1, NTOK)),
                            in0=free(bank(4 + 2 * (u % 2) + f), (2 * NTOK, UI), (1, NTOK)),
                            scalar=const("even"),
                            in1=free(odd_part[:, f, :], (NTOK, UI), (1, NTOK)),
                            op0=ALU.mult, op1=ALU.add).then_inc(oT_ready, 1)

            def norm2_stats(n):
                dve.wait_ge(wo1_done, n + 1)
                dve.tensor_tensor(h[:, n, :], bank(n % 4, 0, D), h[:, n, :], ALU.add).then_inc(h2_ready, 1)
                dve.wait_ge(h2_ready, n + 1)
                dve.bn_stats(stats[:, NTOK + n, :], h[:, n, :]).then_inc(st2_ready, 1)
                dve.wait_ge(st2_ready, n + 1)
                dve.bn_aggr(mv[:, NTOK + n, :], stats[:, NTOK + n, :]).then_inc(mv2_ready, 1)

            def norm2_out(n):
                dve.wait_ge(sd2_ready, n + 1)
                dve.reciprocal(rstd[:, NTOK + n:NTOK + n + 1], sd[:, NTOK + n:NTOK + n + 1]).then_inc(rstd2_ready, 1)
                dve.wait_ge(rstd2_ready, n + 1)
                if n >= 2:
                    dve.wait_ge(xh_ready, n - 1)
                    dve.wait_ge(xl_ready, n - 1)
                dve.tensor_scalar(xs[:, n % 2, :], h[:, n, :], mv[:, NTOK + n, 0:1], rstd[:, NTOK + n:NTOK + n + 1],
                                  ALU.subtract, ALU.mult).then_inc(xs_ready, 1)

            def low_half(n):
                dve.wait_ge(xh_ready, n + 1)
                dve.scalar_tensor_tensor(out=xl[:, n, :], in0=xs[:, n % 2, :], scalar=XS, in1=xh[:, n, :],
                                         op0=ALU.mult, op1=ALU.subtract).then_inc(xl_ready, 1)

            for n in range(NTOK + 2):
                if n < NTOK:
                    norm2_stats(n)
                if 1 <= n <= NTOK:
                    norm2_out(n - 1)
                if n >= 2:
                    low_half(n - 2)

            steps = [0]

            def step(ins):
                steps[0] += 1
                ins.then_inc(route, 1)
                dve.wait_ge(route, steps[0])

            logits, nmax, total, ex = rt[:, 0:16], rt[:, 16:17], rt[:, 17:18], rt[:, 32:48]
            dist, chosen, slot, count = rt[:, 48:64], rt[:, 64:80], rt[:, 80:96], rt[:, 96:112]
            tiles, base, place, end = rt[:, 112:128], rt[:, 128:144], rt[:, 144:160], rt[:, 160:176]
            rank, inv, head, at_slot = rt[:, 176:192], rt[:, 192:193], rt[:, 193:194], rt[:, 196:200]
            in_head, passed = rt[:, 200:216], rt[:, 216:232]
            sq1, sq2, sl = rt[:, 256:512], rt[:, 512:768], rt[:, 768:832]
            hot = rt[:, 832:832 + NPAIR]
            own = ((1, NE), (0, NE))
            other = ((0, NE), (1, NE))
            square = ((NE, NE), (1, NE))
            tri = free(const("tri"), *square)
            dve.wait_ge(msum_done, 1)
            dve.tensor_copy(free(msumT[:, 0, :], (P, KT), (1, P)), free(bank(4), (BANK, KT), (1, P)))\
                .then_inc(msum_ready, 1)
            dve.wait_ge(logits_done, 1)
            dve.wait_ge(w_low, 6)
            step(dve.scalar_tensor_tensor(out=logits, in0=bank(6, 0, NE), scalar=1 / (NTOK * XS),
                                          in1=const("br"), op0=ALU.mult, op1=ALU.add))
            dve.tensor_reduce(nmax, logits, AX_X, ALU.max, negate=True).then_inc(nmax_ready, 1)
            dve.wait_ge(rexp_done, 1)
            step(dve.reciprocal(inv, total))
            step(dve.tensor_scalar(dist, ex, inv, None, ALU.mult))
            step(dve.tensor_tensor(free(sq1, *square), free(dist, *other), free(dist, *own), ALU.is_gt))
            step(dve.tensor_tensor(free(sq2, *square), free(dist, *other), free(dist, *own), ALU.is_equal))
            step(dve.tensor_tensor(free(sq2, *square), free(sq2, *square), tri, ALU.mult))
            step(dve.tensor_tensor(sq1, sq1, sq2, ALU.add))
            step(dve.tensor_reduce(rank, free(sq1, *square), AX_X, ALU.add))
            dve.tensor_scalar(chosen, rank, float(NSLOT), None, ALU.is_lt).then_inc(mask_ready, 1)
            dve.wait_ge(mask_ready, 1)
            step(dve.tensor_tensor(free(sq1, *square), free(chosen, *other), tri, ALU.mult))
            step(dve.tensor_reduce(slot, free(sq1, *square), AX_X, ALU.add))
            dve.wait_ge(ranks_done, 2)
            step(dve.tensor_copy(count, bank(7, 0, NE)))
            step(dve.tensor_copy(in_head, bank(6, 32, 32 + NE)))
            step(dve.tensor_tensor(free(sq2, *square), free(count, *own), free(const("tile_starts"), *other),
                                   ALU.is_gt))
            step(dve.tensor_reduce(tiles, free(sq2, *square), AX_X, ALU.add))
            step(dve.tensor_tensor(free(sq1, *square), free(tiles, *other), tri, ALU.mult))
            step(dve.tensor_reduce(base, free(sq1, *square), AX_X, ALU.add))
            step(dve.tensor_tensor(end, base, tiles, ALU.add))
            step(dve.tensor_scalar(passed, end, const("row"), None, ALU.is_le))
            step(dve.tensor_reduce(head, passed, AX_X, ALU.add))
            dve.tensor_scalar(head, head, float(NE - 1), None, ALU.min).then_inc(head_col, 1)
            step(dve.scalar_tensor_tensor(out=place, in0=base, scalar=float(TP), in1=in_head,
                                          op0=ALU.mult, op1=ALU.add))
            step(dve.tensor_tensor(place, place, chosen, ALU.mult))
            by_slot = ((NE, NSLOT), (1, NE))
            step(dve.tensor_tensor(free(sl, *by_slot), free(slot, (0, NSLOT), (1, NE)),
                                   free(const("slot"), *by_slot), ALU.is_equal))
            step(dve.tensor_tensor(free(sl, *by_slot), free(sl, *by_slot), free(place, (0, NSLOT), (1, NE)),
                                   ALU.mult))
            step(dve.tensor_reduce(at_slot, free(sl, *by_slot), AX_X, ALU.add))
            dve.tensor_copy(idx[:, :], at_slot).then_inc(idx_ready, 1)
            for s in range(NSLOT):
                if s == 0:
                    step(dve.tensor_scalar(hot, const("pair"), at_slot[:, 0:1], None, ALU.is_equal))
                else:
                    last = s == NSLOT - 1
                    ins = dve.scalar_tensor_tensor(out=pairs_of[:, :] if last else hot, in0=const("pair"),
                                                   scalar=at_slot[:, s:s + 1], in1=hot,
                                                   op0=ALU.is_equal, op1=ALU.add)
                    if last:
                        ins.then_inc(pairs_ready, 1)
                    else:
                        step(ins)
            dve.wait_ge(head_row, 1)
            dve.tensor_copy(heads[0:1, :], bank(7, 64, 64 + NTILE)[0:1]).then_inc(heads_ready, 1)

            dve.wait_ge(xg_clear, 1)
            dve.wait_ge(p2_clear, 1)

            def fill_out(v, f):
                at = NFILL * v + f
                dve.wait_ge(fill_done, at + 1)
                if v >= 2 and f == 1:
                    dve.wait_ge(v2_in, 2 * (v - 1))
                    dve.wait_ge(qk_done, 3 * (v - 1))
                dve.tensor_copy(free(xg[:, v % 2, f // 2, 8 * (f % 2):], (QROW, PU), (1, 8)),
                                free(bank(at % 2), (1, PU), (PU, 8))).then_inc(fill_dve, 1)

            def k_out(v, r):
                dve.wait_ge(qk_done, 3 * v + r + 1)
                if v >= 2:
                    dve.wait_ge(s2_done, v - 1)
                lo, n = QK_ROUNDS[r][0] * 136, 136 * len(QK_ROUNDS[r])
                dve.tensor_scalar(k2[:, v % 2, lo:lo + n], bank(2 + (3 * v + r) % 2, 0, n)[HD2:P], 1 / (XS * WS),
                                  None, ALU.mult).then_inc(k2_ready, 1)

            def scores2():
                return free(bank(5), (NTOK, GU), (1, NTOK))

            def soft_in(v):
                dve.wait_ge(s2_done, v + 1)
                dve.tensor_reduce(mx[:, v % 2, 0:GU], scores2(), AX_X, ALU.max).then_inc(mx2_ready, 1)
                dve.wait_ge(mx2_ready, v + 1)
                if v >= 2:
                    dve.wait_ge(p2T_ready, v - 1)
                dve.tensor_tensor(p2[:, v % 2, :, 0:NTOK], scores2(), free(mx[:, v % 2, :], (1, GU), (0, NTOK)),
                                  ALU.subtract).then_inc(sub2_done, 1)

            def soft_out(v):
                dve.wait_ge(exp2_done, v + 1)
                if v >= 2:
                    dve.wait_ge(pv2_done, v - 1)
                dve.transpose(free(p2T[:, v % 2], (1, 512)), free(p2[:, v % 2], (1, 512))).then_inc(p2T_ready, 1)
                dve.tensor_reduce(rs[:, v % 2, 0:GU], p2[:, v % 2, :, 0:NTOK], AX_X, ALU.add).then_inc(rs2_ready, 1)
                dve.wait_ge(rs2_ready, v + 1)
                if v >= 2:
                    dve.wait_ge(o2_ready, v - 1)
                dve.reciprocal(rinv[:, v % 2, 0:GU], rs[:, v % 2, 0:GU]).then_inc(rinv2_ready, 1)

            def head_out(v):
                dve.wait_ge(pv2_done, v + 1)
                dve.wait_ge(rinv2_ready, v + 1)
                if v >= 2:
                    dve.wait_ge(o2_stored[v % 2], v // 2 * 8 * 16)
                dve.tensor_tensor(o2[:, v % 2], free(bank(6), (HD2, GU), (1, HD2)),
                                  free(rinv[:, v % 2, :], (1, GU), (0, HD2)), ALU.mult).then_inc(o2_ready, 1)

            for f in FILL_DVE:
                fill_out(0, f)
            for v in range(NV + 1):
                if v < NV:
                    for r in range(3):
                        k_out(v, r)
                    if v >= 1:
                        soft_out(v - 1)
                    if v + 1 < NV:
                        for f in FILL_DVE[:2]:
                            fill_out(v + 1, f)
                    if v + 1 < NV:
                        for f in FILL_DVE[2:]:
                            fill_out(v + 1, f)
                    soft_in(v)
                else:
                    soft_out(v - 1)
                if v >= 1:
                    head_out(v - 1)

            for s in range(NSLOT):
                dve.wait_ge(og_ready[s], 16)
                dve.tensor_copy(free(og2[:, 0, HD2 * s:], (D, NTOK), (1, HD2)),
                                free(og[:, s, :], (HD2, NTOK), (1, HD2))).then_inc(og2_ready, 1)
            for n in range(NTOK):
                dve.wait_ge(wo2_done, n + 1)
                dve.wait_ge(hbo_ready, n + 1)
                dve.tensor_tensor(h[:, n, :], bank(2 + n % 2, 0, D), h[:, n, :], ALU.add).then_inc(y_ready, 1)

        @block.tensor
        def _(pe):
            def embed(n):
                c, i = divmod(n - 1, 4)
                pe.wait_ge(ld[f"x{c}"], 16)
                if n > 2:
                    pe.wait_ge(h_ready, n - 2)
                for k in range(PKT):
                    mm = pe.matmul(bank((n - 1) % 2, 0, D), xT[:, c, k, i * P:(i + 1) * P], tokw[:, k, :],
                                   start=k == 0, stop=k == PKT - 1)
                mm.then_inc(embedded, 1)

            def turn(c, k):
                pe.wait_ge(xn_ready, CHUNKS[c][min(2 * k + 1, len(CHUNKS[c]) - 1)] + 1)
                if c >= 1 and k == 0:
                    pe.wait_ge(lat_ready, c)
                if c >= 2 and k == 1:
                    pe.wait_ge(xnT_ready, turned_pairs(c - 1))
                for i, n in enumerate(CHUNKS[c][2 * k:2 * k + 2]):
                    for t in range(KT):
                        mm = pe.transpose(bank(2 + k, 256 * t + P * i, 256 * t + P * i + P),
                                          xn[:, n % 8, P * t:P * t + P], ident)
                mm.then_inc(xn_turned, 1)

            def project(r, moving, weights, kts):
                if r >= 4:
                    pe.wait_ge(proj_dve if r % 2 else proj_act, (r - 4) // 2 + 1)
                n = P * len(CHUNKS[r // 4])
                for k in range(kts):
                    mm = pe.matmul(bank(4 + r % 4, 0, n), weights(k)[:, P * (r % 2):P * (r % 2) + P], moving(k),
                                   start=k == 0, stop=k == kts - 1)
                mm.then_inc(proj_in, 1)

            def qkv(c):
                n = P * len(CHUNKS[c])
                pe.wait_ge(xnT_ready, turned_pairs(c))
                tokens = lambda k: xnT[:, c % 2, k, 0:n]
                project(4 * c, tokens, lambda k: wq[:, k, 0, :], KT)
                project(4 * c + 1, tokens, lambda k: wq[:, k, 0, :], KT)
                for k in range(KT):
                    mm = pe.matmul(bank(2, 0, n), wlat[:, k, :], tokens(k), start=k == 0, stop=k == KT - 1)
                mm.then_inc(lat_in, 1)
                pe.wait_ge(lat_ready, c + 1)
                latents = lambda k: free(lat[:, CHUNKS[c][0]:], (1, len(CHUNKS[c])), (QROW, B))
                project(4 * c + 2, latents, lambda k: wk[:, 0, :], 1)
                project(4 * c + 3, latents, lambda k: wk[:, 0, :], 1)

            pe.wait_ge(ps_clear, 1)
            pe.wait_ge(ld["tokw"], 16)
            for c in range(len(CHUNKS) + 1):
                if 1 <= c < len(CHUNKS):
                    for n in CHUNKS[c]:
                        embed(n)
                if c == 1:
                    for name in ("cst", "wlat"):
                        pe.wait_ge(ld[name], 16)
                    pe.wait_ge(rotated, 3)
                if c >= 1:
                    for k in range(-(-len(CHUNKS[c - 1]) // 2)):
                        turn(c - 1, k)
                    qkv(c - 1)
            pe.wait_ge(ld["wv"], 16)
            for r in range(NGRP // 2):
                if r < 4:
                    pe.wait_ge(proj_dve if r % 2 else proj_act, HALF_PROJ - 1 + r // 2)
                else:
                    pe.wait_ge(v_dve if r % 2 else v_act, (r - 4) // 2 + 1)
                for i in range(2):
                    g = 2 * r + i
                    mm = pe.matmul(bank(4 + r % 4, D * i, D * i + D), lat[:, P * g:P * g + P], wv[:, :],
                                   start=True, stop=True)
                mm.then_inc(v_in, 1)

            def scores(u):
                pe.wait_ge(kx0_ready, u + 1)
                pe.wait_ge(kx1_ready, HH * (u + 1))
                if u >= 2:
                    pe.wait_ge(sub_done, u - 1)
                for f in range(2):
                    for i in range(UI):
                        j, at = QROW * (i % IPG), i // IPG * ROWH
                        img = UI * u + i
                        mm = pe.matmul(bank(2 * (u % 2) + f, at, at + ROWH)[j:j + NTOK],
                                       qr[:, f, NTOK * img:NTOK * img + NTOK],
                                       kx[:, u % 2, f, ROWH * i:ROWH * i + ROWH], start=True, stop=True)
                mm.then_inc(s_done, 1)

            def weigh(u):
                pe.wait_ge(p1T_ready, u + 1)
                if u >= 2:
                    pe.wait_ge(oT_ready, 2 * (u - 1))
                for j in range(IPG):
                    rows = slice(QROW * j, QROW * j + NTOK)
                    for f in range(2):
                        if j:
                            pe.wait_ge(row_done, 2 * (IPG * u + j - 1) + f + 1)
                        for g in range(UG):
                            at = (IPG * g + j) * 2 * NTOK
                            for c in range(4):
                                b = 16 * f + HH * g + 2 * c
                                lo = P * f + QROW * c
                                mm = pe.matmul(bank(4 + 2 * (u % 2) + f, at, at + 2 * NTOK)[QROW * c:QROW * c + QROW],
                                               v1[rows, UG * u + g, lo:lo + QROW],
                                               p1T[rows, u % 2, b:b + 2, 0:NTOK], start=True, stop=True)
                        mm.then_inc(row_done, 1)

            scores(0)
            scores(1)
            pe.wait_ge(v_act, NGRP // 4)
            pe.wait_ge(v_dve, NGRP // 4)
            for u in range(NU):
                if u + 2 < NU:
                    scores(u + 2)
                weigh(u)

            pe.wait_ge(ld["wo1"], 16)
            pe.wait_ge(oT_ready, 2 * NU)
            pe.wait_ge(small, 2)

            def sum_tokens(n):
                pe.wait_ge(xl_ready, n + 1)
                for k in range(KT):
                    for x in (xh, xl):
                        mm = pe.matmul(bank(4 + k, 0, P), x[:, n, P * k:P * k + P], ident16[:, :],
                                       start=n == 0 and x is xh, stop=n == NTOK - 1 and x is xl)
                return mm

            for n in range(NTOK + 3):
                if n < NTOK:
                    if n >= 4:
                        pe.wait_ge(h2_ready, n - 3)
                    for k in range(KT):
                        mm = pe.matmul(bank(n % 4, 0, D), free(oT[:, k, n:], (NTOK, B)), wo1[:, k, :],
                                       start=k == 0, stop=k == KT - 1)
                    mm.then_inc(wo1_done, 1)
                if n >= 3:
                    mm = sum_tokens(n - 3)
            mm.then_inc(msum_done, 1)

            pe.wait_ge(ld["wr"], 16)
            pe.wait_ge(msum_ready, 1)
            for k in range(KT):
                mm = pe.matmul(bank(6, 0, NE), msumT[:, k, :], wr[:, k, :], start=k == 0, stop=k == KT - 1)
            mm.then_inc(logits_done, 1)
            pe.wait_ge(mask_ready, 1)
            chosen = rt[:, 64:80]
            pe.matmul(bank(6, 32, 32 + NE), const("before"), chosen, start=True, stop=True).then_inc(ranks_done, 1)
            pe.matmul(bank(7, 0, NE), const("one"), chosen, start=True, stop=True).then_inc(ranks_done, 1)
            pe.wait_ge(head_col, 1)
            pe.matmul(bank(7, 64, 64 + NTILE)[0:1], rt[:, 193:194], cst[:, 0:NTILE], start=True, stop=True)\
                .then_inc(head_row, 1)

            def gather(v, f):
                at = NFILL * v + f
                if at >= 2:
                    prev = (at - 2) % NFILL
                    w = (at - 2) // NFILL
                    if prev in FILL_ACT:
                        pe.wait_ge(fill_act, len(FILL_ACT) * w + FILL_ACT.index(prev) + 1)
                    else:
                        pe.wait_ge(fill_dve, len(FILL_DVE) * w + FILL_DVE.index(prev) + 1)
                jobs = [(f // 2, 8 * (f % 2) + i) for i in range(8)] if f < 8 else [(k, NPATCH) for k in range(4)]
                for i, (k, n) in enumerate(jobs):
                    x = (xh, xl)[k // KT]
                    lo = P * (k % KT)
                    mm = pe.matmul(bank(at % 2, PU * i, PU * i + PU), x[:, n, lo:lo + P],
                                   pairs_of[:, PU * v:PU * v + PU], start=True, stop=True)
                mm.then_inc(fill_done, 1)

            def gathered(v):
                pe.wait_ge(fill_act, len(FILL_ACT) * (v + 1))
                pe.wait_ge(fill_dve, len(FILL_DVE) * (v + 1))

            TERMS = [(k, w, x) for k in range(KT) for w, x in ((wh, 0), (wl, 0), (wh, 1))]

            def qk(v, r, head):
                at = 3 * v + r
                if at >= 2:
                    pe.wait_ge(q2_ready, at - 1)
                    pe.wait_ge(k2_ready, at - 1)
                for i, t in enumerate(QK_ROUNDS[r]):
                    dst = bank(2 + at % 2, 136 * i, 136 * i + 136)
                    for m, (k, w, x) in enumerate(TERMS):
                        pe.matmul(dst, flat(w[:, k, bass.ds(head[t], 1), 0:P]),
                                  free(xg[:, v % 2, KT * x + k, TP * QROW * t:], (QROW, TP), (1, NTOK)),
                                  start=m == 0, stop=False)
                    mm = pe.matmul(dst, flat(wb[:, bass.ds(head[t], 1), 0:P]), ones[:, :], start=False, stop=True)
                mm.then_inc(qk_done, 1)

            def v_of(v, f, head):
                at = 2 * v + f
                if at >= 1:
                    pe.wait_ge(v2_ready, at)
                for i in range(8):
                    g = 8 * f + i
                    e = head[g * IPG // TP]
                    dst = bank(4, HD2 * i, HD2 * i + HD2)
                    for m, (k, w, x) in enumerate(TERMS):
                        pe.matmul(dst, xg[:, v % 2, KT * x + k, P * g:P * g + P],
                                  flat(w[:, k, bass.ds(e, 1), P:]), start=m == 0, stop=False)
                    mm = pe.matmul(dst, ones[:, 0:P], flat(wb[:, bass.ds(e, 1), P:]), start=False, stop=True)
                mm.then_inc(v2_in, 1)

            def scores2(v):
                pe.wait_ge(q2_ready, 3 * (v + 1))
                pe.wait_ge(k2_ready, 3 * (v + 1))
                if v >= 1:
                    pe.wait_ge(sub2_done, v)
                for p in range(PU):
                    j, at = QROW * (p % IPG), p // IPG * NTOK
                    mm = pe.matmul(bank(5, at, at + NTOK)[j:j + NTOK], q2[:, v % 2, NTOK * p:NTOK * p + NTOK],
                                   k2[:, v % 2, NTOK * p:NTOK * p + NTOK], start=True, stop=True)
                mm.then_inc(s2_done, 1)

            def weigh2(v):
                pe.wait_ge(p2T_ready, v + 1)
                pe.wait_ge(v2_ready, 2 * (v + 1))
                if v >= 1:
                    pe.wait_ge(o2_ready, v)
                for j in range(IPG):
                    rows = slice(QROW * j, QROW * j + NTOK)
                    for g in range(GU):
                        mm = pe.matmul(bank(6 + g // 8, g % 8 * HD2, g % 8 * HD2 + HD2)[rows],
                                       p2T[rows, v % 2, g, 0:NTOK], v2[rows, v % 2, g, :], start=True, stop=True)
                mm.then_inc(pv2_done, 1)

            pe.wait_ge(w_low, 6)
            pe.wait_ge(pairs_ready, 1)
            for f in range(NFILL):
                gather(0, f)
            pe.wait_ge(heads_ready, 1)
            for v in range(NV):
                head = [pe.value_load(heads[0:1, TU * v + t:TU * v + t + 1], min_val=0, max_val=NE - 1)
                        for t in range(TU)]
                gathered(v)
                for r in range(3):
                    qk(v, r, head)
                v_of(v, 0, head)
                if v + 1 < NV:
                    for f in range(4):
                        gather(v + 1, f)
                v_of(v, 1, head)
                if v + 1 < NV:
                    for f in range(4, NFILL):
                        gather(v + 1, f)
                if v >= 1:
                    weigh2(v - 1)
                scores2(v)
            weigh2(NV - 1)

            pe.wait_ge(ld["wo2"], 16)
            pe.wait_ge(og2_ready, NSLOT)
            for n in range(NTOK + 1):
                if n < NTOK:
                    if n >= 2:
                        pe.wait_ge(ogT_ready, n - 1)
                    for k in range(KT):
                        mm = pe.transpose(bank(n % 2, P * k, P * k + P), og2[:, n, P * k:P * k + P], ident)
                    mm.then_inc(og_turned, 1)
                if n >= 1:
                    m = n - 1
                    pe.wait_ge(ogT_ready, m + 1)
                    if m >= 2:
                        pe.wait_ge(y_ready, m - 1)
                    for k in range(KT):
                        mm = pe.matmul(bank(2 + m % 2, 0, D), ogT[:, m % 2, P * k:P * k + P], wo2[:, k, :],
                                       start=k == 0, stop=k == KT - 1)
                    mm.then_inc(wo2_done, 1)



def constants(np, br):
    part = np.arange(P)
    tab = np.zeros((P, NCONST), np.float32)

    def put(name, value):
        lo, hi = CONSTS[name]
        tab[:, lo:hi] = value

    put("ident", np.eye(P))
    put("before", part[:, None] < part[None, :])
    put("one", 1.0)
    put("tri", (np.arange(NE)[None, :] < np.arange(NE)[:, None]).reshape(1, -1))
    put("tile_starts", np.arange(NE)[None, :] * TP)
    put("pair", np.arange(NPAIR)[None, :])
    put("row", part[:, None])
    put("own_head", part[:, None] // HD1 == np.arange(HH)[None, :])
    put("even", (part[:, None] // HD1) % 2 == 0)
    put("odd", (part[:, None] // HD1) % 2 == 1)
    inverse = (1.0 / 10000.0 ** (np.arange(0, HD1, 2, dtype=np.float32) / HD1)).astype(np.float32)
    feature = np.arange(D)
    angle = (feature // HD1).astype(np.float32) * inverse[(feature % HD1) // 2]
    put("cos", np.cos(angle)[None, :])
    put("sin", (np.sin(angle) * np.where(feature % 2 == 0, -1, 1))[None, :])
    put("slot", np.repeat(np.arange(NSLOT), NE)[None, :])
    put("br", br[None, :])
    put("eps", EPS)
    return tab


def kernel(**inputs):
    import numpy as np
    import concourse.bacc as bacc
    from concourse import mybir as mb
    from concourse.bass_utils import run_bass_kernel_spmd

    i = {k: np.asarray(v) for k, v in inputs.items()}

    def tiled(w):
        return np.ascontiguousarray(w.reshape(-1, P, w.shape[1]).transpose(1, 0, 2))

    rows = np.concatenate([np.arange(D), np.arange(D) ^ 1])
    image = i["x"].reshape(B, 3, 4, 16, 4, 16).transpose(2, 1, 3, 5, 4, 0).reshape(4, PKT, P, 512)
    wk = np.zeros((P, 2 * D), np.float32)
    wk[:64] = i["L0_attn_wk_b"][rows].T
    wv = np.zeros((P, D), np.float32)
    wv[64:] = i["L0_attn_wv_b"].T
    heads = [i[f"L0_ffn_W{n}"].reshape(KT, P, NE, HD2) for n in "qkv"]
    w = np.concatenate(heads, axis=3)
    w = w.reshape(KT, P, 2, NE // 2 * 192).transpose(0, 2, 1, 3).reshape(4, P, NE // 2 * 192)
    bias = np.concatenate([i[f"L0_ffn_b{n}"].reshape(NE, HD2) for n in "qkv"], axis=1)
    wb = np.zeros((2, P, NE // 2 * 192), np.float32)
    wb[:, 0] = wb[:, QROW] = bias.reshape(2, NE // 2 * 192)
    arrays = {
        "x": np.ascontiguousarray(image.transpose(0, 2, 1, 3)),
        "tokw": tiled(i["L0_tok_W"].T),
        "tokb": i["L0_tok_b"],
        "pos": i["L0_tok_pos_emb"],
        "cls": i["cls_tok"].reshape(D),
        "cst": constants(np, i["L0_ffn_br"]),
        "wq": tiled(i["L0_attn_wq"][rows].T).reshape(P, KT, 2, D),
        "wlat": tiled(np.concatenate([i["L0_attn_wk_a"], i["L0_attn_wv_a"]]).T),
        "wk": wk.reshape(P, 2, D),
        "wv": wv,
        "wo1": tiled(i["L0_attn_wo"].T),
        "w": np.concatenate([w, wb]),
        "wr": tiled(i["L0_ffn_Wr"]),
        "wo2": tiled(i["L0_ffn_Wo"]),
        "bo": i["L0_ffn_bo"],
    }
    nc = bacc.Bacc("TRN2", target_bir_lowering=False, num_devices=1)
    aps = {n: nc.dram_tensor(f"in_{n}", v.shape, mb.dt.from_np(v.dtype), kind="ExternalInput").ap()
           for n, v in arrays.items()}
    out = nc.dram_tensor("out", (B, NTOK, D), F32, kind="ExternalOutput").ap()
    pair_rows = nc.dram_tensor("pair_rows", (NPAIR, NTOK * HD2), F32, kind="Internal").ap()
    build(nc, aps, out, pair_rows)
    r = run_bass_kernel_spmd(nc, [{f"in_{n}": v for n, v in arrays.items()}], core_ids=[0])
    return r.results[0]["out"]
```

```python
from contextlib import ExitStack

import concourse.bass as bass
from concourse import mybir

ALU = mybir.AluOpType
ACT = mybir.ActivationFunctionType
AX_X = mybir.AxisListType.X
F32 = mybir.dt.float32
F16 = mybir.dt.float16
I32 = mybir.dt.int32

P = 128
B = 128
D = 256
KT = D // P
NPATCH = 16
NTOK = NPATCH + 1
PDIM = 768
PKT = PDIM // P
NH1, HD1 = 16, 16
NE, HD2 = 16, 64
NSLOT = 4
EPS = 1e-5
BANK = 512
QROW = 32
IPG = P // QROW
NGRP = B // IPG

CHUNKS = [[0]] + [[4 * c + 1 + i for i in range(4)] for c in range(NPATCH // 4)]

UG = 2
UI = UG * IPG
NU = NGRP // UG
HH = NH1 // 2
ROWH = HH * NTOK

TP = 8
TU = 8
PU = TP * TU
GU = PU // IPG
NV = -(-(B * NSLOT + NE * (TP - 1)) // TP // TU)
NTILE = NV * TU
NPAIR = NTILE * TP
XS, WS = 16.0, 64.0

CONSTS = {}
_at = 0
CST_FIRST = 0
for _name, _n in (("ident", P), ("own_head", HH), ("even", 1), ("odd", 1), ("eps", 1), ("cos", D), ("sin", D),
                  ("before", P), ("one", P), ("tri", NE * NE), ("tile_starts", NE), ("pair", NPAIR),
                  ("row", 1), ("slot", NSLOT * NE), ("br", NE)):
    CONSTS[_name] = (_at, _at + _n)
    _at += _n
    if _name == "sin":
        CST_FIRST = _at
NCONST = _at


def free(ap, *dims):
    return bass.AP(ap.tensor, ap.offset, [tuple(ap.ap[0])] + [tuple(d) for d in dims])


def flat(ap):
    return ap.rearrange("p a b -> p (a b)")


def build(nc, a, out, pair_rows):
    with ExitStack() as ctx:
        def sb(name, cols, dt=F32):
            return ctx.enter_context(nc.sbuf_tensor(name, [P, cols], dt))

        def sem(name):
            return ctx.enter_context(nc.semaphore(name))

        r1 = sb("r1", 2 * 2 * UI * ROWH + NGRP * D)
        xT = r1[:, 0:4 * PKT * 512].rearrange("p (c k n) -> p c k n", c=4, k=PKT)
        kx = r1[:, 0:4 * UI * ROWH].rearrange("p (u f n) -> p u f n", u=2, f=2)
        v1 = r1[:, 4 * UI * ROWH:].rearrange("p (g d) -> p g d", g=NGRP)
        _half = NTOK * D // 2
        xh = r1[:, 0:_half].bitcast(F16).rearrange("p (n d) -> p n d", n=NTOK)
        xl = r1[:, _half:2 * _half].bitcast(F16).rearrange("p (n d) -> p n d", n=NTOK)
        og = r1[:, 2 * _half:2 * _half + NSLOT * NTOK * HD2].rearrange("p (s n) -> p s n", s=NSLOT)
        og2 = r1[:, 0:NTOK * D].rearrange("p (n d) -> p n d", n=NTOK)
        ogT = r1[:, 4 * _half:4 * _half + 2 * D].rearrange("p (u d) -> p u d", u=2)
        r2 = sb("r2", 6144)
        tokw = r2[:, 0:PKT * D].rearrange("p (k d) -> p k d", k=PKT)
        xn = r2[:, 1536:1536 + 8 * D].rearrange("p (r d) -> p r d", r=8)
        xnT = r2[:, 3584:3584 + 2 * KT * 512].rearrange("p (u k n) -> p u k n", u=2, k=KT)
        wst = r2[:, 0:4 * 1536].rearrange("p (s n) -> p s n", s=4)
        v2 = r2[:, 0:2048].rearrange("p (u g d) -> p u g d", u=2, g=GU)
        o2 = r2[:, 2048:4096].rearrange("p (u g d) -> p u g d", u=2, g=GU)
        p2 = r2[:, 4096:5120].rearrange("p (u g q) -> p u g q", u=2, g=GU)
        p2T = r2[:, 5120:6144].rearrange("p (u g q) -> p u g q", u=2, g=GU)
        r3 = sb("r3", 2 * 2 * B * NTOK + B * QROW)
        qr = r3[:, 0:2 * B * NTOK].rearrange("p (f n) -> p f n", f=2)
        oT = qr
        kr = r3[:, 4352:8704].rearrange("p (f n) -> p f n", f=2)
        lat = r3[:, 8704:8704 + B * QROW]
        p1 = lat[:, 0:2048].rearrange("p (u b q) -> p u b q", u=2, b=32)
        p1T = lat[:, 2048:4096].rearrange("p (u b q) -> p u b q", u=2, b=32)
        xg = r3[:, 0:8192].bitcast(F16).rearrange("p (u k n) -> p u k n", u=2, k=2 * KT)
        q2 = r3[0:HD2, 8192:8192 + 2 * PU * NTOK].rearrange("p (u n) -> p u n", u=2)
        k2 = r3[0:HD2, 10368:10368 + 2 * PU * NTOK].rearrange("p (u n) -> p u n", u=2)
        h = sb("h", NTOK * D)[:, :].rearrange("p (n d) -> p n d", n=NTOK)
        wh = sb("wh", KT * NE * 192, F16)[:, :].rearrange("p (k e d) -> p k e d", k=KT, e=NE)
        wl = sb("wl", KT * NE * 192, F16)[:, :].rearrange("p (k e d) -> p k e d", k=KT, e=NE)
        wb = sb("wb", NE * 192, F16)[:, :].rearrange("p (e d) -> p e d", e=NE)
        ones = sb("ones", TP * NTOK, F16)
        ident16 = sb("ident16", P, F16)
        pairs_of = sb("pairs_of", NPAIR, F16)
        cst = sb("cst", NCONST)
        wq = sb("wq", KT * 2 * D)[:, :].rearrange("p (k t d) -> p k t d", k=KT, t=2)
        wlat = sb("wlat", KT * P)[:, :].rearrange("p (k d) -> p k d", k=KT)
        wk = sb("wk", 2 * D)[:, :].rearrange("p (t d) -> p t d", t=2)
        wv = sb("wv", D)
        wo1 = sb("wo1", KT * D)[:, :].rearrange("p (k d) -> p k d", k=KT)
        wo2 = sb("wo2", KT * D)[:, :].rearrange("p (k d) -> p k d", k=KT)
        wr = sb("wr", KT * NE)[:, :].rearrange("p (k e) -> p k e", k=KT)
        tokb = sb("tokb", D)
        bo = sb("bo", D)
        stats = sb("stats", 2 * NTOK * 6)[:, :].rearrange("p (n s) -> p n s", s=6)
        mv = sb("mv", 2 * NTOK * 2)[:, :].rearrange("p (n s) -> p n s", s=2)
        sd = sb("sd", 2 * NTOK)
        rstd = sb("rstd", 2 * NTOK)
        xs = sb("xs", 2 * D)[:, :].rearrange("p (u d) -> p u d", u=2)
        mx = sb("mx", 2 * 32)[:, :].rearrange("p (u b) -> p u b", u=2)
        rs = sb("rs", 2 * 32)[:, :].rearrange("p (u b) -> p u b", u=2)
        rinv = sb("rinv", 2 * 32)[:, :].rearrange("p (u b) -> p u b", u=2)
        odd_part = sb("odd_part", 2 * 136)[:, :].rearrange("p (f n) -> p f n", f=2)
        msumT = sb("msumT", KT * P)[:, :].rearrange("p (k n) -> p k n", k=KT)
        rt = r2[:, 0:1536]
        idx = sb("idx", NSLOT, I32)
        heads = sb("heads", NTILE, I32)
        ps = ctx.enter_context(nc.psum_tensor("ps", [P, 8 * BANK], F32))

        def bank(i, lo=0, hi=BANK):
            return ps[:, i * BANK + lo:i * BANK + hi]

        def const(name):
            lo, hi = CONSTS[name]
            return cst[:, lo:hi]

        ident = const("ident")

        ld = {n: sem(f"ld_{n}") for n in
              ("tokw", "x0_0", "x0_1", "x0_2", "x0_3", "x1", "x2", "x3", "cst", "cst_rest", "cls", "pos0", "pos1", "tokb", "wq", "wlat", "wk", "wv",
               "wo1", "wo2", "wr", "bo", "w0", "w1", "w2", "w3", "w4", "w5")}
        ps_clear = sem("ps_clear")
        lat_clear = sem("lat_clear")
        p1_clear = sem("p1_clear")
        hb_ready = sem("hb_ready")
        embedded = sem("embedded")
        h_ready = sem("h_ready")
        st_ready = sem("st_ready")
        mv_ready = sem("mv_ready")
        sd_ready = sem("sd_ready")
        rstd_ready = sem("rstd_ready")
        xn_ready = sem("xn_ready")
        xn_turned = sem("xn_turned")
        xnT_ready = sem("xnT_ready")
        turning = sem("turning")
        rotated = sem("rotated")
        proj_in = sem("proj_in")
        proj_act = sem("proj_act")
        proj_dve = sem("proj_dve")
        lat_in = sem("lat_in")
        lat_ready = sem("lat_ready")
        v_in = sem("v_in")
        v_act = sem("v_act")
        v_dve = sem("v_dve")
        kx0_ready = sem("kx0_ready")
        kx1_ready = sem("kx1_ready")
        s_done = sem("s_done")
        mx_ready = sem("mx_ready")
        sub_done = sem("sub_done")
        exp_done = sem("exp_done")
        rs_ready = sem("rs_ready")
        rinv_ready = sem("rinv_ready")
        norm_done = sem("norm_done")
        p1T_ready = sem("p1T_ready")
        pv_done = sem("pv_done")
        odd_ready = sem("odd_ready")
        oT_ready = sem("oT_ready")
        w_high = sem("w_high")
        w_low = sem("w_low")
        wo1_done = sem("wo1_done")
        h2_ready = sem("h2_ready")
        st2_ready = sem("st2_ready")
        mv2_ready = sem("mv2_ready")
        sd2_ready = sem("sd2_ready")
        rstd2_ready = sem("rstd2_ready")
        xs_ready = sem("xs_ready")
        xh_ready = sem("xh_ready")
        xl_ready = sem("xl_ready")
        small = sem("small")
        msum_done = sem("msum_done")
        msum_ready = sem("msum_ready")
        logits_done = sem("logits_done")
        nmax_ready = sem("nmax_ready")
        rexp_done = sem("rexp_done")
        route = sem("route")
        mask_ready = sem("mask_ready")
        ranks_done = sem("ranks_done")
        head_col = sem("head_col")
        head_row = sem("head_row")
        heads_ready = sem("heads_ready")
        pairs_ready = sem("pairs_ready")
        idx_ready = sem("idx_ready")
        hbo_ready = sem("hbo_ready")
        xg_clear = sem("xg_clear")
        p2_clear = sem("p2_clear")
        fill_done = sem("fill_done")
        fill_act = sem("fill_act")
        fill_dve = sem("fill_dve")
        qk_done = sem("qk_done")
        q2_ready = sem("q2_ready")
        k2_ready = sem("k2_ready")
        v2_in = sem("v2_in")
        v2_ready = sem("v2_ready")
        s2_done = sem("s2_done")
        mx2_ready = sem("mx2_ready")
        sub2_done = sem("sub2_done")
        exp2_done = sem("exp2_done")
        rs2_ready = sem("rs2_ready")
        rinv2_ready = sem("rinv2_ready")
        p2T_ready = sem("p2T_ready")
        pv2_done = sem("pv2_done")
        o2_ready = sem("o2_ready")
        o2_stored = [sem(f"o2_stored{i}") for i in range(2)]
        og_ready = [sem(f"og_ready{s}") for s in range(NSLOT)]
        og2_ready = sem("og2_ready")
        og_turned = sem("og_turned")
        ogT_ready = sem("ogT_ready")
        wo2_done = sem("wo2_done")
        y_ready = sem("y_ready")
        stored = sem("stored")

        def turned_pairs(c):
            return sum(-(-len(x) // 2) for x in CHUNKS[:c + 1])

        NPROJ = 4 * len(CHUNKS)
        HALF_PROJ = NPROJ // 2
        NFILL = 9
        FILL_ACT = [0, 2, 4, 6, 8]
        FILL_DVE = [1, 3, 5, 7]
        QK_ROUNDS = [[0, 1, 2], [3, 4, 5], [6, 7]]

        block = ctx.enter_context(nc.Block())

        @block.sync
        def _(sp):
            def load(name, dst, src):
                sp.dma_start(dst, src).then_inc(ld[name], 16)

            load("cls", h[:, 0, :], a["cls"].partition_broadcast(P))
            load("tokw", tokw, a["tokw"])
            def patches(i):
                load(f"x0_{i}", xT[:, 0, :, P * i:P * i + P], a["x"][0, :, :, P * i:P * i + P])

            patches(0)
            load("tokb", tokb[:, :], a["tokb"].partition_broadcast(P))
            load("pos0", h[:, 1:5, :], a["pos"][0:4].partition_broadcast(P))
            patches(1)
            load("cst", cst[:, 0:CST_FIRST], a["cst"][:, 0:CST_FIRST])
            load("wq", wq, a["wq"])
            patches(2)
            patches(3)
            load("wlat", wlat, a["wlat"])
            load("wk", wk, a["wk"])
            load("x1", xT[:, 1], a["x"][1])
            load("pos1", h[:, 5:, :], a["pos"][4:].partition_broadcast(P))
            load("cst_rest", cst[:, CST_FIRST:], a["cst"][:, CST_FIRST:])
            for c in range(2, 4):
                load(f"x{c}", xT[:, c], a["x"][c])
            load("wv", wv[:, :], a["wv"])
            load("wo1", wo1, a["wo1"])
            load("wo2", wo2, a["wo2"])
            load("wr", wr, a["wr"])
            load("bo", bo[:, :], a["bo"].partition_broadcast(P))
            sp.wait_ge(lat_in, len(CHUNKS))
            sp.wait_ge(proj_in, NPROJ)
            for s in range(4):
                load(f"w{s}", wst[:, s, :], a["w"][s])
            for s in range(2):
                sp.wait_ge(w_low, s + 1)
                load(f"w{4 + s}", wst[:, s, :], a["w"][4 + s])
            for v in range(NV):
                sp.wait_ge(o2_ready, v + 1)
                rows = pair_rows[v * PU:(v + 1) * PU, :].rearrange("(g j) (q d) -> j q g d", j=IPG, q=NTOK)
                for j in range(IPG):
                    sp.dma_start(rows[j, 0:16], o2[QROW * j:QROW * j + 16, v % 2]).then_inc(o2_stored[v % 2], 16)
                for j in range(IPG):
                    sp.dma_start(rows[j, 16:17], o2[QROW * j + 16:QROW * j + 17, v % 2])\
                        .then_inc(o2_stored[v % 2], 16)
            for c in CHUNKS:
                sp.wait_ge(y_ready, c[-1] + 1)
                sp.dma_start(out[:, c[0]:c[-1] + 1, :], h[:, c[0]:c[-1] + 1, :]).then_inc(stored, 16)
            sp.wait_ge(stored, 16 * len(CHUNKS))

        @block.gpsimd
        def _(pool):
            pool.memset(lat, 0.0).then_inc(lat_clear, 1)
            pool.wait_ge(ld["tokb"], 16)
            pool.wait_ge(ld["pos0"], 16)

            def bias(n):
                pool.tensor_tensor(h[:, n, :], h[:, n, :], tokb[:, :], ALU.add).then_inc(hb_ready, 1)

            def rotate(w, i):
                pool.tensor_tensor(w[:, 0, :], w[:, 0, :], const("cos"), ALU.mult).then_inc(turning, 1)
                pool.tensor_tensor(w[:, 1, :], w[:, 1, :], const("sin"), ALU.mult).then_inc(turning, 1)
                pool.wait_ge(turning, 2 * i + 2)
                pool.tensor_tensor(w[:, 0, :], w[:, 0, :], w[:, 1, :], ALU.add).then_inc(rotated, 1)

            for n in CHUNKS[1]:
                bias(n)
            pool.wait_ge(ld["cst"], 16)
            pool.wait_ge(ld["wq"], 16)
            for k in range(KT):
                rotate(wq[:, k], k)
            pool.wait_ge(ld["pos1"], 16)
            for n in CHUNKS[2]:
                bias(n)
            pool.wait_ge(ld["wk"], 16)
            rotate(wk, KT)
            for c in CHUNKS[3:]:
                for n in c:
                    bias(n)

            def expand(u):
                if u >= 2:
                    pool.wait_ge(s_done, u - 1)
                pool.tensor_tensor(
                    free(kx[:, u % 2, 0, :], (ROWH, UI), (NTOK, HH), (1, NTOK)),
                    free(kr[:, 0, UI * NTOK * u:], (NTOK, UI), (0, HH), (1, NTOK)),
                    free(const("own_head"), (0, UI), (1, HH), (0, NTOK)), ALU.mult).then_inc(kx0_ready, 1)

            def normalise(u):
                pool.wait_ge(rinv_ready, u + 1)
                pool.tensor_tensor(p1[:, u % 2, :, 0:NTOK], p1[:, u % 2, :, 0:NTOK],
                                   free(rinv[:, u % 2, :], (1, 32), (0, NTOK)), ALU.mult).then_inc(norm_done, 1)

            pool.wait_ge(proj_act, HALF_PROJ)
            pool.wait_ge(proj_dve, HALF_PROJ)
            pool.wait_ge(embedded, NPATCH)
            expand(0)
            expand(1)
            pool.wait_ge(v_in, NGRP // 4)
            pool.memset(p1, 0.0).then_inc(p1_clear, 1)
            for u in range(NU):
                if u + 2 < NU:
                    expand(u + 2)
                normalise(u)
            pool.wait_ge(wo1_done, NTOK)
            pool.memset(xg, 0.0).then_inc(xg_clear, 1)
            pool.memset(p2, 0.0).then_inc(p2_clear, 1)
            pool.wait_ge(ld["bo"], 16)
            pool.wait_ge(xs_ready, NTOK)
            for n in range(NTOK):
                pool.tensor_tensor(h[:, n, :], h[:, n, :], bo[:, :], ALU.add).then_inc(hbo_ready, 1)
            for i in range(2):
                pool.wait_ge(o2_stored[i], NV // 2 * 8 * 16)
            pool.wait_ge(idx_ready, 1)
            for s in range(NSLOT):
                pool.indirect_dma_start(og[:, s, :], None, pair_rows,
                                        bass.IndirectOffsetOnAxis(ap=idx[:, s:s + 1], axis=0))\
                    .then_inc(og_ready[s], 16)

        @block.scalar
        def _(act):
            def turned(c, k):
                i = (turned_pairs(c - 1) if c else 0) + k
                act.wait_ge(xn_turned, i + 1)
                if c >= 2:
                    act.wait_ge(proj_in, 4 * (c - 2) + 2)
                    act.wait_ge(lat_in, c - 1)
                n = min(2, len(CHUNKS[c]) - 2 * k) * P
                nc.scalar.activation(free(xnT[:, c % 2, 0, 2 * P * k:], (512, KT), (1, n)),
                                     free(bank(2 + k), (256, KT), (1, n)), ACT.Copy).then_inc(xnT_ready, 1)

            def project_out(r):
                act.wait_ge(proj_in, r + 1)
                chunk = CHUNKS[r // 4]
                nc.scalar.activation(free((qr if r % 4 < 2 else kr)[:, r % 2, chunk[0]:], (1, len(chunk)), (NTOK, B)),
                                     free(bank(4 + r % 4), (P, len(chunk)), (1, P)), ACT.Copy).then_inc(proj_act, 1)

            act.wait_ge(ld["cst"], 16)
            act.wait_ge(lat_clear, 1)
            def deviation(n):
                act.wait_ge(mv_ready, n + 1)
                nc.scalar.activation(sd[:, n:n + 1], mv[:, n, 1:2], ACT.Sqrt, bias=const("eps")).then_inc(sd_ready, 1)

            def latents_out(c):
                chunk = CHUNKS[c]
                act.wait_ge(lat_in, c + 1)
                for g in range(UG):
                    nc.scalar.activation(
                        free(lat[:, chunk[0] + P * g:], (1, len(chunk)), (QROW * UI, NU), (QROW, IPG)),
                        free(bank(2, g), (P, len(chunk)), (UI, NU), (UG, IPG)), ACT.Copy).then_inc(lat_ready, 1)

            deviation(0)
            for c in range(1, len(CHUNKS) + 1):
                positions = CHUNKS[c] if c < len(CHUNKS) else []
                for n in positions[:3]:
                    deviation(n)
                    if n == positions[0] and c >= 2:
                        project_out(4 * (c - 2) + 2)
                for k in range(-(-len(CHUNKS[c - 1]) // 2)):
                    turned(c - 1, k)
                for n in positions[3:]:
                    deviation(n)
                if not positions:
                    project_out(4 * (c - 2) + 2)
                project_out(4 * (c - 1))
                latents_out(c - 1)
            project_out(4 * (len(CHUNKS) - 1) + 2)
            for r in range(0, NGRP // 2, 2):
                act.wait_ge(v_in, r + 1)
                nc.scalar.activation(free(v1[:, 2 * r, :], (1, BANK)), bank(4 + r % 4), ACT.Copy).then_inc(v_act, 1)

            def expand(u):
                if u >= 2:
                    act.wait_ge(s_done, u - 1)
                for e in range(HH):
                    lo = CONSTS["own_head"][0] + e
                    nc.scalar.activation(free(kx[:, u % 2, 1, e * NTOK:], (ROWH, UI), (1, NTOK)),
                                         free(kr[:, 1, UI * NTOK * u:], (NTOK, UI), (1, NTOK)), ACT.Copy,
                                         scale=cst[:, lo:lo + 1]).then_inc(kx1_ready, 1)

            act.wait_ge(proj_act, HALF_PROJ)
            act.wait_ge(proj_dve, HALF_PROJ)
            act.wait_ge(embedded, NPATCH)
            expand(0)
            expand(1)

            def odd_heads(u):
                act.wait_ge(pv_done, IPG * (u + 1))
                if u >= 1:
                    act.wait_ge(oT_ready, 2 * u)
                nc.scalar.activation(free(odd_part[:, 0, :], (136, 2), (NTOK, UI), (1, NTOK)),
                                     free(bank(4 + 2 * (u % 2), NTOK), (2 * NTOK, 2), (P, UI), (1, NTOK)),
                                     ACT.Copy, scale=const("odd")).then_inc(odd_ready, 1)

            def split_high(s):
                act.wait_ge(ld[f"w{s}"], 16)
                dst = free(wh[:, s // 2, NE // 2 * (s % 2), :] if s < 4 else wb[:, NE // 2 * (s - 4), :], (1, 1536))
                nc.scalar.activation(dst, wst[:, s % 4, :], ACT.Copy, scale=WS).then_inc(w_high, 1)

            for i in range(NU + 3):
                if i < NU:
                    act.wait_ge(sub_done, i + 1)
                    nc.scalar.activation(p1[:, i % 2, :, 0:NTOK], p1[:, i % 2, :, 0:NTOK], ACT.Exp,
                                         scale=HD1 ** -0.5).then_inc(exp_done, 1)
                if i >= 3:
                    odd_heads(i - 3)
                if i + 2 < NU:
                    expand(i + 2)
                if i % 2 == 0 and i < 12:
                    split_high(i // 2)
            nc.scalar.activation(ident16[:, :], ident, ACT.Copy).then_inc(small, 1)
            for n in range(NTOK + 1):
                if n < NTOK:
                    at = NTOK + n
                    act.wait_ge(mv2_ready, n + 1)
                    nc.scalar.activation(sd[:, at:at + 1], mv[:, at, 1:2], ACT.Sqrt, bias=const("eps"))\
                        .then_inc(sd2_ready, 1)
                if n == 0:
                    continue
                n -= 1
                act.wait_ge(xs_ready, n + 1)
                nc.scalar.activation(xh[:, n, :], xs[:, n % 2, :], ACT.Copy, scale=XS).then_inc(xh_ready, 1)
            act.wait_ge(nmax_ready, 1)
            nc.scalar.activation(rt[:, 32:48], rt[:, 0:16], ACT.Exp, bias=rt[:, 16:17],
                                 accum_out=rt[:, 17:18]).then_inc(rexp_done, 1)
            act.wait_ge(xg_clear, 1)

            def fill_out(v, f):
                at = NFILL * v + f
                act.wait_ge(fill_done, at + 1)
                if v >= 2 and f == 0:
                    act.wait_ge(v2_in, 2 * (v - 1))
                    act.wait_ge(qk_done, 3 * (v - 1))
                if f < 8:
                    dst = free(xg[:, v % 2, f // 2, 8 * (f % 2):], (QROW, PU), (1, 8))
                    src = free(bank(at % 2), (1, PU), (PU, 8))
                else:
                    dst = free(xg[:, v % 2, 0, NPATCH:], (PU * QROW, 4), (QROW, PU))
                    src = free(bank(at % 2), (PU, 4), (1, PU))
                nc.scalar.activation(dst, src, ACT.Copy).then_inc(fill_act, 1)

            def q_out(v, r):
                act.wait_ge(qk_done, 3 * v + r + 1)
                if v >= 2:
                    act.wait_ge(s2_done, v - 1)
                lo, n = QK_ROUNDS[r][0] * 136, 136 * len(QK_ROUNDS[r])
                nc.scalar.activation(q2[:, v % 2, lo:lo + n], bank(2 + (3 * v + r) % 2, 0, n)[0:HD2], ACT.Copy,
                                     scale=1 / (XS * WS)).then_inc(q2_ready, 1)

            def v_out(v, f):
                act.wait_ge(v2_in, 2 * v + f + 1)
                if v >= 2:
                    act.wait_ge(pv2_done, IPG * (v - 1))
                nc.scalar.activation(free(v2[:, v % 2, 8 * f, :], (1, BANK)), bank(4), ACT.Copy,
                                     scale=1 / (XS * WS)).then_inc(v2_ready, 1)

            for f in FILL_ACT:
                fill_out(0, f)
            for v in range(NV):
                def next_fill(f):
                    if v + 1 < NV:
                        fill_out(v + 1, f)

                q_out(v, 0)
                next_fill(0)
                q_out(v, 1)
                q_out(v, 2)
                next_fill(2)
                v_out(v, 0)
                next_fill(4)
                v_out(v, 1)
                next_fill(6)
                next_fill(8)
                act.wait_ge(sub2_done, v + 1)
                nc.scalar.activation(p2[:, v % 2, :, 0:NTOK], p2[:, v % 2, :, 0:NTOK], ACT.Exp,
                                     scale=HD2 ** -0.5).then_inc(exp2_done, 1)
            for n in range(NTOK):
                act.wait_ge(og_turned, n + 1)
                if n >= 2:
                    act.wait_ge(wo2_done, n - 1)
                nc.scalar.activation(ogT[:, n % 2, :], bank(n % 2, 0, D), ACT.Copy).then_inc(ogT_ready, 1)

        @block.vector
        def _(dve):
            dve.memset(ps[:, 0:4 * BANK], 0.0).then_inc(ps_clear, 1)
            dve.memset(ones[:, :], XS).then_inc(small, 1)

            def norm_stats(n):
                if n:
                    dve.wait_ge(embedded, n)
                    dve.wait_ge(hb_ready, n)
                    dve.tensor_tensor(h[:, n, :], bank((n - 1) % 2, 0, D), h[:, n, :], ALU.add).then_inc(h_ready, 1)
                    dve.wait_ge(h_ready, n)
                dve.bn_stats(stats[:, n, :], h[:, n, :]).then_inc(st_ready, 1)
                dve.wait_ge(st_ready, n + 1)
                dve.bn_aggr(mv[:, n, :], stats[:, n, :]).then_inc(mv_ready, 1)

            def norm_out(n):
                dve.wait_ge(sd_ready, n + 1)
                dve.reciprocal(rstd[:, n:n + 1], sd[:, n:n + 1]).then_inc(rstd_ready, 1)
                dve.wait_ge(rstd_ready, n + 1)
                if n >= 8:
                    c = (n - 8 + 3) // 4
                    dve.wait_ge(xn_turned, turned_pairs(c))
                dve.tensor_scalar(xn[:, n % 8, :], h[:, n, :], mv[:, n, 0:1], rstd[:, n:n + 1],
                                  ALU.subtract, ALU.mult).then_inc(xn_ready, 1)

            def project_out(r):
                dve.wait_ge(proj_in, r + 1)
                chunk = CHUNKS[r // 4]
                dve.tensor_copy(free((qr if r % 4 < 2 else kr)[:, r % 2, chunk[0]:], (1, len(chunk)), (NTOK, B)),
                                free(bank(4 + r % 4), (P, len(chunk)), (1, P))).then_inc(proj_dve, 1)

            dve.wait_ge(ld["cls"], 16)
            norm_stats(0)
            norm_out(0)
            for c in range(1, len(CHUNKS) + 1):
                if c < len(CHUNKS):
                    for n in CHUNKS[c]:
                        norm_stats(n)
                        if n != CHUNKS[c][0]:
                            norm_out(n - 1)
                        elif c >= 2:
                            project_out(4 * (c - 2) + 3)
                    norm_out(CHUNKS[c][-1])
                else:
                    project_out(4 * (c - 2) + 3)
                project_out(4 * (c - 1) + 1)
            project_out(4 * (len(CHUNKS) - 1) + 3)
            for r in range(1, NGRP // 2, 2):
                dve.wait_ge(v_in, r + 1)
                dve.tensor_copy(free(v1[:, 2 * r, :], (1, BANK)), bank(4 + r % 4)).then_inc(v_dve, 1)

            def scores(u):
                return free(bank(2 * (u % 2)), (BANK, 2), (NTOK, 16), (1, NTOK))

            def split_low(s):
                dve.wait_ge(w_high, s + 1)
                if s < 4:
                    dst = free(wl[:, s // 2, NE // 2 * (s % 2), :], (1, 1536))
                    high = free(wh[:, s // 2, NE // 2 * (s % 2), :], (1, 1536))
                    src = wst[:, s % 4, :]
                else:
                    dst = high = free(wb[QROW:2 * QROW, NE // 2 * (s - 4), :], (1, 1536))
                    src = wst[QROW:2 * QROW, s % 4, :]
                dve.scalar_tensor_tensor(out=dst, in0=src, scalar=WS, in1=high, op0=ALU.mult, op1=ALU.subtract)\
                    .then_inc(w_low, 1)

            dve.wait_ge(p1_clear, 1)
            for i in range(NU + 3):
                if 2 <= i < NU + 2:
                    u = i - 2
                    dve.wait_ge(norm_done, u + 1)
                    if u >= 2:
                        dve.wait_ge(pv_done, IPG * (u - 1))
                    dve.transpose(free(p1T[:, u % 2], (1, 1024)), free(p1[:, u % 2], (1, 1024)))\
                        .then_inc(p1T_ready, 1)
                if i < NU:
                    u = i
                    dve.wait_ge(s_done, u + 1)
                    dve.tensor_reduce(mx[:, u % 2, :], scores(u), AX_X, ALU.max).then_inc(mx_ready, 1)
                    dve.wait_ge(mx_ready, u + 1)
                    if u >= 2:
                        dve.wait_ge(p1T_ready, u - 1)
                    dve.tensor_tensor(free(p1[:, u % 2], (512, 2), (32, 16), (1, NTOK)), scores(u),
                                      free(mx[:, u % 2, :], (16, 2), (1, 16), (0, NTOK)),
                                      ALU.subtract).then_inc(sub_done, 1)
                if 1 <= i < NU + 1:
                    u = i - 1
                    dve.wait_ge(exp_done, u + 1)
                    dve.tensor_reduce(rs[:, u % 2, :], p1[:, u % 2, :, 0:NTOK], AX_X, ALU.add).then_inc(rs_ready, 1)
                    dve.wait_ge(rs_ready, u + 1)
                    if u >= 2:
                        dve.wait_ge(norm_done, u - 1)
                    dve.reciprocal(rinv[:, u % 2, :], rs[:, u % 2, :]).then_inc(rinv_ready, 1)
                if i >= 3:
                    u = i - 3
                    dve.wait_ge(odd_ready, u + 1)
                    for f in range(2):
                        dve.scalar_tensor_tensor(
                            out=free(oT[:, f, UI * NTOK * u:], (NTOK, UI), (1, NTOK)),
                            in0=free(bank(4 + 2 * (u % 2), 2 * NTOK * f), (P, UI), (1, NTOK)),
                            scalar=const("even"),
                            in1=free(odd_part[:, f, :], (NTOK, UI), (1, NTOK)),
                            op0=ALU.mult, op1=ALU.add).then_inc(oT_ready, 1)
                if i % 2 == 0 and i < 12:
                    split_low(i // 2)

            def norm2_stats(n):
                dve.wait_ge(wo1_done, n + 1)
                dve.tensor_tensor(h[:, n, :], bank(n % 4, 0, D), h[:, n, :], ALU.add).then_inc(h2_ready, 1)
                dve.wait_ge(h2_ready, n + 1)
                dve.bn_stats(stats[:, NTOK + n, :], h[:, n, :]).then_inc(st2_ready, 1)
                dve.wait_ge(st2_ready, n + 1)
                dve.bn_aggr(mv[:, NTOK + n, :], stats[:, NTOK + n, :]).then_inc(mv2_ready, 1)

            def norm2_out(n):
                dve.wait_ge(sd2_ready, n + 1)
                dve.reciprocal(rstd[:, NTOK + n:NTOK + n + 1], sd[:, NTOK + n:NTOK + n + 1]).then_inc(rstd2_ready, 1)
                dve.wait_ge(rstd2_ready, n + 1)
                if n >= 2:
                    dve.wait_ge(xh_ready, n - 1)
                    dve.wait_ge(xl_ready, n - 1)
                dve.tensor_scalar(xs[:, n % 2, :], h[:, n, :], mv[:, NTOK + n, 0:1], rstd[:, NTOK + n:NTOK + n + 1],
                                  ALU.subtract, ALU.mult).then_inc(xs_ready, 1)

            def low_half(n):
                dve.wait_ge(xh_ready, n + 1)
                dve.scalar_tensor_tensor(out=xl[:, n, :], in0=xs[:, n % 2, :], scalar=XS, in1=xh[:, n, :],
                                         op0=ALU.mult, op1=ALU.subtract).then_inc(xl_ready, 1)

            for n in range(NTOK + 2):
                if n < NTOK:
                    norm2_stats(n)
                if 1 <= n <= NTOK:
                    norm2_out(n - 1)
                if n >= 2:
                    low_half(n - 2)

            steps = [0]

            def step(ins):
                steps[0] += 1
                ins.then_inc(route, 1)
                dve.wait_ge(route, steps[0])

            logits, nmax, total, ex = rt[:, 0:16], rt[:, 16:17], rt[:, 17:18], rt[:, 32:48]
            dist, chosen, slot, count = rt[:, 48:64], rt[:, 64:80], rt[:, 80:96], rt[:, 96:112]
            tiles, base, place, end = rt[:, 112:128], rt[:, 128:144], rt[:, 144:160], rt[:, 160:176]
            rank, inv, head, at_slot = rt[:, 176:192], rt[:, 192:193], rt[:, 193:194], rt[:, 196:200]
            in_head, passed = rt[:, 200:216], rt[:, 216:232]
            sq1, sq2, sl = rt[:, 256:512], rt[:, 512:768], rt[:, 768:832]
            hot = rt[:, 832:832 + NPAIR]
            own = ((1, NE), (0, NE))
            other = ((0, NE), (1, NE))
            square = ((NE, NE), (1, NE))
            tri = free(const("tri"), *square)
            dve.wait_ge(msum_done, 1)
            dve.tensor_copy(free(msumT[:, 0, :], (P, KT), (1, P)), free(bank(4), (BANK, KT), (1, P)))\
                .then_inc(msum_ready, 1)
            dve.wait_ge(logits_done, 1)
            dve.wait_ge(ld["cst_rest"], 16)
            dve.wait_ge(w_low, 6)
            step(dve.scalar_tensor_tensor(out=logits, in0=bank(6, 0, NE), scalar=1 / (NTOK * XS),
                                          in1=const("br"), op0=ALU.mult, op1=ALU.add))
            dve.tensor_reduce(nmax, logits, AX_X, ALU.max, negate=True).then_inc(nmax_ready, 1)
            dve.wait_ge(rexp_done, 1)
            step(dve.reciprocal(inv, total))
            step(dve.tensor_scalar(dist, ex, inv, None, ALU.mult))
            step(dve.tensor_tensor(free(sq1, *square), free(dist, *other), free(dist, *own), ALU.is_gt))
            step(dve.tensor_tensor(free(sq2, *square), free(dist, *other), free(dist, *own), ALU.is_equal))
            step(dve.tensor_tensor(free(sq2, *square), free(sq2, *square), tri, ALU.mult))
            step(dve.tensor_tensor(sq1, sq1, sq2, ALU.add))
            step(dve.tensor_reduce(rank, free(sq1, *square), AX_X, ALU.add))
            dve.tensor_scalar(chosen, rank, float(NSLOT), None, ALU.is_lt).then_inc(mask_ready, 1)
            dve.wait_ge(mask_ready, 1)
            step(dve.tensor_tensor(free(sq1, *square), free(chosen, *other), tri, ALU.mult))
            step(dve.tensor_reduce(slot, free(sq1, *square), AX_X, ALU.add))
            dve.wait_ge(ranks_done, 2)
            step(dve.tensor_copy(count, bank(7, 0, NE)))
            step(dve.tensor_copy(in_head, bank(6, 32, 32 + NE)))
            step(dve.tensor_tensor(free(sq2, *square), free(count, *own), free(const("tile_starts"), *other),
                                   ALU.is_gt))
            step(dve.tensor_reduce(tiles, free(sq2, *square), AX_X, ALU.add))
            step(dve.tensor_tensor(free(sq1, *square), free(tiles, *other), tri, ALU.mult))
            step(dve.tensor_reduce(base, free(sq1, *square), AX_X, ALU.add))
            step(dve.tensor_tensor(end, base, tiles, ALU.add))
            step(dve.tensor_scalar(passed, end, const("row"), None, ALU.is_le))
            step(dve.tensor_reduce(head, passed, AX_X, ALU.add))
            dve.tensor_scalar(head, head, float(NE - 1), None, ALU.min).then_inc(head_col, 1)
            step(dve.scalar_tensor_tensor(out=place, in0=base, scalar=float(TP), in1=in_head,
                                          op0=ALU.mult, op1=ALU.add))
            step(dve.tensor_tensor(place, place, chosen, ALU.mult))
            by_slot = ((NE, NSLOT), (1, NE))
            step(dve.tensor_tensor(free(sl, *by_slot), free(slot, (0, NSLOT), (1, NE)),
                                   free(const("slot"), *by_slot), ALU.is_equal))
            step(dve.tensor_tensor(free(sl, *by_slot), free(sl, *by_slot), free(place, (0, NSLOT), (1, NE)),
                                   ALU.mult))
            step(dve.tensor_reduce(at_slot, free(sl, *by_slot), AX_X, ALU.add))
            dve.tensor_copy(idx[:, :], at_slot).then_inc(idx_ready, 1)
            for s in range(NSLOT):
                if s == 0:
                    step(dve.tensor_scalar(hot, const("pair"), at_slot[:, 0:1], None, ALU.is_equal))
                else:
                    last = s == NSLOT - 1
                    ins = dve.scalar_tensor_tensor(out=pairs_of[:, :] if last else hot, in0=const("pair"),
                                                   scalar=at_slot[:, s:s + 1], in1=hot,
                                                   op0=ALU.is_equal, op1=ALU.add)
                    if last:
                        ins.then_inc(pairs_ready, 1)
                    else:
                        step(ins)
            dve.wait_ge(head_row, 1)
            dve.tensor_copy(heads[0:1, :], bank(7, 64, 64 + NTILE)[0:1]).then_inc(heads_ready, 1)

            dve.wait_ge(xg_clear, 1)
            dve.wait_ge(p2_clear, 1)

            def fill_out(v, f):
                at = NFILL * v + f
                dve.wait_ge(fill_done, at + 1)
                if v >= 2 and f == 1:
                    dve.wait_ge(v2_in, 2 * (v - 1))
                    dve.wait_ge(qk_done, 3 * (v - 1))
                dve.tensor_copy(free(xg[:, v % 2, f // 2, 8 * (f % 2):], (QROW, PU), (1, 8)),
                                free(bank(at % 2), (1, PU), (PU, 8))).then_inc(fill_dve, 1)

            def k_out(v, r):
                dve.wait_ge(qk_done, 3 * v + r + 1)
                if v >= 2:
                    dve.wait_ge(s2_done, v - 1)
                lo, n = QK_ROUNDS[r][0] * 136, 136 * len(QK_ROUNDS[r])
                dve.tensor_scalar(k2[:, v % 2, lo:lo + n], bank(2 + (3 * v + r) % 2, 0, n)[HD2:P], 1 / (XS * WS),
                                  None, ALU.mult).then_inc(k2_ready, 1)

            def scores2():
                return free(bank(5), (NTOK, GU), (1, NTOK))

            def soft_in(v):
                dve.wait_ge(s2_done, v + 1)
                dve.tensor_reduce(mx[:, v % 2, 0:GU], scores2(), AX_X, ALU.max).then_inc(mx2_ready, 1)
                dve.wait_ge(mx2_ready, v + 1)
                if v >= 2:
                    dve.wait_ge(p2T_ready, v - 1)
                dve.tensor_tensor(p2[:, v % 2, :, 0:NTOK], scores2(), free(mx[:, v % 2, :], (1, GU), (0, NTOK)),
                                  ALU.subtract).then_inc(sub2_done, 1)

            def soft_out(v):
                dve.wait_ge(exp2_done, v + 1)
                if v >= 2:
                    dve.wait_ge(pv2_done, IPG * (v - 1))
                dve.transpose(free(p2T[:, v % 2], (1, 512)), free(p2[:, v % 2], (1, 512))).then_inc(p2T_ready, 1)
                dve.tensor_reduce(rs[:, v % 2, 0:GU], p2[:, v % 2, :, 0:NTOK], AX_X, ALU.add).then_inc(rs2_ready, 1)
                dve.wait_ge(rs2_ready, v + 1)
                if v >= 2:
                    dve.wait_ge(o2_ready, v - 1)
                dve.reciprocal(rinv[:, v % 2, 0:GU], rs[:, v % 2, 0:GU]).then_inc(rinv2_ready, 1)

            def head_out(v):
                dve.wait_ge(pv2_done, IPG * (v + 1))
                dve.wait_ge(rinv2_ready, v + 1)
                if v >= 2:
                    dve.wait_ge(o2_stored[v % 2], v // 2 * 8 * 16)
                dve.tensor_tensor(o2[:, v % 2], free(bank(6), (HD2, GU), (1, HD2)),
                                  free(rinv[:, v % 2, :], (1, GU), (0, HD2)), ALU.mult).then_inc(o2_ready, 1)

            for f in FILL_DVE:
                fill_out(0, f)
            for v in range(NV):
                def next_fill(f):
                    if v + 1 < NV:
                        fill_out(v + 1, f)

                k_out(v, 0)
                k_out(v, 1)
                next_fill(1)
                k_out(v, 2)
                if v >= 1:
                    soft_out(v - 1)
                next_fill(3)
                next_fill(5)
                next_fill(7)
                if v >= 1:
                    head_out(v - 1)
                soft_in(v)
            soft_out(NV - 1)
            head_out(NV - 1)

            for s in range(NSLOT):
                dve.wait_ge(og_ready[s], 16)
                dve.tensor_copy(free(og2[:, 0, HD2 * s:], (D, NTOK), (1, HD2)),
                                free(og[:, s, :], (HD2, NTOK), (1, HD2))).then_inc(og2_ready, 1)
            for n in range(NTOK):
                dve.wait_ge(wo2_done, n + 1)
                dve.wait_ge(hbo_ready, n + 1)
                dve.tensor_tensor(h[:, n, :], bank(2 + n % 2, 0, D), h[:, n, :], ALU.add).then_inc(y_ready, 1)

        @block.tensor
        def _(pe):
            def embed(n):
                c, i = divmod(n - 1, 4)
                pe.wait_ge(ld[f"x{c}" if c else f"x0_{i}"], 16)
                if n > 2:
                    pe.wait_ge(h_ready, n - 2)
                for k in range(PKT):
                    mm = pe.matmul(bank((n - 1) % 2, 0, D), xT[:, c, k, i * P:(i + 1) * P], tokw[:, k, :],
                                   start=k == 0, stop=k == PKT - 1)
                mm.then_inc(embedded, 1)

            def turn(c, k):
                pe.wait_ge(xn_ready, CHUNKS[c][min(2 * k + 1, len(CHUNKS[c]) - 1)] + 1)
                if c >= 1 and k == 0:
                    pe.wait_ge(lat_ready, UG * c)
                if c >= 2 and k == 1:
                    pe.wait_ge(xnT_ready, turned_pairs(c - 1))
                for i, n in enumerate(CHUNKS[c][2 * k:2 * k + 2]):
                    for t in range(KT):
                        mm = pe.transpose(bank(2 + k, 256 * t + P * i, 256 * t + P * i + P),
                                          xn[:, n % 8, P * t:P * t + P], ident)
                mm.then_inc(xn_turned, 1)

            def project(r, moving, weights, kts):
                if r >= 4:
                    pe.wait_ge(proj_dve if r % 2 else proj_act, (r - 4) // 2 + 1)
                n = P * len(CHUNKS[r // 4])
                for k in range(kts):
                    mm = pe.matmul(bank(4 + r % 4, 0, n), weights(k)[:, P * (r % 2):P * (r % 2) + P], moving(k),
                                   start=k == 0, stop=k == kts - 1)
                mm.then_inc(proj_in, 1)

            def q_and_latents(c):
                n = P * len(CHUNKS[c])
                pe.wait_ge(xnT_ready, turned_pairs(c))
                if c == 0:
                    pe.wait_ge(rotated, 2)
                tokens = lambda k: xnT[:, c % 2, k, 0:n]
                project(4 * c, tokens, lambda k: wq[:, k, 0, :], KT)
                project(4 * c + 1, tokens, lambda k: wq[:, k, 0, :], KT)
                if c == 0:
                    pe.wait_ge(ld["wlat"], 16)
                for k in range(KT):
                    mm = pe.matmul(bank(2, 0, n), wlat[:, k, :], tokens(k), start=k == 0, stop=k == KT - 1)
                mm.then_inc(lat_in, 1)

            def keys(c):
                if c == 0:
                    pe.wait_ge(rotated, 3)
                pe.wait_ge(lat_ready, UG * (c + 1))
                latents = lambda k: free(lat[:, CHUNKS[c][0]:], (1, len(CHUNKS[c])), (QROW, B))
                project(4 * c + 2, latents, lambda k: wk[:, 0, :], 1)
                project(4 * c + 3, latents, lambda k: wk[:, 0, :], 1)

            pe.wait_ge(ps_clear, 1)
            pe.wait_ge(ld["tokw"], 16)
            for c in range(1, len(CHUNKS) + 1):
                positions = CHUNKS[c] if c < len(CHUNKS) else []
                for n in positions[:3]:
                    embed(n)
                    if n == positions[0] and c >= 2:
                        keys(c - 2)
                if c == 1:
                    pe.wait_ge(ld["cst"], 16)
                for k in range(-(-len(CHUNKS[c - 1]) // 2)):
                    turn(c - 1, k)
                for n in positions[3:]:
                    embed(n)
                if not positions:
                    keys(c - 2)
                q_and_latents(c - 1)
            keys(len(CHUNKS) - 1)
            pe.wait_ge(ld["wv"], 16)
            for r in range(NGRP // 2):
                if r < 4:
                    pe.wait_ge(proj_dve if r % 2 else proj_act, HALF_PROJ - 1 + r // 2)
                else:
                    pe.wait_ge(v_dve if r % 2 else v_act, (r - 4) // 2 + 1)
                for i in range(2):
                    g = 2 * r + i
                    mm = pe.matmul(bank(4 + r % 4, D * i, D * i + D), lat[:, P * g:P * g + P], wv[:, :],
                                   start=True, stop=True)
                mm.then_inc(v_in, 1)

            def scores(u):
                pe.wait_ge(kx0_ready, u + 1)
                pe.wait_ge(kx1_ready, HH * (u + 1))
                if u >= 2:
                    pe.wait_ge(sub_done, u - 1)
                for f in range(2):
                    for i in range(UI):
                        j, at = QROW * (i % IPG), i // IPG * ROWH
                        img = UI * u + UG * (i % IPG) + i // IPG
                        mm = pe.matmul(bank(2 * (u % 2) + f, at, at + ROWH)[j:j + NTOK],
                                       qr[:, f, NTOK * img:NTOK * img + NTOK],
                                       kx[:, u % 2, f, ROWH * i:ROWH * i + ROWH], start=True, stop=True)
                mm.then_inc(s_done, 1)

            def weigh(u):
                pe.wait_ge(p1T_ready, u + 1)
                if u >= 2:
                    pe.wait_ge(oT_ready, 2 * (u - 1))
                for turn, j in enumerate((0, 2, 1, 3)):
                    rows = slice(QROW * j, QROW * j + NTOK)
                    if turn >= 2:
                        pe.wait_ge(pv_done, IPG * u + turn - 1)
                    for g in range(UG):
                        for f in range(2):
                            at = 2 * P * (j % 2) + P * g + 2 * NTOK * f
                            for c in range(4):
                                b = 16 * f + HH * g + 2 * c
                                lo = P * f + QROW * c
                                mm = pe.matmul(bank(4 + 2 * (u % 2) + j // 2, at, at + 2 * NTOK)[QROW * c:QROW * c + QROW],
                                               v1[rows, UG * u + g, lo:lo + QROW],
                                               p1T[rows, u % 2, b:b + 2, 0:NTOK], start=True, stop=True)
                    mm.then_inc(pv_done, 1)

            scores(0)
            scores(1)
            pe.wait_ge(v_act, NGRP // 4)
            pe.wait_ge(v_dve, NGRP // 4)
            for u in range(NU):
                if u + 2 < NU:
                    scores(u + 2)
                weigh(u)

            pe.wait_ge(ld["wo1"], 16)
            pe.wait_ge(oT_ready, 2 * NU)
            pe.wait_ge(small, 2)

            def sum_tokens(n):
                pe.wait_ge(xl_ready, n + 1)
                for k in range(KT):
                    for x in (xh, xl):
                        mm = pe.matmul(bank(4 + k, 0, P), x[:, n, P * k:P * k + P], ident16[:, :],
                                       start=n == 0 and x is xh, stop=n == NTOK - 1 and x is xl)
                return mm

            for n in range(NTOK + 3):
                if n < NTOK:
                    if n >= 4:
                        pe.wait_ge(h2_ready, n - 3)
                    for k in range(KT):
                        mm = pe.matmul(bank(n % 4, 0, D), free(oT[:, k, n:], (NTOK, B)), wo1[:, k, :],
                                       start=k == 0, stop=k == KT - 1)
                    mm.then_inc(wo1_done, 1)
                if n >= 3:
                    mm = sum_tokens(n - 3)
            mm.then_inc(msum_done, 1)

            pe.wait_ge(ld["wr"], 16)
            pe.wait_ge(msum_ready, 1)
            for k in range(KT):
                mm = pe.matmul(bank(6, 0, NE), msumT[:, k, :], wr[:, k, :], start=k == 0, stop=k == KT - 1)
            mm.then_inc(logits_done, 1)
            pe.wait_ge(mask_ready, 1)
            chosen = rt[:, 64:80]
            pe.matmul(bank(6, 32, 32 + NE), const("before"), chosen, start=True, stop=True).then_inc(ranks_done, 1)
            pe.matmul(bank(7, 0, NE), const("one"), chosen, start=True, stop=True).then_inc(ranks_done, 1)
            pe.wait_ge(head_col, 1)
            pe.matmul(bank(7, 64, 64 + NTILE)[0:1], rt[:, 193:194], cst[:, 0:NTILE], start=True, stop=True)\
                .then_inc(head_row, 1)

            def gather(v, f):
                at = NFILL * v + f
                if at >= 2:
                    prev = (at - 2) % NFILL
                    w = (at - 2) // NFILL
                    if prev in FILL_ACT:
                        pe.wait_ge(fill_act, len(FILL_ACT) * w + FILL_ACT.index(prev) + 1)
                    else:
                        pe.wait_ge(fill_dve, len(FILL_DVE) * w + FILL_DVE.index(prev) + 1)
                jobs = [(f // 2, 8 * (f % 2) + i) for i in range(8)] if f < 8 else [(k, NPATCH) for k in range(4)]
                for i, (k, n) in enumerate(jobs):
                    x = (xh, xl)[k // KT]
                    lo = P * (k % KT)
                    mm = pe.matmul(bank(at % 2, PU * i, PU * i + PU), x[:, n, lo:lo + P],
                                   pairs_of[:, PU * v:PU * v + PU], start=True, stop=True)
                mm.then_inc(fill_done, 1)

            def gathered(v):
                pe.wait_ge(fill_act, len(FILL_ACT) * (v + 1))
                pe.wait_ge(fill_dve, len(FILL_DVE) * (v + 1))

            TERMS = [(k, w, x) for k in range(KT) for w, x in ((wh, 0), (wl, 0), (wh, 1))]

            def qk(v, r, head):
                at = 3 * v + r
                if at >= 2:
                    pe.wait_ge(q2_ready, at - 1)
                    pe.wait_ge(k2_ready, at - 1)
                for i, t in enumerate(QK_ROUNDS[r]):
                    dst = bank(2 + at % 2, 136 * i, 136 * i + 136)
                    for m, (k, w, x) in enumerate(TERMS):
                        pe.matmul(dst, flat(w[:, k, bass.ds(head[t], 1), 0:P]),
                                  free(xg[:, v % 2, KT * x + k, TP * QROW * t:], (QROW, TP), (1, NTOK)),
                                  start=m == 0, stop=False)
                    mm = pe.matmul(dst, flat(wb[:, bass.ds(head[t], 1), 0:P]), ones[:, :], start=False, stop=True)
                mm.then_inc(qk_done, 1)

            def v_of(v, f, head):
                at = 2 * v + f
                if at >= 1:
                    pe.wait_ge(v2_ready, at)
                for i in range(8):
                    g = 8 * f + i
                    e = head[g * IPG // TP]
                    dst = bank(4, HD2 * i, HD2 * i + HD2)
                    for m, (k, w, x) in enumerate(TERMS):
                        pe.matmul(dst, xg[:, v % 2, KT * x + k, P * g:P * g + P],
                                  flat(w[:, k, bass.ds(e, 1), P:]), start=m == 0, stop=False)
                    mm = pe.matmul(dst, ones[:, 0:P], flat(wb[:, bass.ds(e, 1), P:]), start=False, stop=True)
                mm.then_inc(v2_in, 1)

            def scores2(v):
                pe.wait_ge(q2_ready, 3 * (v + 1))
                pe.wait_ge(k2_ready, 3 * (v + 1))
                if v >= 1:
                    pe.wait_ge(sub2_done, v)
                for p in range(PU):
                    j, at = QROW * (p % IPG), p // IPG * NTOK
                    mm = pe.matmul(bank(5, at, at + NTOK)[j:j + NTOK], q2[:, v % 2, NTOK * p:NTOK * p + NTOK],
                                   k2[:, v % 2, NTOK * p:NTOK * p + NTOK], start=True, stop=True)
                mm.then_inc(s2_done, 1)

            def weigh2(v, js=range(IPG)):
                pe.wait_ge(p2T_ready, v + 1)
                pe.wait_ge(v2_ready, 2 * (v + 1))
                if v >= 1:
                    pe.wait_ge(o2_ready, v)
                for j in js:
                    rows = slice(QROW * j, QROW * j + NTOK)
                    for g in range(GU):
                        mm = pe.matmul(bank(6 + g // 8, g % 8 * HD2, g % 8 * HD2 + HD2)[rows],
                                       p2T[rows, v % 2, g, 0:NTOK], v2[rows, v % 2, g, :], start=True, stop=True)
                    mm.then_inc(pv2_done, 1)

            pe.wait_ge(w_low, 6)
            pe.wait_ge(pairs_ready, 1)
            for f in range(NFILL):
                gather(0, f)
            def heads_of(v):
                _, head = nc.values_load_multi_w_load_instructions(
                    heads[0:1, TU * v:TU * v + TU], engines=(mybir.EngineType.PE,), min_val=0, max_val=NE - 1,
                    skip_runtime_bounds_check_because="a count of heads, and no more than NE - 1")
                return head

            pe.wait_ge(heads_ready, 1)
            for v in range(NV):
                head = heads_of(v)
                gathered(v)

                def next_fill(f):
                    if v + 1 < NV:
                        gather(v + 1, f)

                for r in range(3):
                    qk(v, r, head)
                    next_fill(r)
                v_of(v, 0, head)
                next_fill(3)
                next_fill(4)
                v_of(v, 1, head)
                next_fill(5)
                next_fill(6)
                if v >= 1:
                    weigh2(v - 1, range(2))
                next_fill(7)
                if v >= 1:
                    weigh2(v - 1, range(2, IPG))
                next_fill(8)
                scores2(v)
            weigh2(NV - 1)

            pe.wait_ge(ld["wo2"], 16)
            pe.wait_ge(og2_ready, NSLOT)
            for n in range(NTOK + 1):
                if n < NTOK:
                    if n >= 2:
                        pe.wait_ge(ogT_ready, n - 1)
                    for k in range(KT):
                        mm = pe.transpose(bank(n % 2, P * k, P * k + P), og2[:, n, P * k:P * k + P], ident)
                    mm.then_inc(og_turned, 1)
                if n >= 1:
                    m = n - 1
                    pe.wait_ge(ogT_ready, m + 1)
                    if m >= 2:
                        pe.wait_ge(y_ready, m - 1)
                    for k in range(KT):
                        mm = pe.matmul(bank(2 + m % 2, 0, D), ogT[:, m % 2, P * k:P * k + P], wo2[:, k, :],
                                       start=k == 0, stop=k == KT - 1)
                    mm.then_inc(wo2_done, 1)



def constants(np, br):
    part = np.arange(P)
    tab = np.zeros((P, NCONST), np.float32)

    def put(name, value):
        lo, hi = CONSTS[name]
        tab[:, lo:hi] = value

    put("ident", np.eye(P))
    put("before", part[:, None] < part[None, :])
    put("one", 1.0)
    put("tri", (np.arange(NE)[None, :] < np.arange(NE)[:, None]).reshape(1, -1))
    put("tile_starts", np.arange(NE)[None, :] * TP)
    put("pair", np.arange(NPAIR)[None, :])
    put("row", part[:, None])
    put("own_head", part[:, None] // HD1 == np.arange(HH)[None, :])
    put("even", (part[:, None] // HD1) % 2 == 0)
    put("odd", (part[:, None] // HD1) % 2 == 1)
    inverse = (1.0 / 10000.0 ** (np.arange(0, HD1, 2, dtype=np.float32) / HD1)).astype(np.float32)
    feature = np.arange(D)
    angle = (feature // HD1).astype(np.float32) * inverse[(feature % HD1) // 2]
    put("cos", np.cos(angle)[None, :])
    put("sin", (np.sin(angle) * np.where(feature % 2 == 0, -1, 1))[None, :])
    put("slot", np.repeat(np.arange(NSLOT), NE)[None, :])
    put("br", br[None, :])
    put("eps", EPS)
    return tab


def kernel(**inputs):
    import numpy as np
    import concourse.bacc as bacc
    from concourse import mybir as mb
    from concourse.bass_utils import run_bass_kernel_spmd

    i = {k: np.asarray(v) for k, v in inputs.items()}

    def tiled(w):
        return np.ascontiguousarray(w.reshape(-1, P, w.shape[1]).transpose(1, 0, 2))

    rows = np.concatenate([np.arange(D), np.arange(D) ^ 1])
    image = i["x"].reshape(B, 3, 4, 16, 4, 16).transpose(2, 1, 3, 5, 4, 0).reshape(4, PKT, P, 512)
    wk = np.zeros((P, 2 * D), np.float32)
    wk[:64] = i["L0_attn_wk_b"][rows].T
    wv = np.zeros((P, D), np.float32)
    wv[64:] = i["L0_attn_wv_b"].T
    heads = [i[f"L0_ffn_W{n}"].reshape(KT, P, NE, HD2) for n in "qkv"]
    w = np.concatenate(heads, axis=3)
    w = w.reshape(KT, P, 2, NE // 2 * 192).transpose(0, 2, 1, 3).reshape(4, P, NE // 2 * 192)
    bias = np.concatenate([i[f"L0_ffn_b{n}"].reshape(NE, HD2) for n in "qkv"], axis=1)
    wb = np.zeros((2, P, NE // 2 * 192), np.float32)
    wb[:, 0] = wb[:, QROW] = bias.reshape(2, NE // 2 * 192)
    arrays = {
        "x": np.ascontiguousarray(image.transpose(0, 2, 1, 3)),
        "tokw": tiled(i["L0_tok_W"].T),
        "tokb": i["L0_tok_b"],
        "pos": i["L0_tok_pos_emb"],
        "cls": i["cls_tok"].reshape(D),
        "cst": constants(np, i["L0_ffn_br"]),
        "wq": tiled(i["L0_attn_wq"][rows].T).reshape(P, KT, 2, D),
        "wlat": tiled(np.concatenate([i["L0_attn_wk_a"], i["L0_attn_wv_a"]]).T),
        "wk": wk.reshape(P, 2, D),
        "wv": wv,
        "wo1": tiled(i["L0_attn_wo"].T),
        "w": np.concatenate([w, wb]),
        "wr": tiled(i["L0_ffn_Wr"]),
        "wo2": tiled(i["L0_ffn_Wo"]),
        "bo": i["L0_ffn_bo"],
    }
    nc = bacc.Bacc("TRN2", target_bir_lowering=False, num_devices=1)
    aps = {n: nc.dram_tensor(f"in_{n}", v.shape, mb.dt.from_np(v.dtype), kind="ExternalInput").ap()
           for n, v in arrays.items()}
    out = nc.dram_tensor("out", (B, NTOK, D), F32, kind="ExternalOutput").ap()
    pair_rows = nc.dram_tensor("pair_rows", (NPAIR, NTOK * HD2), F32, kind="Internal").ap()
    build(nc, aps, out, pair_rows)
    r = run_bass_kernel_spmd(nc, [{f"in_{n}": v for n, v in arrays.items()}], core_ids=[0])
    return r.results[0]["out"]
```

```python
from contextlib import ExitStack

import concourse.bass as bass
from concourse import mybir

ALU = mybir.AluOpType
ACT = mybir.ActivationFunctionType
AX_X = mybir.AxisListType.X
F32 = mybir.dt.float32
F16 = mybir.dt.float16
I32 = mybir.dt.int32

P = 128
B = 128
D = 256
KT = D // P
NPATCH = 16
NTOK = NPATCH + 1
PDIM = 768
PKT = PDIM // P
NH1, HD1 = 16, 16
NE, HD2 = 16, 64
NSLOT = 4
EPS = 1e-5
BANK = 512
QROW = 32
IPG = P // QROW
NGRP = B // IPG

CHUNKS = [[0]] + [[4 * c + 1 + i for i in range(4)] for c in range(NPATCH // 4)]

UG = 2
UI = UG * IPG
NU = NGRP // UG
HH = NH1 // 2
ROWH = HH * NTOK

TP = 8
TU = 8
PU = TP * TU
GU = PU // IPG
NV = -(-(B * NSLOT + NE * (TP - 1)) // TP // TU)
NTILE = NV * TU
NPAIR = NTILE * TP
XS, WS = 16.0, 64.0

CONSTS = {}
_at = 0
CST_FIRST = 0
for _name, _n in (("ident", P), ("own_head", HH), ("even", 1), ("odd", 1), ("eps", 1), ("eps_scaled", 1), ("cos", D), ("sin", D),
                  ("before", P), ("one", P), ("tri", NE * NE), ("tile_starts", B // TP), ("pair", NPAIR),
                  ("row", 1), ("slot", NSLOT * NE), ("br", NE)):
    CONSTS[_name] = (_at, _at + _n)
    _at += _n
    if _name == "sin":
        CST_FIRST = _at
NCONST = _at


def free(ap, *dims):
    return bass.AP(ap.tensor, ap.offset, [tuple(ap.ap[0])] + [tuple(d) for d in dims])


def flat(ap):
    return ap.rearrange("p a b -> p (a b)")


def build(nc, a, out, pair_rows):
    with ExitStack() as ctx:
        def sb(name, cols, dt=F32):
            return ctx.enter_context(nc.sbuf_tensor(name, [P, cols], dt))

        def sem(name):
            return ctx.enter_context(nc.semaphore(name))

        r1 = sb("r1", 2 * 2 * UI * ROWH + NGRP * D)
        xT = r1[:, 0:4 * PKT * 512].rearrange("p (c k n) -> p c k n", c=4, k=PKT)
        kx = r1[:, 0:4 * UI * ROWH].rearrange("p (u f n) -> p u f n", u=2, f=2)
        v1 = r1[:, 4 * UI * ROWH:].rearrange("p (g d) -> p g d", g=NGRP)
        _half = NTOK * D // 2
        xh = r1[:, 0:_half].bitcast(F16).rearrange("p (n d) -> p n d", n=NTOK)
        xl = r1[:, _half:2 * _half].bitcast(F16).rearrange("p (n d) -> p n d", n=NTOK)
        og = r1[:, 2 * _half:2 * _half + NSLOT * NTOK * HD2].rearrange("p (s n) -> p s n", s=NSLOT)
        og2 = r1[:, 0:NTOK * D].rearrange("p (n d) -> p n d", n=NTOK)
        ogT0 = r1[:, 4 * _half:4 * _half + NTOK * P].bitcast(F16).rearrange("p (x n) -> p x n", x=2)
        ogT1 = r1[:, 4 * _half + NTOK * P:4 * _half + NTOK * P + 2 * BANK].bitcast(F16)\
            .rearrange("p (u x n) -> p u x n", u=2, x=2)
        r2 = sb("r2", 6144)
        tokw = r2[:, 0:PKT * D].rearrange("p (k d) -> p k d", k=PKT)
        xn = r2[:, 1536:1536 + 8 * D].rearrange("p (r d) -> p r d", r=8)
        xnT = r2[:, 3584:3584 + 2 * KT * 512].rearrange("p (u k n) -> p u k n", u=2, k=KT)
        wst = r2[:, 0:4 * 1536].rearrange("p (s n) -> p s n", s=4)
        v2 = r2[:, 0:2048].rearrange("p (u g d) -> p u g d", u=2, g=GU)
        o2 = r2[:, 2048:4096].rearrange("p (u g d) -> p u g d", u=2, g=GU)
        p2 = r2[:, 4096:5120].rearrange("p (u g q) -> p u g q", u=2, g=GU)
        p2T = r2[:, 5120:6144].rearrange("p (u g q) -> p u g q", u=2, g=GU)
        r3 = sb("r3", 2 * 2 * B * NTOK + B * QROW)
        qr = r3[:, 0:2 * B * NTOK].rearrange("p (f n) -> p f n", f=2)
        oT = qr
        kr = r3[:, 4352:8704].rearrange("p (f n) -> p f n", f=2)
        lat = r3[:, 8704:8704 + B * QROW]
        p1 = lat[:, 0:2048].rearrange("p (u b q) -> p u b q", u=2, b=32)
        p1T = lat[:, 2048:4096].rearrange("p (u b q) -> p u b q", u=2, b=32)
        xg = r3[:, 0:8192].bitcast(F16).rearrange("p (u k n) -> p u k n", u=2, k=2 * KT)
        xg32 = r3[:, 0:8192].rearrange("p (u n) -> p u n", u=2)
        q2 = r3[0:HD2, 8192:8192 + 2 * PU * NTOK].rearrange("p (u n) -> p u n", u=2)
        k2 = r3[0:HD2, 10368:10368 + 2 * PU * NTOK].rearrange("p (u n) -> p u n", u=2)
        h = sb("h", NTOK * D)[:, :].rearrange("p (n d) -> p n d", n=NTOK)
        wh = sb("wh", KT * NE * 192, F16)[:, :].rearrange("p (k e d) -> p k e d", k=KT, e=NE)
        wl = sb("wl", KT * NE * 192, F16)[:, :].rearrange("p (k e d) -> p k e d", k=KT, e=NE)
        wb = sb("wb", NE * 192, F16)[:, :].rearrange("p (e d) -> p e d", e=NE)
        ones = sb("ones", max(P, TP * NTOK), F16)
        ident16 = sb("ident16", P, F16)
        pairs_of = sb("pairs_of", NPAIR, F16)
        cst = sb("cst", NCONST)
        wq_all = sb("wq", KT * 2 * D)[:, :]
        wq = wq_all.rearrange("p (k t d) -> p k t d", k=KT, t=2)
        wo2x = wq_all[:, 0:KT * D].bitcast(F16).rearrange("p (x k d) -> p x k d", x=2, k=KT)
        wlat = sb("wlat", KT * P)[:, :].rearrange("p (k d) -> p k d", k=KT)
        wk = sb("wk", 2 * D)[:, :].rearrange("p (t d) -> p t d", t=2)
        wv = sb("wv", D)
        wo1 = sb("wo1", KT * D)[:, :].rearrange("p (k d) -> p k d", k=KT)
        wo2 = sb("wo2", KT * D)[:, :].rearrange("p (k d) -> p k d", k=KT)
        wr = sb("wr", KT * NE)[:, :].rearrange("p (k e) -> p k e", k=KT)
        tokb = sb("tokb", D)
        bo = sb("bo", D)
        stats = sb("stats", 2 * NTOK * 6)[:, :].rearrange("p (n s) -> p n s", s=6)
        mv = sb("mv", 2 * NTOK * 2)[:, :].rearrange("p (n s) -> p n s", s=2)
        sd = sb("sd", 2 * NTOK)
        rstd = sb("rstd", 2 * NTOK)
        shift = sb("shift", NTOK)
        xs = sb("xs", 2 * D)[:, :].rearrange("p (u d) -> p u d", u=2)
        mx = sb("mx", 2 * 32)[:, :].rearrange("p (u b) -> p u b", u=2)
        rs = sb("rs", 2 * 32)[:, :].rearrange("p (u b) -> p u b", u=2)
        rinv = sb("rinv", 2 * 32)[:, :].rearrange("p (u b) -> p u b", u=2)
        odd_part = sb("odd_part", 2 * 136)[:, :].rearrange("p (f n) -> p f n", f=2)
        msumT = sb("msumT", KT * P)[:, :].rearrange("p (k n) -> p k n", k=KT)
        rt = r2[:, 2048:3584]
        warm = sb("warm", 1)
        idx = sb("idx", NSLOT, I32)
        heads = sb("heads", NTILE, I32)
        ps = ctx.enter_context(nc.psum_tensor("ps", [P, 8 * BANK], F32))

        def bank(i, lo=0, hi=BANK):
            return ps[:, i * BANK + lo:i * BANK + hi]

        def const(name):
            lo, hi = CONSTS[name]
            return cst[:, lo:hi]

        ident = const("ident")

        ld = {n: sem(f"ld_{n}") for n in
              ("tokw", "x0_0", "x0_1", "x0_2", "x0_3", "x1", "x2", "x3", "cst", "cst_rest", "cls", "pos0", "pos1", "tokb", "wq", "wlat", "wk", "wv",
               "wo1", "wo2", "wr", "bo", "w0", "w1", "w2", "w3", "w4", "w5")}
        ps_clear = sem("ps_clear")
        lat_clear = sem("lat_clear")
        hb_ready = sem("hb_ready")
        embedded = sem("embedded")
        h_ready = sem("h_ready")
        st_ready = sem("st_ready")
        mv_ready = sem("mv_ready")
        sd_ready = sem("sd_ready")
        rstd_ready = sem("rstd_ready")
        xn_ready = sem("xn_ready")
        xn_turned = sem("xn_turned")
        xnT_ready = sem("xnT_ready")
        turning = sem("turning")
        rotated = sem("rotated")
        proj_in = sem("proj_in")
        proj_act = sem("proj_act")
        proj_dve = sem("proj_dve")
        lat_in = sem("lat_in")
        lat_ready = sem("lat_ready")
        v_in = sem("v_in")
        v_act = sem("v_act")
        v_dve = sem("v_dve")
        kx0_ready = sem("kx0_ready")
        kx1_ready = sem("kx1_ready")
        s_done = sem("s_done")
        mx_ready = sem("mx_ready")
        sub_done = sem("sub_done")
        exp_done = sem("exp_done")
        rs_ready = sem("rs_ready")
        rinv_ready = sem("rinv_ready")
        norm_done = sem("norm_done")
        p1T_ready = sem("p1T_ready")
        pv_done = sem("pv_done")
        odd_ready = sem("odd_ready")
        oT_ready = sem("oT_ready")
        w_high = sem("w_high")
        w_low = sem("w_low")
        wo1_done = sem("wo1_done")
        h2_ready = sem("h2_ready")
        st2_ready = sem("st2_ready")
        mv2_ready = sem("mv2_ready")
        sd2_ready = sem("sd2_ready")
        rstd2_ready = sem("rstd2_ready")
        shift_ready = sem("shift_ready")
        xs_ready = sem("xs_ready")
        xh_ready = sem("xh_ready")
        xl_ready = sem("xl_ready")
        small = sem("small")
        msum_done = sem("msum_done")
        msum_ready = sem("msum_ready")
        logits_done = sem("logits_done")
        nmax_ready = sem("nmax_ready")
        rexp_done = sem("rexp_done")
        route = sem("route")
        mask_ready = sem("mask_ready")
        ranks_done = sem("ranks_done")
        head_col = sem("head_col")
        head_row = sem("head_row")
        heads_ready = sem("heads_ready")
        pairs_ready = sem("pairs_ready")
        idx_ready = sem("idx_ready")
        hbo_ready = sem("hbo_ready")
        xg_clear = sem("xg_clear")
        fill_done = sem("fill_done")
        fill_act = sem("fill_act")
        fill_dve = sem("fill_dve")
        qk_done = sem("qk_done")
        q2_ready = sem("q2_ready")
        k2_ready = sem("k2_ready")
        v2_in = sem("v2_in")
        v2_ready = sem("v2_ready")
        s2_done = sem("s2_done")
        mx2_ready = sem("mx2_ready")
        sub2_done = sem("sub2_done")
        exp2_done = sem("exp2_done")
        rs2_ready = sem("rs2_ready")
        rinv2_ready = sem("rinv2_ready")
        p2T_ready = sem("p2T_ready")
        pv2_done = sem("pv2_done")
        o2_ready = sem("o2_ready")
        o2_stored = [sem(f"o2_stored{i}") for i in range(2)]
        og_ready = [sem(f"og_ready{s}") for s in range(NSLOT)]
        og2_dve = sem("og2_dve")
        og2_act = sem("og2_act")
        og_turned = sem("og_turned")
        ogT_high = sem("ogT_high")
        ogT_ready = sem("ogT_ready")
        wo2_high = sem("wo2_high")
        wo2_split = sem("wo2_split")
        wo2_done = sem("wo2_done")
        y_ready = sem("y_ready")
        stored = sem("stored")

        def turned_pairs(c):
            return sum(-(-len(x) // 2) for x in CHUNKS[:c + 1])

        NPROJ = 4 * len(CHUNKS)
        HALF_PROJ = NPROJ // 2
        def pair_rows_of(v):
            return pair_rows[v * PU:(v + 1) * PU, :].rearrange("(g j) (q d) -> j q g d", j=IPG, q=NTOK)

        def fill_bank(at):
            return at % 4 if at < NFILL else at % 2

        def turn_bank(k, i):
            return i % 2 if k else i

        def turned_heads(k, i, x):
            lo, n = P * BATCHES[i][0], P * len(BATCHES[i])
            return ogT1[:, i % 2, x, 0:n] if k else ogT0[:, x, lo:lo + n]

        BATCHES = [list(range(n, min(n + 4, NTOK))) for n in range(0, NTOK, 4)]
        WO_BANKS = 6
        OG_FIRST = 4
        NFILL = 9
        FILL_ACT = [0, 2, 4, 6, 8]
        FILL_DVE = [1, 3, 5, 7]
        QK_ROUNDS = [range(0, 3), range(3, 6), range(6, TU)]
        TCOL = TP * NTOK

        block = ctx.enter_context(nc.Block())

        @block.sync
        def _(sp):
            def load(name, dst, src):
                sp.dma_start(dst, src).then_inc(ld[name], 16)

            load("cls", h[:, 0, :], a["cls"].partition_broadcast(P))
            load("tokw", tokw, a["tokw"])
            def patches(i):
                load(f"x0_{i}", xT[:, 0, :, P * i:P * i + P], a["x"][0, :, :, P * i:P * i + P])

            patches(0)
            load("tokb", tokb[:, :], a["tokb"].partition_broadcast(P))
            load("pos0", h[:, 1:5, :], a["pos"][0:4].partition_broadcast(P))
            patches(1)
            load("cst", cst[:, 0:CST_FIRST], a["cst"][:, 0:CST_FIRST])
            load("wq", wq, a["wq"])
            patches(2)
            patches(3)
            load("wlat", wlat, a["wlat"])
            load("wk", wk, a["wk"])
            load("x1", xT[:, 1], a["x"][1])
            load("pos1", h[:, 5:, :], a["pos"][4:].partition_broadcast(P))
            load("cst_rest", cst[:, CST_FIRST:], a["cst"][:, CST_FIRST:])
            for c in range(2, 4):
                load(f"x{c}", xT[:, c], a["x"][c])
            load("wv", wv[:, :], a["wv"])
            load("wo1", wo1, a["wo1"])
            load("wo2", wo2, a["wo2"])
            load("wr", wr, a["wr"])
            load("bo", bo[:, :], a["bo"].partition_broadcast(P))
            sp.wait_ge(lat_in, len(CHUNKS))
            sp.wait_ge(proj_in, NPROJ)
            for s in range(4):
                load(f"w{s}", wst[:, s, :], a["w"][s])
            for s in range(2):
                sp.wait_ge(w_low, s + 1)
                load(f"w{4 + s}", wst[:, s, :], a["w"][4 + s])
            for v in range(NV):
                sp.wait_ge(o2_ready, v + 1)
                for j in range(IPG if v < NV - 1 else IPG // 2):
                    sp.dma_start(pair_rows_of(v)[j], o2[QROW * j:QROW * j + NTOK, v % 2])\
                        .then_inc(o2_stored[v % 2], 16)
            STORES = ((0, 4), (4, 8), (8, 12), (12, 15), (15, 17))
            for lo, hi in STORES:
                sp.wait_ge(y_ready, hi)
                sp.dma_start(out[:, lo:hi, :], h[:, lo:hi, :]).then_inc(stored, 16)
            sp.wait_ge(stored, 16 * len(STORES))

        @block.gpsimd
        def _(pool):
            pool.memset(lat, 0.0).then_inc(lat_clear, 1)
            pool.wait_ge(ld["tokb"], 16)
            pool.wait_ge(ld["pos0"], 16)

            def bias(n):
                pool.tensor_tensor(h[:, n, :], h[:, n, :], tokb[:, :], ALU.add).then_inc(hb_ready, 1)

            def rotate(w, i):
                pool.tensor_tensor(w[:, 0, :], w[:, 0, :], const("cos"), ALU.mult).then_inc(turning, 1)
                pool.tensor_tensor(w[:, 1, :], w[:, 1, :], const("sin"), ALU.mult).then_inc(turning, 1)
                pool.wait_ge(turning, 2 * i + 2)
                pool.tensor_tensor(w[:, 0, :], w[:, 0, :], w[:, 1, :], ALU.add).then_inc(rotated, 1)

            for n in CHUNKS[1]:
                bias(n)
            pool.wait_ge(ld["cst"], 16)
            pool.wait_ge(ld["wq"], 16)
            for k in range(KT):
                rotate(wq[:, k], k)
            pool.wait_ge(ld["wk"], 16)
            rotate(wk, KT)
            pool.wait_ge(ld["pos1"], 16)
            for c in CHUNKS[2:]:
                for n in c:
                    bias(n)

            def expand(u):
                if u >= 2:
                    pool.wait_ge(s_done, u - 1)
                pool.tensor_tensor(
                    free(kx[:, u % 2, 0, :], (ROWH, UI), (NTOK, HH), (1, NTOK)),
                    free(kr[:, 0, UI * NTOK * u:], (NTOK, UI), (0, HH), (1, NTOK)),
                    free(const("own_head"), (0, UI), (1, HH), (0, NTOK)), ALU.mult).then_inc(kx0_ready, 1)

            def normalise(u):
                pool.wait_ge(rinv_ready, u + 1)
                pool.tensor_tensor(p1[:, u % 2, :, 0:NTOK], p1[:, u % 2, :, 0:NTOK],
                                   free(rinv[:, u % 2, :], (1, 32), (0, NTOK)), ALU.mult).then_inc(norm_done, 1)

            pool.wait_ge(proj_act, HALF_PROJ)
            pool.wait_ge(proj_dve, HALF_PROJ)
            pool.wait_ge(embedded, NPATCH)
            expand(0)
            expand(1)
            for u in range(NU):
                if u + 2 < NU:
                    expand(u + 2)
                normalise(u)
            def low_half(n):
                pool.wait_ge(xh_ready, n + 1)
                pool.tensor_tensor(xl[:, n, :], xs[:, n % 2, :], xh[:, n, :], ALU.subtract).then_inc(xl_ready, 1)

            for n in range(NTOK):
                low_half(n)
            pool.wait_ge(wo1_done, NTOK)
            for u in range(2):
                pool.memset(free(xg[:, u, 0, NTOK:], (QROW, 2 * KT * PU), (1, 1)), 0.0).then_inc(xg_clear, 1)
                pool.memset(free(xg32[:, u, NTOK // 2 + 1:], (QROW // 2, 2 * KT * PU), (1, QROW // 2 - NTOK // 2 - 1)),
                            0.0).then_inc(xg_clear, 1)
            pool.wait_ge(ld["bo"], 16)
            pool.wait_ge(xs_ready, NTOK)
            for n in range(NTOK):
                pool.tensor_tensor(h[:, n, :], h[:, n, :], bo[:, :], ALU.add).then_inc(hbo_ready, 1)
            for i in range(2):
                pool.wait_ge(o2_stored[i], len(range(i, NV, 2)) * IPG * 16)
            pool.wait_ge(idx_ready, 1)
            for s in range(NSLOT):
                pool.indirect_dma_start(og[:, s, :], None, pair_rows,
                                        bass.IndirectOffsetOnAxis(ap=idx[:, s:s + 1], axis=0))\
                    .then_inc(og_ready[s], 16)

        @block.scalar
        def _(act):
            def turned(c, k):
                i = (turned_pairs(c - 1) if c else 0) + k
                act.wait_ge(xn_turned, i + 1)
                if c >= 2:
                    act.wait_ge(proj_in, 4 * (c - 2) + 2)
                    act.wait_ge(lat_in, c - 1)
                n = min(2, len(CHUNKS[c]) - 2 * k) * P
                nc.scalar.activation(free(xnT[:, c % 2, 0, 2 * P * k:], (512, KT), (1, n)),
                                     free(bank(2 + k), (256, KT), (1, n)), ACT.Copy).then_inc(xnT_ready, 1)

            def project_out(r):
                act.wait_ge(proj_in, r + 1)
                chunk = CHUNKS[r // 4]
                nc.scalar.activation(free((qr if r % 4 < 2 else kr)[:, r % 2, chunk[0]:], (1, len(chunk)), (NTOK, B)),
                                     free(bank(4 + r % 4), (P, len(chunk)), (1, P)), ACT.Copy).then_inc(proj_act, 1)

            act.wait_ge(ld["cst"], 16)
            act.wait_ge(lat_clear, 1)
            def deviation(n):
                act.wait_ge(mv_ready, n + 1)
                nc.scalar.activation(sd[:, n:n + 1], mv[:, n, 1:2], ACT.Sqrt, bias=const("eps")).then_inc(sd_ready, 1)

            def latents_out(c):
                chunk = CHUNKS[c]
                act.wait_ge(lat_in, c + 1)
                for g in range(UG):
                    nc.scalar.activation(
                        free(lat[:, chunk[0] + P * g:], (1, len(chunk)), (QROW * UI, NU), (QROW, IPG)),
                        free(bank(2, g), (P, len(chunk)), (UI, NU), (UG, IPG)), ACT.Copy).then_inc(lat_ready, 1)

            deviation(0)
            for c in range(1, len(CHUNKS) + 1):
                positions = CHUNKS[c] if c < len(CHUNKS) else []
                for n in positions[:3]:
                    deviation(n)
                    if n == positions[0] and c >= 2:
                        project_out(4 * (c - 2) + 2)
                for k in range(-(-len(CHUNKS[c - 1]) // 2)):
                    turned(c - 1, k)
                for n in positions[3:]:
                    deviation(n)
                if not positions:
                    project_out(4 * (c - 2) + 2)
                project_out(4 * (c - 1))
                latents_out(c - 1)
            project_out(4 * (len(CHUNKS) - 1) + 2)
            def v1_out(r):
                act.wait_ge(v_in, r + 1)
                nc.scalar.activation(free(v1[:, 2 * r, :], (1, BANK)), bank(4 + r % 4), ACT.Copy).then_inc(v_act, 1)


            def expand(u):
                if u >= 2:
                    act.wait_ge(s_done, u - 1)
                for e in range(HH):
                    lo = CONSTS["own_head"][0] + e
                    nc.scalar.activation(free(kx[:, u % 2, 1, e * NTOK:], (ROWH, UI), (1, NTOK)),
                                         free(kr[:, 1, UI * NTOK * u:], (NTOK, UI), (1, NTOK)), ACT.Copy,
                                         scale=cst[:, lo:lo + 1]).then_inc(kx1_ready, 1)

            act.wait_ge(proj_act, HALF_PROJ)
            act.wait_ge(proj_dve, HALF_PROJ)
            act.wait_ge(embedded, NPATCH)
            v1_out(0)
            expand(0)
            for r in (2, 4, 6):
                v1_out(r)
            expand(1)
            v1_out(8)
            v1_out(10)

            def odd_heads(u):
                act.wait_ge(pv_done, IPG * (u + 1))
                if u >= 1:
                    act.wait_ge(oT_ready, 2 * u)
                nc.scalar.activation(free(odd_part[:, 0, :], (136, 2), (NTOK, UI), (1, NTOK)),
                                     free(bank(4 + 2 * (u % 2), NTOK), (2 * NTOK, 2), (P, UI), (1, NTOK)),
                                     ACT.Copy, scale=const("odd")).then_inc(odd_ready, 1)

            def split_high(s):
                act.wait_ge(ld[f"w{s}"], 16)
                dst = free(wh[:, s // 2, NE // 2 * (s % 2), :] if s < 4 else wb[:, NE // 2 * (s - 4), :], (1, 1536))
                nc.scalar.activation(dst, wst[:, s % 4, :], ACT.Copy, scale=WS).then_inc(w_high, 1)

            for i in range(NU + 3):
                if i < NU:
                    act.wait_ge(sub_done, i + 1)
                    nc.scalar.activation(p1[:, i % 2, :, 0:NTOK], p1[:, i % 2, :, 0:NTOK], ACT.Exp,
                                         scale=HD1 ** -0.5).then_inc(exp_done, 1)
                if i >= 3:
                    odd_heads(i - 3)
                if i + 2 < NU:
                    expand(i + 2)
                if i == 0:
                    v1_out(12)
                    v1_out(14)
                if i % 2 == 0 and 2 <= i < 14:
                    split_high(i // 2 - 1)
            nc.scalar.activation(ident16[:, :], ident, ACT.Copy).then_inc(small, 1)
            for i in range(NTOK + 2):
                if i >= 2:
                    n = i - 2
                    act.wait_ge(shift_ready, n + 1)
                    if n >= 2:
                        act.wait_ge(xl_ready, n - 1)
                    nc.scalar.activation(xs[:, n % 2, :], h[:, n, :], ACT.Identity, bias=shift[:, n:n + 1],
                                         scale=rstd[:, NTOK + n:NTOK + n + 1]).then_inc(xs_ready, 1)
                if i < NTOK:
                    at = NTOK + i
                    act.wait_ge(mv2_ready, i + 1)
                    nc.scalar.activation(sd[:, at:at + 1], mv[:, at, 1:2], ACT.Sqrt, bias=const("eps_scaled"),
                                         scale=XS ** -2).then_inc(sd2_ready, 1)
                if i >= 2:
                    act.wait_ge(xs_ready, n + 1)
                    nc.scalar.activation(xh[:, n, :], xs[:, n % 2, :], ACT.Copy).then_inc(xh_ready, 1)
            nc.scalar.activation(warm[:, :], const("eps"), ACT.Exp).then_inc(small, 1)
            act.wait_ge(nmax_ready, 1)
            nc.scalar.activation(rt[:, 32:48], rt[:, 0:16], ACT.Exp, bias=rt[:, 16:17],
                                 accum_out=rt[:, 17:18]).then_inc(rexp_done, 1)
            act.wait_ge(wo1_done, NTOK)

            def fill_out(v, f):
                at = NFILL * v + f
                act.wait_ge(fill_done, at + 1)
                if v >= 2 and f == 0:
                    act.wait_ge(v2_in, 2 * (v - 1))
                    act.wait_ge(qk_done, 3 * (v - 1))
                if f < 8:
                    dst = free(xg[:, v % 2, f // 2, 8 * (f % 2):], (QROW, PU), (1, 8))
                    src = free(bank(fill_bank(at)), (1, PU), (PU, 8))
                else:
                    dst = free(xg[:, v % 2, 0, NPATCH:], (PU * QROW, 4), (QROW, PU))
                    src = free(bank(fill_bank(at)), (PU, 4), (1, PU))
                nc.scalar.activation(dst, src, ACT.Copy).then_inc(fill_act, 1)

            def q_out(v, r):
                act.wait_ge(qk_done, 3 * v + r + 1)
                if v >= 2:
                    act.wait_ge(s2_done, v - 1)
                lo, n = QK_ROUNDS[r][0] * TCOL, TCOL * len(QK_ROUNDS[r])
                nc.scalar.activation(q2[:, v % 2, lo:lo + n], bank(2 + (3 * v + r) % 2, 0, n)[0:HD2], ACT.Copy,
                                     scale=1 / (XS * WS)).then_inc(q2_ready, 1)

            def v_out(v, f):
                act.wait_ge(v2_in, 2 * v + f + 1)
                if v >= 2:
                    act.wait_ge(pv2_done, IPG * (v - 1))
                nc.scalar.activation(free(v2[:, v % 2, 8 * f, :], (1, BANK)), bank(4), ACT.Copy,
                                     scale=1 / (XS * WS)).then_inc(v2_ready, 1)

            for f in FILL_ACT:
                fill_out(0, f)
            for v in range(NV):
                def next_fill(f):
                    if v + 1 < NV:
                        fill_out(v + 1, f)

                q_out(v, 0)
                next_fill(0)
                q_out(v, 1)
                q_out(v, 2)
                next_fill(2)
                next_fill(4)
                v_out(v, 0)
                act.wait_ge(sub2_done, v + 1)
                nc.scalar.activation(p2[:, v % 2, :, 0:NTOK], p2[:, v % 2, :, 0:NTOK], ACT.Exp,
                                     scale=HD2 ** -0.5).then_inc(exp2_done, 1)
                next_fill(6)
                v_out(v, 1)
                next_fill(8)
            act.wait_ge(ld["wo2"], 16)
            nc.scalar.activation(free(wo2x[:, 0, 0, :], (1, KT * D)), free(wo2[:, 0, :], (1, KT * D)), ACT.Copy,
                                 scale=WS).then_inc(wo2_high, 1)
            act.wait_ge(o2_ready, NV)
            for j in range(IPG // 2, IPG):
                act.dma_start(pair_rows_of(NV - 1)[j], o2[QROW * j:QROW * j + NTOK, (NV - 1) % 2])\
                    .then_inc(o2_stored[(NV - 1) % 2], 16)
            for k in range(KT):
                s = 2 * k + 1
                act.wait_ge(og_ready[s], 16)
                for lo, hi in ((0, OG_FIRST), (OG_FIRST, NTOK)):
                    nc.scalar.activation(free(og2[:, lo, HD2 * s:], (D, hi - lo), (1, HD2)),
                                         free(og[:, s, HD2 * lo:], (HD2, hi - lo), (1, HD2)), ACT.Copy)\
                        .then_inc(og2_act, 1)
                for i, batch in enumerate(BATCHES):
                    e = len(BATCHES) * k + i
                    act.wait_ge(og_turned, e + 1)
                    if k == 1 and i >= 2:
                        act.wait_ge(wo2_done, BATCHES[i - 2][-1] + 1)
                    n = P * len(batch)
                    nc.scalar.activation(turned_heads(k, i, 0), bank(turn_bank(k, i), 0, n), ACT.Copy, scale=XS)\
                        .then_inc(ogT_high, 1)

        @block.vector
        def _(dve):
            dve.memset(ps[:, 0:4 * BANK], 0.0).then_inc(ps_clear, 1)
            dve.memset(ones[:, :], XS).then_inc(small, 1)

            def norm_stats(n):
                if n:
                    dve.wait_ge(embedded, n)
                    dve.wait_ge(hb_ready, n)
                    dve.tensor_tensor(h[:, n, :], bank((n - 1) % 2, 0, D), h[:, n, :], ALU.add).then_inc(h_ready, 1)
                    dve.wait_ge(h_ready, n)
                dve.bn_stats(stats[:, n, :], h[:, n, :]).then_inc(st_ready, 1)
                dve.wait_ge(st_ready, n + 1)
                dve.bn_aggr(mv[:, n, :], stats[:, n, :]).then_inc(mv_ready, 1)

            def norm_out(n):
                dve.wait_ge(sd_ready, n + 1)
                dve.reciprocal(rstd[:, n:n + 1], sd[:, n:n + 1]).then_inc(rstd_ready, 1)
                dve.wait_ge(rstd_ready, n + 1)
                if n >= 8:
                    c = (n - 8 + 3) // 4
                    dve.wait_ge(xn_turned, turned_pairs(c))
                dve.tensor_scalar(xn[:, n % 8, :], h[:, n, :], mv[:, n, 0:1], rstd[:, n:n + 1],
                                  ALU.subtract, ALU.mult).then_inc(xn_ready, 1)

            def project_out(r):
                dve.wait_ge(proj_in, r + 1)
                chunk = CHUNKS[r // 4]
                dve.tensor_copy(free((qr if r % 4 < 2 else kr)[:, r % 2, chunk[0]:], (1, len(chunk)), (NTOK, B)),
                                free(bank(4 + r % 4), (P, len(chunk)), (1, P))).then_inc(proj_dve, 1)

            dve.wait_ge(ld["cls"], 16)
            norm_stats(0)
            norm_out(0)
            for c in range(1, len(CHUNKS) + 1):
                if c < len(CHUNKS):
                    for n in CHUNKS[c]:
                        norm_stats(n)
                        if n != CHUNKS[c][0]:
                            norm_out(n - 1)
                        elif c >= 2:
                            project_out(4 * (c - 2) + 3)
                    norm_out(CHUNKS[c][-1])
                else:
                    project_out(4 * (c - 2) + 3)
                project_out(4 * (c - 1) + 1)
            project_out(4 * (len(CHUNKS) - 1) + 3)
            def v_out(r):
                dve.wait_ge(v_in, r + 1)
                dve.tensor_copy(free(v1[:, 2 * r, :], (1, BANK)), bank(4 + r % 4)).then_inc(v_dve, 1)

            for r in range(1, 8, 2):
                v_out(r)

            def scores(u):
                return free(bank(2 * (u % 2)), (BANK, 2), (NTOK, 16), (1, NTOK))

            def split_low(s):
                dve.wait_ge(w_high, s + 1)
                if s < 4:
                    dst = free(wl[:, s // 2, NE // 2 * (s % 2), :], (1, 1536))
                    high = free(wh[:, s // 2, NE // 2 * (s % 2), :], (1, 1536))
                    src = wst[:, s % 4, :]
                else:
                    dst = high = free(wb[QROW:2 * QROW, NE // 2 * (s - 4), :], (1, 1536))
                    src = wst[QROW:2 * QROW, s % 4, :]
                dve.scalar_tensor_tensor(out=dst, in0=src, scalar=WS, in1=high, op0=ALU.mult, op1=ALU.subtract)\
                    .then_inc(w_low, 1)

            def soft_in(u):
                dve.wait_ge(s_done, u + 1)
                dve.tensor_reduce(mx[:, u % 2, :], scores(u), AX_X, ALU.max).then_inc(mx_ready, 1)
                dve.wait_ge(mx_ready, u + 1)
                if u >= 2:
                    dve.wait_ge(p1T_ready, u - 1)
                dve.tensor_tensor(free(p1[:, u % 2], (512, 2), (32, 16), (1, NTOK)), scores(u),
                                  free(mx[:, u % 2, :], (16, 2), (1, 16), (0, NTOK)),
                                  ALU.subtract).then_inc(sub_done, 1)

            dve.wait_ge(v_in, NGRP // 4)
            for i in range(NU + 3):
                if 2 <= i < NU + 2:
                    u = i - 2
                    dve.wait_ge(norm_done, u + 1)
                    if u >= 2:
                        dve.wait_ge(pv_done, IPG * (u - 1))
                    dve.transpose(free(p1T[:, u % 2], (1, 1024)), free(p1[:, u % 2], (1, 1024)))\
                        .then_inc(p1T_ready, 1)
                if i < NU:
                    soft_in(i)
                if i == 0:
                    v_out(9)
                    v_out(11)
                if 1 <= i < NU + 1:
                    u = i - 1
                    dve.wait_ge(exp_done, u + 1)
                    dve.tensor_reduce(rs[:, u % 2, :], p1[:, u % 2, :, 0:NTOK], AX_X, ALU.add).then_inc(rs_ready, 1)
                    dve.wait_ge(rs_ready, u + 1)
                    if u >= 2:
                        dve.wait_ge(norm_done, u - 1)
                    dve.reciprocal(rinv[:, u % 2, :], rs[:, u % 2, :]).then_inc(rinv_ready, 1)
                if i == 1:
                    v_out(13)
                    v_out(15)
                    dve.wait_ge(v_in, NGRP // 2)
                if i >= 3:
                    u = i - 3
                    dve.wait_ge(odd_ready, u + 1)
                    for f in range(2):
                        dve.scalar_tensor_tensor(
                            out=free(oT[:, f, UI * NTOK * u:], (NTOK, UI), (1, NTOK)),
                            in0=free(bank(4 + 2 * (u % 2), 2 * NTOK * f), (P, UI), (1, NTOK)),
                            scalar=const("even"),
                            in1=free(odd_part[:, f, :], (NTOK, UI), (1, NTOK)),
                            op0=ALU.mult, op1=ALU.add).then_inc(oT_ready, 1)
                if i % 2 == 1 and 3 <= i < 15:
                    split_low(i // 2 - 1)

            def residual(n):
                dve.wait_ge(wo1_done, n + 1)
                dve.tensor_tensor(h[:, n, :], bank(n % 4, 0, D), h[:, n, :], ALU.add).then_inc(h2_ready, 1)

            def moments(n):
                dve.wait_ge(h2_ready, n + 1)
                dve.bn_stats(stats[:, NTOK + n, :], h[:, n, :]).then_inc(st2_ready, 1)

            def spread(n):
                dve.wait_ge(st2_ready, n + 1)
                dve.bn_aggr(mv[:, NTOK + n, :], stats[:, NTOK + n, :]).then_inc(mv2_ready, 1)

            def scale(n):
                dve.wait_ge(sd2_ready, n + 1)
                dve.reciprocal(rstd[:, NTOK + n:NTOK + n + 1], sd[:, NTOK + n:NTOK + n + 1]).then_inc(rstd2_ready, 1)

            def shift_of(n):
                dve.wait_ge(rstd2_ready, n + 1)
                dve.scalar_tensor_tensor(out=shift[:, n:n + 1], in0=mv[:, NTOK + n, 0:1], scalar=-1.0,
                                         in1=rstd[:, NTOK + n:NTOK + n + 1], op0=ALU.mult, op1=ALU.mult)\
                    .then_inc(shift_ready, 1)

            for n in range(NTOK + 2):
                if n < NTOK:
                    residual(n)
                if n >= 2:
                    scale(n - 2)
                if n < NTOK:
                    moments(n)
                if n >= 2:
                    shift_of(n - 2)
                if n < NTOK:
                    spread(n)

            steps = [0]

            def step(ins):
                steps[0] += 1
                ins.then_inc(route, 1)
                dve.wait_ge(route, steps[0])

            logits, nmax, total, ex = rt[:, 0:16], rt[:, 16:17], rt[:, 17:18], rt[:, 32:48]
            dist, chosen, slot, count = rt[:, 48:64], rt[:, 64:80], rt[:, 80:96], rt[:, 96:112]
            tiles, base, place, end = rt[:, 112:128], rt[:, 128:144], rt[:, 144:160], rt[:, 160:176]
            rank, inv, head, at_slot = rt[:, 176:192], rt[:, 192:193], rt[:, 193:194], rt[:, 196:200]
            in_head, passed = rt[:, 200:216], rt[:, 216:232]
            starts = rt[:, 256:768]
            sq1, sq2, sl = rt[:, 256:512], rt[:, 512:768], rt[:, 768:832]
            hot = rt[:, 832:832 + NPAIR]
            own = ((1, NE), (0, NE))
            other = ((0, NE), (1, NE))
            square = ((NE, NE), (1, NE))
            tri = free(const("tri"), *square)
            dve.wait_ge(msum_done, 1)
            dve.tensor_copy(free(msumT[:, 0, :], (P, KT), (1, P)), free(bank(4), (BANK, KT), (1, P)))\
                .then_inc(msum_ready, 1)
            dve.wait_ge(logits_done, 1)
            dve.wait_ge(ld["cst_rest"], 16)
            dve.wait_ge(w_low, 6)
            step(dve.scalar_tensor_tensor(out=logits, in0=bank(6, 0, NE), scalar=1 / (NTOK * XS),
                                          in1=const("br"), op0=ALU.mult, op1=ALU.add))
            dve.tensor_reduce(nmax, logits, AX_X, ALU.max, negate=True).then_inc(nmax_ready, 1)
            dve.wait_ge(rexp_done, 1)
            step(dve.reciprocal(inv, total))
            step(dve.tensor_scalar(dist, ex, inv, None, ALU.mult))
            step(dve.tensor_tensor(free(sq1, *square), free(dist, *other), free(dist, *own), ALU.is_gt))
            step(dve.tensor_tensor(free(sq2, *square), free(dist, *other), free(dist, *own), ALU.is_equal))
            step(dve.tensor_tensor(free(sq2, *square), free(sq2, *square), tri, ALU.mult))
            step(dve.tensor_tensor(sq1, sq1, sq2, ALU.add))
            step(dve.tensor_reduce(rank, free(sq1, *square), AX_X, ALU.add))
            dve.tensor_scalar(chosen, rank, float(NSLOT), None, ALU.is_lt).then_inc(mask_ready, 1)
            dve.wait_ge(mask_ready, 1)
            step(dve.tensor_tensor(free(sq1, *square), free(chosen, *other), tri, ALU.mult))
            step(dve.tensor_reduce(slot, free(sq1, *square), AX_X, ALU.add))
            dve.wait_ge(ranks_done, 2)
            step(dve.tensor_copy(count, bank(7, 0, NE)))
            step(dve.tensor_copy(in_head, bank(6, 32, 32 + NE)))
            most = B // TP
            step(dve.tensor_tensor(free(starts, (most, NE), (1, most)), free(count, (1, NE), (0, most)),
                                   free(const("tile_starts"), (0, NE), (1, most)), ALU.is_gt))
            step(dve.tensor_reduce(tiles, free(starts, (most, NE), (1, most)), AX_X, ALU.add))
            step(dve.tensor_tensor(free(sq1, *square), free(tiles, *other), tri, ALU.mult))
            step(dve.tensor_reduce(base, free(sq1, *square), AX_X, ALU.add))
            step(dve.tensor_tensor(end, base, tiles, ALU.add))
            step(dve.tensor_scalar(passed, end, const("row"), None, ALU.is_le))
            step(dve.tensor_reduce(head, passed, AX_X, ALU.add))
            dve.tensor_scalar(head, head, float(NE - 1), None, ALU.min).then_inc(head_col, 1)
            step(dve.scalar_tensor_tensor(out=place, in0=base, scalar=float(TP), in1=in_head,
                                          op0=ALU.mult, op1=ALU.add))
            step(dve.tensor_tensor(place, place, chosen, ALU.mult))
            by_slot = ((NE, NSLOT), (1, NE))
            step(dve.tensor_tensor(free(sl, *by_slot), free(slot, (0, NSLOT), (1, NE)),
                                   free(const("slot"), *by_slot), ALU.is_equal))
            step(dve.tensor_tensor(free(sl, *by_slot), free(sl, *by_slot), free(place, (0, NSLOT), (1, NE)),
                                   ALU.mult))
            step(dve.tensor_reduce(at_slot, free(sl, *by_slot), AX_X, ALU.add))
            dve.tensor_copy(idx[:, :], at_slot).then_inc(idx_ready, 1)

            def one_hot(lo, hi):
                for s in range(NSLOT):
                    if s == 0:
                        step(dve.tensor_scalar(hot[:, lo:hi], const("pair")[:, lo:hi], at_slot[:, 0:1], None,
                                               ALU.is_equal))
                    else:
                        last = s == NSLOT - 1
                        ins = dve.scalar_tensor_tensor(
                            out=pairs_of[:, lo:hi] if last else hot[:, lo:hi], in0=const("pair")[:, lo:hi],
                            scalar=at_slot[:, s:s + 1], in1=hot[:, lo:hi], op0=ALU.is_equal, op1=ALU.add)
                        if last:
                            ins.then_inc(pairs_ready, 1)
                        else:
                            step(ins)

            one_hot(0, 2 * PU)
            dve.wait_ge(head_row, 1)
            dve.tensor_copy(heads[0:1, :], bank(7, 64, 64 + NTILE)[0:1]).then_inc(heads_ready, 1)


            def fill_out(v, f):
                at = NFILL * v + f
                dve.wait_ge(fill_done, at + 1)
                if v >= 2 and f == 1:
                    dve.wait_ge(v2_in, 2 * (v - 1))
                    dve.wait_ge(qk_done, 3 * (v - 1))
                dve.tensor_copy(free(xg[:, v % 2, f // 2, 8 * (f % 2):], (QROW, PU), (1, 8)),
                                free(bank(fill_bank(at)), (1, PU), (PU, 8))).then_inc(fill_dve, 1)

            def k_out(v, r):
                dve.wait_ge(qk_done, 3 * v + r + 1)
                if v >= 2:
                    dve.wait_ge(s2_done, v - 1)
                lo, n = QK_ROUNDS[r][0] * TCOL, TCOL * len(QK_ROUNDS[r])
                dve.tensor_scalar(k2[:, v % 2, lo:lo + n], bank(2 + (3 * v + r) % 2, 0, n)[HD2:P], 1 / (XS * WS),
                                  None, ALU.mult).then_inc(k2_ready, 1)

            def scores2():
                return free(bank(5), (NTOK, GU), (1, NTOK))

            def soft_in(v):
                dve.wait_ge(s2_done, v + 1)
                dve.tensor_reduce(mx[:, v % 2, 0:GU], scores2(), AX_X, ALU.max).then_inc(mx2_ready, 1)
                dve.wait_ge(mx2_ready, v + 1)
                if v >= 2:
                    dve.wait_ge(p2T_ready, v - 1)
                dve.tensor_tensor(p2[:, v % 2, :, 0:NTOK], scores2(), free(mx[:, v % 2, :], (1, GU), (0, NTOK)),
                                  ALU.subtract).then_inc(sub2_done, 1)

            def soft_out(v):
                dve.wait_ge(exp2_done, v + 1)
                if v >= 2:
                    dve.wait_ge(pv2_done, IPG * (v - 1))
                dve.transpose(free(p2T[:, v % 2], (1, 512)), free(p2[:, v % 2], (1, 512))).then_inc(p2T_ready, 1)
                dve.tensor_reduce(rs[:, v % 2, 0:GU], p2[:, v % 2, :, 0:NTOK], AX_X, ALU.add).then_inc(rs2_ready, 1)
                dve.wait_ge(rs2_ready, v + 1)
                if v >= 2:
                    dve.wait_ge(o2_ready, v - 1)
                dve.reciprocal(rinv[:, v % 2, 0:GU], rs[:, v % 2, 0:GU]).then_inc(rinv2_ready, 1)

            def head_out(v):
                dve.wait_ge(pv2_done, IPG * (v + 1))
                dve.wait_ge(rinv2_ready, v + 1)
                if v >= 2:
                    dve.wait_ge(o2_stored[v % 2], v // 2 * IPG * 16)
                dve.tensor_tensor(o2[:, v % 2], free(bank(6), (HD2, GU), (1, HD2)),
                                  free(rinv[:, v % 2, :], (1, GU), (0, HD2)), ALU.mult).then_inc(o2_ready, 1)

            for f in FILL_DVE:
                fill_out(0, f)
            for v in range(NV):
                def next_fill(f):
                    if v + 1 < NV:
                        fill_out(v + 1, f)

                k_out(v, 0)
                k_out(v, 1)
                next_fill(1)
                k_out(v, 2)
                if v == 0:
                    one_hot(2 * PU, NPAIR)
                next_fill(3)
                soft_in(v)
                next_fill(5)
                soft_out(v)
                next_fill(7)
                if v >= 1:
                    head_out(v - 1)
            head_out(NV - 1)

            dve.wait_ge(wo2_high, 1)
            dve.scalar_tensor_tensor(out=free(wo2x[:, 1, 0, :], (1, KT * D)), in0=free(wo2[:, 0, :], (1, KT * D)),
                                     scalar=WS, in1=free(wo2x[:, 0, 0, :], (1, KT * D)), op0=ALU.mult,
                                     op1=ALU.subtract).then_inc(wo2_split, 1)

            def lay_out(s):
                dve.wait_ge(og_ready[s], 16)
                for lo, hi in ((0, OG_FIRST), (OG_FIRST, NTOK)):
                    dve.tensor_copy(free(og2[:, lo, HD2 * s:], (D, hi - lo), (1, HD2)),
                                    free(og[:, s, HD2 * lo:], (HD2, hi - lo), (1, HD2))).then_inc(og2_dve, 1)

            def low_heads(k, i):
                e = len(BATCHES) * k + i
                dve.wait_ge(ogT_high, e + 1)
                dve.scalar_tensor_tensor(out=turned_heads(k, i, 1), in0=bank(turn_bank(k, i), 0, P * len(BATCHES[i])),
                                         scalar=XS, in1=turned_heads(k, i, 0), op0=ALU.mult, op1=ALU.subtract)\
                    .then_inc(ogT_ready, 1)

            lay_out(0)
            low_heads(0, 0)
            low_heads(0, 1)
            lay_out(2)
            for i in range(2, len(BATCHES)):
                low_heads(0, i)
            low_heads(1, 0)
            for i, batch in enumerate(BATCHES):
                if i + 1 < len(BATCHES):
                    low_heads(1, i + 1)
                for n in batch:
                    dve.wait_ge(wo2_done, n + 1)
                    dve.wait_ge(hbo_ready, n + 1)
                    dve.scalar_tensor_tensor(out=h[:, n, :], in0=bank(2 + n % WO_BANKS, 0, D), scalar=1 / (XS * WS),
                                             in1=h[:, n, :], op0=ALU.mult, op1=ALU.add).then_inc(y_ready, 1)

        @block.tensor
        def _(pe):
            def embed(n):
                c, i = divmod(n - 1, 4)
                pe.wait_ge(ld[f"x{c}" if c else f"x0_{i}"], 16)
                if n > 2:
                    pe.wait_ge(h_ready, n - 2)
                for k in range(PKT):
                    mm = pe.matmul(bank((n - 1) % 2, 0, D), xT[:, c, k, i * P:(i + 1) * P], tokw[:, k, :],
                                   start=k == 0, stop=k == PKT - 1)
                mm.then_inc(embedded, 1)

            def turn(c, k):
                pe.wait_ge(xn_ready, CHUNKS[c][min(2 * k + 1, len(CHUNKS[c]) - 1)] + 1)
                if c >= 1 and k == 0:
                    pe.wait_ge(lat_ready, UG * c)
                if c >= 2 and k == 1:
                    pe.wait_ge(xnT_ready, turned_pairs(c - 1))
                for i, n in enumerate(CHUNKS[c][2 * k:2 * k + 2]):
                    for t in range(KT):
                        mm = pe.transpose(bank(2 + k, 256 * t + P * i, 256 * t + P * i + P),
                                          xn[:, n % 8, P * t:P * t + P], ident)
                mm.then_inc(xn_turned, 1)

            def project(r, moving, weights, kts):
                if r >= 4:
                    pe.wait_ge(proj_dve if r % 2 else proj_act, (r - 4) // 2 + 1)
                n = P * len(CHUNKS[r // 4])
                for k in range(kts):
                    mm = pe.matmul(bank(4 + r % 4, 0, n), weights(k)[:, P * (r % 2):P * (r % 2) + P], moving(k),
                                   start=k == 0, stop=k == kts - 1)
                mm.then_inc(proj_in, 1)

            def q_and_latents(c):
                n = P * len(CHUNKS[c])
                pe.wait_ge(xnT_ready, turned_pairs(c))
                if c == 0:
                    pe.wait_ge(rotated, 2)
                tokens = lambda k: xnT[:, c % 2, k, 0:n]
                project(4 * c, tokens, lambda k: wq[:, k, 0, :], KT)
                project(4 * c + 1, tokens, lambda k: wq[:, k, 0, :], KT)
                if c == 0:
                    pe.wait_ge(ld["wlat"], 16)
                for k in range(KT):
                    mm = pe.matmul(bank(2, 0, n), wlat[:, k, :], tokens(k), start=k == 0, stop=k == KT - 1)
                mm.then_inc(lat_in, 1)

            def keys(c):
                if c == 0:
                    pe.wait_ge(rotated, 3)
                pe.wait_ge(lat_ready, UG * (c + 1))
                latents = lambda k: free(lat[:, CHUNKS[c][0]:], (1, len(CHUNKS[c])), (QROW, B))
                project(4 * c + 2, latents, lambda k: wk[:, 0, :], 1)
                project(4 * c + 3, latents, lambda k: wk[:, 0, :], 1)

            pe.wait_ge(ps_clear, 1)
            pe.wait_ge(ld["tokw"], 16)
            for c in range(1, len(CHUNKS) + 1):
                positions = CHUNKS[c] if c < len(CHUNKS) else []
                for n in positions[:3]:
                    embed(n)
                    if n == positions[0] and c >= 2:
                        keys(c - 2)
                if c == 1:
                    pe.wait_ge(ld["cst"], 16)
                for k in range(-(-len(CHUNKS[c - 1]) // 2)):
                    turn(c - 1, k)
                for n in positions[3:]:
                    embed(n)
                if not positions:
                    keys(c - 2)
                q_and_latents(c - 1)
            keys(len(CHUNKS) - 1)
            def scores(u):
                pe.wait_ge(kx0_ready, u + 1)
                pe.wait_ge(kx1_ready, HH * (u + 1))
                if u >= 2:
                    pe.wait_ge(sub_done, u - 1)
                for f in range(2):
                    for i in range(UI):
                        j, at = QROW * (i % IPG), i // IPG * ROWH
                        img = UI * u + UG * (i % IPG) + i // IPG
                        mm = pe.matmul(bank(2 * (u % 2) + f, at, at + ROWH)[j:j + NTOK],
                                       qr[:, f, NTOK * img:NTOK * img + NTOK],
                                       kx[:, u % 2, f, ROWH * i:ROWH * i + ROWH], start=True, stop=True)
                mm.then_inc(s_done, 1)

            def weigh(u):
                pe.wait_ge(p1T_ready, u + 1)
                if u >= 2:
                    pe.wait_ge(oT_ready, 2 * (u - 1))
                for turn, j in enumerate((0, 2, 1, 3)):
                    rows = slice(QROW * j, QROW * j + NTOK)
                    if turn >= 2:
                        pe.wait_ge(pv_done, IPG * u + turn - 1)
                    for g in range(UG):
                        for f in range(2):
                            at = 2 * P * (j % 2) + P * g + 2 * NTOK * f
                            for c in range(4):
                                b = 16 * f + HH * g + 2 * c
                                lo = P * f + QROW * c
                                mm = pe.matmul(bank(4 + 2 * (u % 2) + j // 2, at, at + 2 * NTOK)[QROW * c:QROW * c + QROW],
                                               v1[rows, UG * u + g, lo:lo + QROW],
                                               p1T[rows, u % 2, b:b + 2, 0:NTOK], start=True, stop=True)
                    mm.then_inc(pv_done, 1)

            pe.wait_ge(ld["wv"], 16)
            for r in range(NGRP // 2):
                if r == 8:
                    scores(0)
                if r == 12:
                    scores(1)
                if r < 4:
                    pe.wait_ge(proj_dve if r % 2 else proj_act, HALF_PROJ - 1 + r // 2)
                else:
                    pe.wait_ge(v_dve if r % 2 else v_act, (r - 4) // 2 + 1)
                for i in range(2):
                    g = 2 * r + i
                    mm = pe.matmul(bank(4 + r % 4, D * i, D * i + D), lat[:, P * g:P * g + P], wv[:, :],
                                   start=True, stop=True)
                mm.then_inc(v_in, 1)

            pe.wait_ge(v_act, NGRP // 4)
            pe.wait_ge(v_dve, NGRP // 4)
            for u in range(NU):
                if u + 2 < NU:
                    scores(u + 2)
                weigh(u)

            pe.wait_ge(ld["wo1"], 16)
            pe.wait_ge(oT_ready, 2 * NU)
            pe.wait_ge(small, 2)

            def sum_tokens(n):
                pe.wait_ge(xl_ready, n + 1)
                for k in range(KT):
                    for x in (xh, xl):
                        mm = pe.matmul(bank(4 + k, 0, P), x[:, n, P * k:P * k + P], ident16[:, :],
                                       start=n == 0 and x is xh, stop=n == NTOK - 1 and x is xl)
                return mm

            SUM_LAG = 5
            for n in range(NTOK + SUM_LAG):
                if n < NTOK:
                    if n >= 4:
                        pe.wait_ge(h2_ready, n - 3)
                    for k in range(KT):
                        mm = pe.matmul(bank(n % 4, 0, D), free(oT[:, k, n:], (NTOK, B)), wo1[:, k, :],
                                       start=k == 0, stop=k == KT - 1)
                    mm.then_inc(wo1_done, 1)
                if n >= SUM_LAG:
                    mm = sum_tokens(n - SUM_LAG)
            mm.then_inc(msum_done, 1)

            pe.wait_ge(ld["wr"], 16)
            pe.wait_ge(msum_ready, 1)
            for k in range(KT):
                mm = pe.matmul(bank(6, 0, NE), msumT[:, k, :], wr[:, k, :], start=k == 0, stop=k == KT - 1)
            mm.then_inc(logits_done, 1)
            pe.wait_ge(mask_ready, 1)
            chosen = rt[:, 64:80]
            pe.matmul(bank(6, 32, 32 + NE), const("before"), chosen, start=True, stop=True).then_inc(ranks_done, 1)
            pe.matmul(bank(7, 0, NE), const("one"), chosen, start=True, stop=True).then_inc(ranks_done, 1)
            pe.wait_ge(head_col, 1)
            pe.matmul(bank(7, 64, 64 + NTILE)[0:1], rt[:, 193:194], ident[:, 0:NTILE], start=True, stop=True)\
                .then_inc(head_row, 1)

            def gather(v, f):
                at = NFILL * v + f
                if v == 2 and f == 0:
                    pe.wait_ge(pairs_ready, 2)
                before = [i for i in range(at) if fill_bank(i) == fill_bank(at)]
                if before:
                    w, prev = divmod(before[-1], NFILL)
                    if prev in FILL_ACT:
                        pe.wait_ge(fill_act, len(FILL_ACT) * w + FILL_ACT.index(prev) + 1)
                    else:
                        pe.wait_ge(fill_dve, len(FILL_DVE) * w + FILL_DVE.index(prev) + 1)
                jobs = [(f // 2, 8 * (f % 2) + i) for i in range(8)] if f < 8 else [(k, NPATCH) for k in range(4)]
                for i, (k, n) in enumerate(jobs):
                    x = (xh, xl)[k // KT]
                    lo = P * (k % KT)
                    mm = pe.matmul(bank(fill_bank(at), PU * i, PU * i + PU), x[:, n, lo:lo + P],
                                   pairs_of[:, PU * v:PU * v + PU], start=True, stop=True)
                mm.then_inc(fill_done, 1)

            def gathered(v):
                pe.wait_ge(fill_act, len(FILL_ACT) * (v + 1))
                pe.wait_ge(fill_dve, len(FILL_DVE) * (v + 1))

            TERMS = [(k, w, x) for k in range(KT) for w, x in ((wh, 0), (wl, 0), (wh, 1))]

            def qk(v, r, head, between):
                at = 3 * v + r
                if at >= 2:
                    pe.wait_ge(q2_ready, at - 1)
                    pe.wait_ge(k2_ready, at - 1)
                for i, t in enumerate(QK_ROUNDS[r]):
                    dst = bank(2 + at % 2, TCOL * i, TCOL * i + TCOL)
                    for m, (k, w, x) in enumerate(TERMS):
                        pe.matmul(dst, flat(w[:, k, bass.ds(head[t], 1), 0:P]),
                                  free(xg[:, v % 2, KT * x + k, TP * QROW * t:], (QROW, TP), (1, NTOK)),
                                  start=m == 0, stop=False)
                    mm = pe.matmul(dst, flat(wb[:, bass.ds(head[t], 1), 0:P]), ones[:, 0:TCOL], start=False, stop=True)
                    if i == 0:
                        between()
                mm.then_inc(qk_done, 1)

            def v_of(v, f, head, between):
                at = 2 * v + f
                if v < 2:
                    pe.wait_ge(xg_clear, 2 * (v + 1))
                if at >= 1:
                    pe.wait_ge(v2_ready, at)
                for i in range(8):
                    g = 8 * f + i
                    e = head[g * IPG // TP]
                    dst = bank(4, HD2 * i, HD2 * i + HD2)
                    for m, (k, w, x) in enumerate(TERMS):
                        pe.matmul(dst, xg[:, v % 2, KT * x + k, P * g:P * g + P],
                                  flat(w[:, k, bass.ds(e, 1), P:]), start=m == 0, stop=False)
                    mm = pe.matmul(dst, ones[:, 0:P], flat(wb[:, bass.ds(e, 1), P:]), start=False, stop=True)
                    if i == 7:
                        mm.then_inc(v2_in, 1)
                    if i % 2 and between[i // 2]:
                        between[i // 2]()

            def scores2(v):
                pe.wait_ge(q2_ready, 3 * (v + 1))
                pe.wait_ge(k2_ready, 3 * (v + 1))
                if v >= 1:
                    pe.wait_ge(sub2_done, v)
                for p in range(PU):
                    j, at = QROW * (p % IPG), p // IPG * NTOK
                    mm = pe.matmul(bank(5, at, at + NTOK)[j:j + NTOK], q2[:, v % 2, NTOK * p:NTOK * p + NTOK],
                                   k2[:, v % 2, NTOK * p:NTOK * p + NTOK], start=True, stop=True)
                mm.then_inc(s2_done, 1)

            def weigh2(v, j):
                pe.wait_ge(p2T_ready, v + 1)
                pe.wait_ge(v2_ready, 2 * (v + 1))
                if v >= 1:
                    pe.wait_ge(o2_ready, v)
                rows = slice(QROW * j, QROW * j + NTOK)
                for g in range(GU):
                    mm = pe.matmul(bank(6 + g // 8, g % 8 * HD2, g % 8 * HD2 + HD2)[rows],
                                   p2T[rows, v % 2, g, 0:NTOK], v2[rows, v % 2, g, :], start=True, stop=True)
                mm.then_inc(pv2_done, 1)

            pe.wait_ge(w_low, 6)
            pe.wait_ge(pairs_ready, 1)
            for f in range(NFILL):
                gather(0, f)
            def heads_of(v):
                _, head = nc.values_load_multi_w_load_instructions(
                    heads[0:1, TU * v:TU * v + TU], engines=(mybir.EngineType.PE,), min_val=0, max_val=NE - 1,
                    skip_runtime_bounds_check_because="a count of heads, and no more than NE - 1")
                return head

            pe.wait_ge(heads_ready, 1)
            for v in range(NV):
                head = heads_of(v)
                gathered(v)

                def next_fill(f):
                    if v + 1 < NV:
                        gather(v + 1, f)

                def last_weigh(j):
                    if v >= 1:
                        weigh2(v - 1, j)

                def fill(f):
                    return lambda: next_fill(f)

                for r in range(3):
                    qk(v, r, head, fill(r))
                last_weigh(0)
                v_of(v, 0, head, [fill(3), None, fill(4), None])
                scores2(v)
                last_weigh(1)
                v_of(v, 1, head, [fill(5), fill(6), fill(7), fill(8)])
                last_weigh(2)
                last_weigh(3)
            for j in range(IPG):
                weigh2(NV - 1, j)

            pe.wait_ge(ld["wo2"], 16)
            def turn_heads(k, i):
                e = len(BATCHES) * k + i
                pe.wait_ge(og2_dve, 2 * (k + 1) - (i == 0))
                pe.wait_ge(og2_act, 2 * (k + 1) - (i == 0))
                if k == 1:
                    pe.wait_ge(ogT_ready, i + 1 if i < 2 else e - 1)
                for at, n in enumerate(BATCHES[i]):
                    mm = pe.transpose(bank(turn_bank(k, i), P * at, P * at + P), og2[:, n, P * k:P * k + P], ident)
                mm.then_inc(og_turned, 1)

            pe.wait_ge(wo2_split, 1)
            for i in range(len(BATCHES)):
                turn_heads(0, i)
            turn_heads(1, 0)
            for i, batch in enumerate(BATCHES):
                if i + 1 < len(BATCHES):
                    turn_heads(1, i + 1)
                pe.wait_ge(ogT_ready, len(BATCHES) + i + 1)
                for at, n in enumerate(batch):
                    if n >= WO_BANKS:
                        pe.wait_ge(y_ready, n - WO_BANKS + 1)
                    terms = [(k, x, w) for k in range(KT) for x, w in ((0, 0), (0, 1), (1, 0))]
                    for m, (k, x, w) in enumerate(terms):
                        mm = pe.matmul(bank(2 + n % WO_BANKS, 0, D), turned_heads(k, i, x)[:, P * at:P * at + P],
                                       wo2x[:, w, k, :], start=m == 0, stop=m == len(terms) - 1)
                    mm.then_inc(wo2_done, 1)



def constants(np, br):
    part = np.arange(P)
    tab = np.zeros((P, NCONST), np.float32)

    def put(name, value):
        lo, hi = CONSTS[name]
        tab[:, lo:hi] = value

    put("ident", np.eye(P))
    put("before", part[:, None] < part[None, :])
    put("one", 1.0)
    put("tri", (np.arange(NE)[None, :] < np.arange(NE)[:, None]).reshape(1, -1))
    put("tile_starts", np.arange(B // TP)[None, :] * TP)
    put("pair", np.arange(NPAIR)[None, :])
    put("row", part[:, None])
    put("own_head", part[:, None] // HD1 == np.arange(HH)[None, :])
    put("even", (part[:, None] // HD1) % 2 == 0)
    put("odd", (part[:, None] // HD1) % 2 == 1)
    inverse = (1.0 / 10000.0 ** (np.arange(0, HD1, 2, dtype=np.float32) / HD1)).astype(np.float32)
    feature = np.arange(D)
    angle = (feature // HD1).astype(np.float32) * inverse[(feature % HD1) // 2]
    put("cos", np.cos(angle)[None, :])
    put("sin", (np.sin(angle) * np.where(feature % 2 == 0, -1, 1))[None, :])
    put("slot", np.repeat(np.arange(NSLOT), NE)[None, :])
    put("br", br[None, :])
    put("eps", EPS)
    put("eps_scaled", EPS / XS ** 2)
    return tab


def kernel(**inputs):
    import numpy as np
    import concourse.bacc as bacc
    from concourse import mybir as mb
    from concourse.bass_utils import run_bass_kernel_spmd

    i = {k: np.asarray(v) for k, v in inputs.items()}

    def tiled(w):
        return np.ascontiguousarray(w.reshape(-1, P, w.shape[1]).transpose(1, 0, 2))

    rows = np.concatenate([np.arange(D), np.arange(D) ^ 1])
    image = i["x"].reshape(B, 3, 4, 16, 4, 16).transpose(2, 1, 3, 5, 4, 0).reshape(4, PKT, P, 512)
    wk = np.zeros((P, 2 * D), np.float32)
    wk[:64] = i["L0_attn_wk_b"][rows].T
    wv = np.zeros((P, D), np.float32)
    wv[64:] = i["L0_attn_wv_b"].T
    heads = [i[f"L0_ffn_W{n}"].reshape(KT, P, NE, HD2) for n in "qkv"]
    w = np.concatenate(heads, axis=3)
    w = w.reshape(KT, P, 2, NE // 2 * 192).transpose(0, 2, 1, 3).reshape(4, P, NE // 2 * 192)
    bias = np.concatenate([i[f"L0_ffn_b{n}"].reshape(NE, HD2) for n in "qkv"], axis=1)
    wb = np.zeros((2, P, NE // 2 * 192), np.float32)
    wb[:, 0] = wb[:, QROW] = bias.reshape(2, NE // 2 * 192)
    arrays = {
        "x": np.ascontiguousarray(image.transpose(0, 2, 1, 3)),
        "tokw": tiled(i["L0_tok_W"].T),
        "tokb": i["L0_tok_b"],
        "pos": i["L0_tok_pos_emb"],
        "cls": i["cls_tok"].reshape(D),
        "cst": constants(np, i["L0_ffn_br"]),
        "wq": tiled(i["L0_attn_wq"][rows].T).reshape(P, KT, 2, D),
        "wlat": tiled(np.concatenate([i["L0_attn_wk_a"], i["L0_attn_wv_a"]]).T),
        "wk": wk.reshape(P, 2, D),
        "wv": wv,
        "wo1": tiled(i["L0_attn_wo"].T),
        "w": np.concatenate([w, wb]),
        "wr": tiled(i["L0_ffn_Wr"]),
        "wo2": tiled(i["L0_ffn_Wo"]),
        "bo": i["L0_ffn_bo"],
    }
    nc = bacc.Bacc("TRN2", target_bir_lowering=False, num_devices=1)
    aps = {n: nc.dram_tensor(f"in_{n}", v.shape, mb.dt.from_np(v.dtype), kind="ExternalInput").ap()
           for n, v in arrays.items()}
    out = nc.dram_tensor("out", (B, NTOK, D), F32, kind="ExternalOutput").ap()
    pair_rows = nc.dram_tensor("pair_rows", (NPAIR, NTOK * HD2), F32, kind="Internal").ap()
    build(nc, aps, out, pair_rows)
    r = run_bass_kernel_spmd(nc, [{f"in_{n}": v for n, v in arrays.items()}], core_ids=[0])
    return r.results[0]["out"]
```
